# Optimizing a Trainium2 kernel written in Bass

```python
import numpy as np
import jax
import jax.numpy as jnp

def _softmax(x, axis=-1):
    return jax.nn.softmax(x, axis=axis)

def _gelu(x):
    return jax.nn.gelu(x, approximate=True)

def _silu(x):
    return jax.nn.silu(x)

def _sigmoid(x):
    return jax.nn.sigmoid(x)

def _layernorm(x, axis=-1, eps=1e-05):
    m = jnp.mean(x, axis=axis, keepdims=True)
    v = jnp.var(x, axis=axis, keepdims=True)
    return (x - m) / jnp.sqrt(v + eps)

def _scatter_add(tgt, idx, src, axis=0):
    return tgt.at[idx].add(src)

def _segment_sum(src, seg, n):
    return jax.ops.segment_sum(src, seg, n)
kernel_name = 'mk_xattn_seq_d4_seqx_r4_d02e42'

def setup_inputs(seed: int=0):
    np.random.seed(seed)
    _w = jnp.asarray

    def _rec_inputs():
        import jax
        import jax.numpy as jnp
        _rk = jax.random.key(seed)
        x = -0.000125 + 0.9999 * jax.random.normal(jax.random.fold_in(_rk, 1), (4, 512, 512), jnp.float32)
        _lenS = 512 - jax.random.randint(jax.random.fold_in(_rk, 7), (4,), 0, max(1, 512 // 4) + 1, jnp.int32)
        _lenS2 = 64 - jax.random.randint(jax.random.fold_in(_rk, 8), (4,), 0, max(1, 64 // 4) + 1, jnp.int32)
        _ctx_1024P = jax.random.normal(jax.random.fold_in(_rk, 11), (4, 16, 256), jnp.float32)
        _ctx_1024c = jax.random.dirichlet(jax.random.fold_in(_rk, 511), 0.3 * jnp.ones((16,), jnp.float32), (4, 64))
        _ctx_1024t = jnp.einsum('bsk,bkd->bsd', _ctx_1024c, _ctx_1024P)
        _ctx_1024t = _ctx_1024t * jax.lax.rsqrt(jnp.mean(jnp.square(_ctx_1024t)) + 1e-12) * 0.953939
        ctx_1024 = 4.13588e-05 + 0.999923 * (_ctx_1024t + 0.3 * jax.random.normal(jax.random.fold_in(_rk, 611), (4, 64, 256), jnp.float32))
        pos_1xS = jnp.broadcast_to(jnp.arange(512, dtype=jnp.int32), (1, 512))
        _validS = jnp.arange(512)[None, :] < _lenS[:, None]
        _validS2 = jnp.arange(64)[None, :] < _lenS2[:, None]
        _causal = jnp.tril(jnp.ones((512, 512), dtype=bool))
        mask_BxS2_bk0 = jnp.logical_not(jnp.broadcast_to(_validS2[:, :], (4, 64)))
        mask_BxS_ik0 = jnp.where(jnp.broadcast_to(_validS[:, :], (4, 512)), 0, 1).astype(jnp.int32)
        return (x, ctx_1024, pos_1xS, mask_BxS2_bk0, mask_BxS_ik0)
    x, ctx_1024, pos_1xS, mask_BxS2_bk0, mask_BxS_ik0 = _rec_inputs()

    def _L0_xattn_setup():
        import jax, jax.numpy as jnp
        import numpy as np
        EPS = 1e-06

        def _rmsnorm(x, w):
            var = jnp.mean(jnp.square(x), axis=-1, keepdims=True)
            return x * jax.lax.rsqrt(var + EPS) * w
        key = jax.random.key(seed)
        ks = jax.random.split(key, 6)
        B, N, M = (4, 1024, 512)
        d_model, memory_dim = (512, 256)
        hidden_states = jax.random.normal(ks[0], (B, N, d_model), dtype=jnp.float32)
        memory = jax.random.normal(ks[1], (B, M, memory_dim), dtype=jnp.float32)
        W_mem = jax.random.normal(ks[2], (d_model, memory_dim), dtype=jnp.float32) / np.sqrt(memory_dim)
        W_gate = jax.random.normal(ks[3], (d_model, 2 * d_model), dtype=jnp.float32) / np.sqrt(2 * d_model)
        b_gate = jax.random.normal(ks[4], (d_model,), dtype=jnp.float32) * 0.01
        norm_w = jnp.ones((d_model,), dtype=jnp.float32)
        return {'hidden_states': hidden_states, 'memory': memory, 'W_mem': W_mem, 'W_gate': W_gate, 'b_gate': b_gate, 'norm_w': norm_w}
    _L0_xattn_all = _L0_xattn_setup()
    _L0_xattn_in = {k: v for k, v in _L0_xattn_all.items() if k in ('W_mem', 'W_gate', 'b_gate', 'norm_w')}
    del _L0_xattn_all

    def _L1_xattn_setup():
        import jax, jax.numpy as jnp
        import numpy as np
        DIM = 512
        DIM_MEDIA = 256
        HEADS = 16
        DIM_HEAD = 64
        INNER = HEADS * DIM_HEAD
        FF_INNER = 4 * DIM
        B, N_TOK, N_LAT = (4, 512, 64)
        EPS = 1e-05

        def layernorm(x, g, b):
            mu = jnp.mean(x, axis=-1, keepdims=True)
            var = jnp.var(x, axis=-1, keepdims=True)
            return (x - mu) * jax.lax.rsqrt(var + EPS) * g + b
        key = jax.random.key(seed)
        ks = jax.random.split(key, 12)
        x = jax.random.normal(ks[0], (B, N_TOK, DIM), dtype=jnp.float32)
        media = jax.random.normal(ks[1], (B, N_LAT, DIM_MEDIA), dtype=jnp.float32)
        media_mask = jax.random.randint(ks[2], (B, N_LAT), 0, 2).astype(bool)
        media_mask = media_mask.at[:, 0].set(True)
        s = lambda d: 1.0 / np.sqrt(d)
        Wq = jax.random.normal(ks[3], (DIM, INNER), dtype=jnp.float32) * s(DIM)
        Wkv = jax.random.normal(ks[4], (DIM_MEDIA, 2 * INNER), dtype=jnp.float32) * s(DIM_MEDIA)
        Wo = jax.random.normal(ks[5], (INNER, DIM), dtype=jnp.float32) * s(INNER)
        W1 = jax.random.normal(ks[6], (DIM, FF_INNER), dtype=jnp.float32) * s(DIM)
        W2 = jax.random.normal(ks[7], (FF_INNER, DIM), dtype=jnp.float32) * s(FF_INNER)
        return {'x': x, 'media': media, 'media_mask': media_mask, 'ln_q_g': jnp.ones((DIM,), jnp.float32), 'ln_q_b': jnp.zeros((DIM,), jnp.float32), 'Wq': Wq, 'Wkv': Wkv, 'Wo': Wo, 'attn_gate': jax.random.normal(ks[8], (1,), jnp.float32) * 0.5, 'ln_ff_g': jnp.ones((DIM,), jnp.float32), 'ln_ff_b': jnp.zeros((DIM,), jnp.float32), 'W1': W1, 'W2': W2, 'ff_gate': jax.random.normal(ks[9], (1,), jnp.float32) * 0.5}
    _L1_xattn_all = _L1_xattn_setup()
    _L1_xattn_in = {k: v for k, v in _L1_xattn_all.items() if k in ('ln_q_g', 'ln_q_b', 'Wq', 'Wkv', 'Wo', 'attn_gate', 'ln_ff_g', 'ln_ff_b', 'W1', 'W2', 'ff_gate')}
    del _L1_xattn_all

    def _L2_xattn_setup():
        import jax, jax.numpy as jnp
        import numpy as np
        DIM = 512
        DIM_MEDIA = 256
        HEADS = 16
        DIM_HEAD = 64
        INNER = HEADS * DIM_HEAD
        FF_INNER = 4 * DIM
        B, N_TOK, N_LAT = (4, 512, 64)
        EPS = 1e-05

        def layernorm(x, g, b):
            mu = jnp.mean(x, axis=-1, keepdims=True)
            var = jnp.var(x, axis=-1, keepdims=True)
            return (x - mu) * jax.lax.rsqrt(var + EPS) * g + b
        key = jax.random.key(seed)
        ks = jax.random.split(key, 12)
        x = jax.random.normal(ks[0], (B, N_TOK, DIM), dtype=jnp.float32)
        media = jax.random.normal(ks[1], (B, N_LAT, DIM_MEDIA), dtype=jnp.float32)
        media_mask = jax.random.randint(ks[2], (B, N_LAT), 0, 2).astype(bool)
        media_mask = media_mask.at[:, 0].set(True)
        s = lambda d: 1.0 / np.sqrt(d)
        Wq = jax.random.normal(ks[3], (DIM, INNER), dtype=jnp.float32) * s(DIM)
        Wkv = jax.random.normal(ks[4], (DIM_MEDIA, 2 * INNER), dtype=jnp.float32) * s(DIM_MEDIA)
        Wo = jax.random.normal(ks[5], (INNER, DIM), dtype=jnp.float32) * s(INNER)
        W1 = jax.random.normal(ks[6], (DIM, FF_INNER), dtype=jnp.float32) * s(DIM)
        W2 = jax.random.normal(ks[7], (FF_INNER, DIM), dtype=jnp.float32) * s(FF_INNER)
        return {'x': x, 'media': media, 'media_mask': media_mask, 'ln_q_g': jnp.ones((DIM,), jnp.float32), 'ln_q_b': jnp.zeros((DIM,), jnp.float32), 'Wq': Wq, 'Wkv': Wkv, 'Wo': Wo, 'attn_gate': jax.random.normal(ks[8], (1,), jnp.float32) * 0.5, 'ln_ff_g': jnp.ones((DIM,), jnp.float32), 'ln_ff_b': jnp.zeros((DIM,), jnp.float32), 'W1': W1, 'W2': W2, 'ff_gate': jax.random.normal(ks[9], (1,), jnp.float32) * 0.5}
    _L2_xattn_all = _L2_xattn_setup()
    _L2_xattn_in = {k: v for k, v in _L2_xattn_all.items() if k in ('ln_q_g', 'ln_q_b', 'Wq', 'Wkv', 'Wo', 'attn_gate', 'ln_ff_g', 'ln_ff_b', 'W1', 'W2', 'ff_gate')}
    del _L2_xattn_all

    def _L3_xattn_setup():
        import jax, jax.numpy as jnp
        import numpy as np
        H = 512
        NH = 16
        HD = H // NH
        CH = 256
        CC = 256
        CHD = CC // NH
        I = 1376
        B = 2
        L = 512
        LE = 256
        EPS = 1e-06

        def rms_norm(x, w):
            xf = x.astype(jnp.float32)
            var = jnp.mean(xf * xf, axis=-1, keepdims=True)
            return (w * (xf * jax.lax.rsqrt(var + EPS))).astype(x.dtype)

        def expert_mask(tt):
            vm = jnp.zeros(tt.shape, dtype=bool)
            vm = vm.at[:, :-1].set((tt[:, :-1] == 1) & (tt[:, 1:] == 1))
            return vm

        def rotate_half(x):
            d = x.shape[-1] // 2
            return jnp.concatenate([-x[..., d:], x[..., :d]], axis=-1)

        def apply_rotary(q, k, position_ids, seq_len):
            inv = 1.0 / 10000.0 ** (jnp.arange(0, HD, 2, dtype=jnp.float32) / HD)
            t = jnp.arange(seq_len, dtype=jnp.float32)
            freqs = jnp.outer(t, inv)
            emb = jnp.concatenate([freqs, freqs], axis=-1)
            cos = jnp.cos(emb)[position_ids][:, None].astype(q.dtype)
            sin = jnp.sin(emb)[position_ids][:, None].astype(q.dtype)
            return (q * cos + rotate_half(q) * sin, k * cos + rotate_half(k) * sin)

        def sdpa(q, k, v, causal):
            scale = 1.0 / np.sqrt(q.shape[-1])
            scores = jnp.einsum('bhqd,bhkd->bhqk', q * scale, k)
            if causal:
                mask = jnp.tril(jnp.ones((q.shape[-2], k.shape[-2]), dtype=bool))
                scores = jnp.where(mask, scores, jnp.finfo(jnp.float32).min)
            p = jax.nn.softmax(scores.astype(jnp.float32), axis=-1).astype(q.dtype)
            return jnp.einsum('bhqk,bhkd->bhqd', p, v)

        def heads(x, nh, hd):
            b, l, _ = x.shape
            return x.reshape(b, l, nh, hd).transpose(0, 2, 1, 3)
        key = jax.random.key(seed)
        ks = jax.random.split(key, 20)
        s = 0.02
        f32 = jnp.float32
        return {'hidden_states': jax.random.normal(ks[0], (B, L, H), f32), 'encoder_outputs': jax.random.normal(ks[1], (B, LE, CH), f32), 'token_type_ids': jax.random.randint(ks[2], (B, L), 0, 2, jnp.int32), 'position_ids': jnp.arange(L, dtype=jnp.int32)[None, :], 'ln_in_w': jnp.ones((H,), f32), 'ln_post_attn_w': jnp.ones((H,), f32), 'ln_post_cross_w': jnp.ones((H,), f32), 'v_qkv': jax.random.normal(ks[3], (H, 3 * H), f32) * s, 'l_qkv': jax.random.normal(ks[4], (H, 3 * H), f32) * s, 'v_dense': jax.random.normal(ks[5], (H, H), f32) * s, 'l_dense': jax.random.normal(ks[6], (H, H), f32) * s, 'cq_w': jax.random.normal(ks[7], (H, CC), f32) * s, 'ckv_w': jax.random.normal(ks[8], (CH, 2 * CC), f32) * s, 'cdense_w': jax.random.normal(ks[9], (CC, H), f32) * s, 'v_gate': jax.random.normal(ks[10], (H, I), f32) * s, 'v_up': jax.random.normal(ks[11], (H, I), f32) * s, 'v_down': jax.random.normal(ks[12], (I, H), f32) * s, 'l_gate': jax.random.normal(ks[13], (H, I), f32) * s, 'l_up': jax.random.normal(ks[14], (H, I), f32) * s, 'l_down': jax.random.normal(ks[15], (I, H), f32) * s}
    _L3_xattn_all = _L3_xattn_setup()
    _L3_xattn_in = {k: v for k, v in _L3_xattn_all.items() if k in ('ln_in_w', 'ln_post_attn_w', 'ln_post_cross_w', 'v_qkv', 'l_qkv', 'v_dense', 'l_dense', 'cq_w', 'ckv_w', 'cdense_w', 'v_gate', 'v_up', 'v_down', 'l_gate', 'l_up', 'l_down')}
    del _L3_xattn_all
    return {'x': x, 'ctx_1024': ctx_1024, 'pos_1xS': pos_1xS, 'mask_BxS2_bk0': mask_BxS2_bk0, 'mask_BxS_ik0': mask_BxS_ik0, 'L0_xattn_W_mem': _L0_xattn_in['W_mem'], 'L0_xattn_W_gate': _L0_xattn_in['W_gate'], 'L0_xattn_b_gate': _L0_xattn_in['b_gate'], 'L0_xattn_norm_w': _L0_xattn_in['norm_w'], 'L1_xattn_ln_q_g': _L1_xattn_in['ln_q_g'], 'L1_xattn_ln_q_b': _L1_xattn_in['ln_q_b'], 'L1_xattn_Wq': _L1_xattn_in['Wq'], 'L1_xattn_Wkv': _L1_xattn_in['Wkv'], 'L1_xattn_Wo': _L1_xattn_in['Wo'], 'L1_xattn_attn_gate': _L1_xattn_in['attn_gate'], 'L1_xattn_ln_ff_g': _L1_xattn_in['ln_ff_g'], 'L1_xattn_ln_ff_b': _L1_xattn_in['ln_ff_b'], 'L1_xattn_W1': _L1_xattn_in['W1'], 'L1_xattn_W2': _L1_xattn_in['W2'], 'L1_xattn_ff_gate': _L1_xattn_in['ff_gate'], 'L2_xattn_ln_q_g': _L2_xattn_in['ln_q_g'], 'L2_xattn_ln_q_b': _L2_xattn_in['ln_q_b'], 'L2_xattn_Wq': _L2_xattn_in['Wq'], 'L2_xattn_Wkv': _L2_xattn_in['Wkv'], 'L2_xattn_Wo': _L2_xattn_in['Wo'], 'L2_xattn_attn_gate': _L2_xattn_in['attn_gate'], 'L2_xattn_ln_ff_g': _L2_xattn_in['ln_ff_g'], 'L2_xattn_ln_ff_b': _L2_xattn_in['ln_ff_b'], 'L2_xattn_W1': _L2_xattn_in['W1'], 'L2_xattn_W2': _L2_xattn_in['W2'], 'L2_xattn_ff_gate': _L2_xattn_in['ff_gate'], 'L3_xattn_ln_in_w': _L3_xattn_in['ln_in_w'], 'L3_xattn_ln_post_attn_w': _L3_xattn_in['ln_post_attn_w'], 'L3_xattn_ln_post_cross_w': _L3_xattn_in['ln_post_cross_w'], 'L3_xattn_v_qkv': _L3_xattn_in['v_qkv'], 'L3_xattn_l_qkv': _L3_xattn_in['l_qkv'], 'L3_xattn_v_dense': _L3_xattn_in['v_dense'], 'L3_xattn_l_dense': _L3_xattn_in['l_dense'], 'L3_xattn_cq_w': _L3_xattn_in['cq_w'], 'L3_xattn_ckv_w': _L3_xattn_in['ckv_w'], 'L3_xattn_cdense_w': _L3_xattn_in['cdense_w'], 'L3_xattn_v_gate': _L3_xattn_in['v_gate'], 'L3_xattn_v_up': _L3_xattn_in['v_up'], 'L3_xattn_v_down': _L3_xattn_in['v_down'], 'L3_xattn_l_gate': _L3_xattn_in['l_gate'], 'L3_xattn_l_up': _L3_xattn_in['l_up'], 'L3_xattn_l_down': _L3_xattn_in['l_down']}

def reference(x, ctx_1024, pos_1xS, mask_BxS2_bk0, mask_BxS_ik0, L0_xattn_W_mem, L0_xattn_W_gate, L0_xattn_b_gate, L0_xattn_norm_w, L1_xattn_ln_q_g, L1_xattn_ln_q_b, L1_xattn_Wq, L1_xattn_Wkv, L1_xattn_Wo, L1_xattn_attn_gate, L1_xattn_ln_ff_g, L1_xattn_ln_ff_b, L1_xattn_W1, L1_xattn_W2, L1_xattn_ff_gate, L2_xattn_ln_q_g, L2_xattn_ln_q_b, L2_xattn_Wq, L2_xattn_Wkv, L2_xattn_Wo, L2_xattn_attn_gate, L2_xattn_ln_ff_g, L2_xattn_ln_ff_b, L2_xattn_W1, L2_xattn_W2, L2_xattn_ff_gate, L3_xattn_ln_in_w, L3_xattn_ln_post_attn_w, L3_xattn_ln_post_cross_w, L3_xattn_v_qkv, L3_xattn_l_qkv, L3_xattn_v_dense, L3_xattn_l_dense, L3_xattn_cq_w, L3_xattn_ckv_w, L3_xattn_cdense_w, L3_xattn_v_gate, L3_xattn_v_up, L3_xattn_v_down, L3_xattn_l_gate, L3_xattn_l_up, L3_xattn_l_down):
    import jax
    import jax.numpy as jnp

    def _L0_xattn_ref(hidden_states, memory, W_mem, W_gate, b_gate, norm_w):
        import jax, jax.numpy as jnp
        import numpy as np
        EPS = 1e-06

        def _rmsnorm(x, w):
            var = jnp.mean(jnp.square(x), axis=-1, keepdims=True)
            return x * jax.lax.rsqrt(var + EPS) * w
        D = hidden_states.shape[-1]
        memory_proj = jnp.einsum('bme,de->bmd', memory, W_mem)
        scores = jnp.einsum('bnd,bmd->bnm', hidden_states, memory_proj) / jnp.sqrt(jnp.float32(D))
        attn = jax.nn.softmax(scores, axis=-1)
        memory_context = jnp.einsum('bnm,bmd->bnd', attn, memory_proj)
        gate_input = jnp.concatenate([hidden_states, memory_context], axis=-1)
        gate = jax.nn.sigmoid(jnp.einsum('bnf,df->bnd', gate_input, W_gate) + b_gate)
        fused = hidden_states + gate * memory_context
        return _rmsnorm(fused, norm_w)

    def _L1_xattn_ref(x, media, media_mask, ln_q_g, ln_q_b, Wq, Wkv, Wo, attn_gate, ln_ff_g, ln_ff_b, W1, W2, ff_gate):
        import jax, jax.numpy as jnp
        import numpy as np
        DIM = 512
        DIM_MEDIA = 256
        HEADS = 16
        DIM_HEAD = 64
        INNER = HEADS * DIM_HEAD
        FF_INNER = 4 * DIM
        B, N_TOK, N_LAT = (4, 512, 64)
        EPS = 1e-05

        def layernorm(x, g, b):
            mu = jnp.mean(x, axis=-1, keepdims=True)
            var = jnp.var(x, axis=-1, keepdims=True)
            return (x - mu) * jax.lax.rsqrt(var + EPS) * g + b
        scale = DIM_HEAD ** (-0.5)
        qn = layernorm(x, ln_q_g, ln_q_b)
        q = qn @ Wq * scale
        kv = media @ Wkv
        k, v = jnp.split(kv, 2, axis=-1)
        split_heads = lambda t: t.reshape(t.shape[0], t.shape[1], HEADS, DIM_HEAD).transpose(0, 2, 1, 3)
        q, k, v = (split_heads(q), split_heads(k), split_heads(v))
        sim = jnp.einsum('bhid,bhjd->bhij', q, k)
        neg_inf = jnp.finfo(sim.dtype).min
        sim = jnp.where(media_mask[:, None, None, :], sim, neg_inf)
        attn = jax.nn.softmax(sim, axis=-1)
        out = jnp.einsum('bhij,bhjd->bhid', attn, v)
        out = out.transpose(0, 2, 1, 3).reshape(x.shape[0], x.shape[1], INNER)
        attn_out = out @ Wo
        x = x + jnp.tanh(attn_gate) * attn_out
        h = layernorm(x, ln_ff_g, ln_ff_b)
        h = jax.nn.gelu(h @ W1, approximate=False) @ W2
        x = x + jnp.tanh(ff_gate) * h
        return x

    def _L2_xattn_ref(x, media, media_mask, ln_q_g, ln_q_b, Wq, Wkv, Wo, attn_gate, ln_ff_g, ln_ff_b, W1, W2, ff_gate):
        import jax, jax.numpy as jnp
        import numpy as np
        DIM = 512
        DIM_MEDIA = 256
        HEADS = 16
        DIM_HEAD = 64
        INNER = HEADS * DIM_HEAD
        FF_INNER = 4 * DIM
        B, N_TOK, N_LAT = (4, 512, 64)
        EPS = 1e-05

        def layernorm(x, g, b):
            mu = jnp.mean(x, axis=-1, keepdims=True)
            var = jnp.var(x, axis=-1, keepdims=True)
            return (x - mu) * jax.lax.rsqrt(var + EPS) * g + b
        scale = DIM_HEAD ** (-0.5)
        qn = layernorm(x, ln_q_g, ln_q_b)
        q = qn @ Wq * scale
        kv = media @ Wkv
        k, v = jnp.split(kv, 2, axis=-1)
        split_heads = lambda t: t.reshape(t.shape[0], t.shape[1], HEADS, DIM_HEAD).transpose(0, 2, 1, 3)
        q, k, v = (split_heads(q), split_heads(k), split_heads(v))
        sim = jnp.einsum('bhid,bhjd->bhij', q, k)
        neg_inf = jnp.finfo(sim.dtype).min
        sim = jnp.where(media_mask[:, None, None, :], sim, neg_inf)
        attn = jax.nn.softmax(sim, axis=-1)
        out = jnp.einsum('bhij,bhjd->bhid', attn, v)
        out = out.transpose(0, 2, 1, 3).reshape(x.shape[0], x.shape[1], INNER)
        attn_out = out @ Wo
        x = x + jnp.tanh(attn_gate) * attn_out
        h = layernorm(x, ln_ff_g, ln_ff_b)
        h = jax.nn.gelu(h @ W1, approximate=False) @ W2
        x = x + jnp.tanh(ff_gate) * h
        return x

    def _L3_xattn_ref(hidden_states, encoder_outputs, token_type_ids, position_ids, ln_in_w, ln_post_attn_w, ln_post_cross_w, v_qkv, l_qkv, v_dense, l_dense, cq_w, ckv_w, cdense_w, v_gate, v_up, v_down, l_gate, l_up, l_down):
        import jax, jax.numpy as jnp
        import numpy as np
        H = 512
        NH = 16
        HD = H // NH
        CH = 256
        CC = 256
        CHD = CC // NH
        I = 1376
        B = 2
        L = 512
        LE = 256
        EPS = 1e-06

        def rms_norm(x, w):
            xf = x.astype(jnp.float32)
            var = jnp.mean(xf * xf, axis=-1, keepdims=True)
            return (w * (xf * jax.lax.rsqrt(var + EPS))).astype(x.dtype)

        def expert_mask(tt):
            vm = jnp.zeros(tt.shape, dtype=bool)
            vm = vm.at[:, :-1].set((tt[:, :-1] == 1) & (tt[:, 1:] == 1))
            return vm

        def rotate_half(x):
            d = x.shape[-1] // 2
            return jnp.concatenate([-x[..., d:], x[..., :d]], axis=-1)

        def apply_rotary(q, k, position_ids, seq_len):
            inv = 1.0 / 10000.0 ** (jnp.arange(0, HD, 2, dtype=jnp.float32) / HD)
            t = jnp.arange(seq_len, dtype=jnp.float32)
            freqs = jnp.outer(t, inv)
            emb = jnp.concatenate([freqs, freqs], axis=-1)
            cos = jnp.cos(emb)[position_ids][:, None].astype(q.dtype)
            sin = jnp.sin(emb)[position_ids][:, None].astype(q.dtype)
            return (q * cos + rotate_half(q) * sin, k * cos + rotate_half(k) * sin)

        def sdpa(q, k, v, causal):
            scale = 1.0 / np.sqrt(q.shape[-1])
            scores = jnp.einsum('bhqd,bhkd->bhqk', q * scale, k)
            if causal:
                mask = jnp.tril(jnp.ones((q.shape[-2], k.shape[-2]), dtype=bool))
                scores = jnp.where(mask, scores, jnp.finfo(jnp.float32).min)
            p = jax.nn.softmax(scores.astype(jnp.float32), axis=-1).astype(q.dtype)
            return jnp.einsum('bhqk,bhkd->bhqd', p, v)

        def heads(x, nh, hd):
            b, l, _ = x.shape
            return x.reshape(b, l, nh, hd).transpose(0, 2, 1, 3)
        b, l, _ = hidden_states.shape
        vm = expert_mask(token_type_ids)[..., None]
        residual = hidden_states
        x = rms_norm(hidden_states, ln_in_w)
        mixed = jnp.where(vm, x @ v_qkv, x @ l_qkv)
        q, k, v = jnp.split(mixed, 3, axis=-1)
        q, k, v = (heads(q, NH, HD), heads(k, NH, HD), heads(v, NH, HD))
        q, k = apply_rotary(q, k, position_ids, l)
        ctx = sdpa(q, k, v, causal=True)
        ctx = ctx.transpose(0, 2, 1, 3).reshape(b, l, H)
        attn_out = jnp.where(vm, ctx @ v_dense, ctx @ l_dense)
        hidden_states = residual + attn_out
        ci = rms_norm(hidden_states, ln_post_cross_w)
        cq = heads(ci @ cq_w, NH, CHD)
        ckv = encoder_outputs @ ckv_w
        ck, cv = jnp.split(ckv, 2, axis=-1)
        ck, cv = (heads(ck, NH, CHD), heads(cv, NH, CHD))
        cctx = sdpa(cq, ck, cv, causal=False)
        cctx = cctx.transpose(0, 2, 1, 3).reshape(b, l, CC)
        hidden_states = hidden_states + cctx @ cdense_w
        mi = rms_norm(hidden_states, ln_post_attn_w)
        v_out = jax.nn.silu(mi @ v_gate) * (mi @ v_up) @ v_down
        l_out = jax.nn.silu(mi @ l_gate) * (mi @ l_up) @ l_down
        hidden_states = hidden_states + jnp.where(vm, v_out, l_out)
        return hidden_states
    x = _L0_xattn_ref(x, ctx_1024, L0_xattn_W_mem, L0_xattn_W_gate, L0_xattn_b_gate, L0_xattn_norm_w)
    x = _L1_xattn_ref(x, ctx_1024, mask_BxS2_bk0, L1_xattn_ln_q_g, L1_xattn_ln_q_b, L1_xattn_Wq, L1_xattn_Wkv, L1_xattn_Wo, L1_xattn_attn_gate, L1_xattn_ln_ff_g, L1_xattn_ln_ff_b, L1_xattn_W1, L1_xattn_W2, L1_xattn_ff_gate)
    x = _L2_xattn_ref(x, ctx_1024, mask_BxS2_bk0, L2_xattn_ln_q_g, L2_xattn_ln_q_b, L2_xattn_Wq, L2_xattn_Wkv, L2_xattn_Wo, L2_xattn_attn_gate, L2_xattn_ln_ff_g, L2_xattn_ln_ff_b, L2_xattn_W1, L2_xattn_W2, L2_xattn_ff_gate)
    x = _L3_xattn_ref(x, ctx_1024, mask_BxS_ik0, pos_1xS, L3_xattn_ln_in_w, L3_xattn_ln_post_attn_w, L3_xattn_ln_post_cross_w, L3_xattn_v_qkv, L3_xattn_l_qkv, L3_xattn_v_dense, L3_xattn_l_dense, L3_xattn_cq_w, L3_xattn_ckv_w, L3_xattn_cdense_w, L3_xattn_v_gate, L3_xattn_v_up, L3_xattn_v_down, L3_xattn_l_gate, L3_xattn_l_up, L3_xattn_l_down)
    return x

_drawn_inputs = setup_inputs


def setup_inputs(seed=0):
    import zlib

    import numpy as np

    out = dict(_drawn_inputs(seed))
    spreads = {'L0_xattn_norm_w': (1.0, 0.2),
     'L1_xattn_ln_q_g': (1.0, 0.6),
     'L1_xattn_ln_q_b': (0.0, 0.8),
     'L1_xattn_ln_ff_g': (1.0, 0.6),
     'L1_xattn_ln_ff_b': (0.0, 0.8),
     'L2_xattn_ln_q_g': (1.0, 0.6),
     'L2_xattn_ln_q_b': (0.0, 0.8),
     'L2_xattn_ln_ff_g': (1.0, 0.6),
     'L2_xattn_ln_ff_b': (0.0, 0.8),
     'L3_xattn_ln_in_w': (1.0, 0.6),
     'L3_xattn_ln_post_attn_w': (1.0, 0.6),
     'L3_xattn_ln_post_cross_w': (1.0, 0.6)}
    factors = {'L0_xattn_b_gate': 8.0,
     'L1_xattn_W1': 2.847,
     'L2_xattn_W1': 2.861,
     'L3_xattn_v_qkv': 8.0,
     'L3_xattn_cq_w': 8.0}
    for name, (base, spread) in spreads.items():
        noise = np.random.default_rng([zlib.crc32(name.encode()), seed]).standard_normal(out[name].shape)
        drawn = base * np.exp(spread * noise) if base else spread * noise
        out[name] = jnp.asarray(drawn.astype(out[name].dtype))
    for name, factor in factors.items():
        out[name] = (out[name] * factor).astype(out[name].dtype)
    return out
```

```python
from contextlib import ExitStack

import numpy as np

import concourse.bass as bass
from concourse import mybir

F32 = mybir.dt.float32
F32R = mybir.dt.float32r
I32 = mybir.dt.int32
U8 = mybir.dt.uint8
ALU = mybir.AluOpType
ACT = mybir.ActivationFunctionType
AX = mybir.AxisListType.X

P = 128
B = 4
SEQ = 512
T = SEQ // P
D = 512
KT = D // P
M = 64
MD = 256
PAIRS = 8
FF = 2048 // P
HID = 1376
HT = -(-HID // P)
HEADS3 = 16
HD3 = 32
FLT_MAX = 3.4028234663852886e38
SLOTS = 34
SLOTS_A = 16
STAGES = 3
PARAMS = ["L1_xattn_ln_q_g", "L1_xattn_ln_q_b", "L1_xattn_ln_ff_g", "L1_xattn_ln_ff_b",
          "L2_xattn_ln_q_g", "L2_xattn_ln_q_b", "L2_xattn_ln_ff_g", "L2_xattn_ln_ff_b",
          "L3_xattn_ln_in_w", "L3_xattn_ln_post_cross_w", "L3_xattn_ln_post_attn_w"]
GATES = ["L1_xattn_attn_gate", "L1_xattn_ff_gate", "L2_xattn_attn_gate", "L2_xattn_ff_gate"]

Q3_BODY = [("P", 0), ("P", 1), ("X", 0), ("P", 2), ("X", 1), ("P", 3), ("X", 2), ("TRl", 0), ("TRv", 0), ("X", 3)]
Q3_SIZE = {"P": 3, "X": 2, "TRl": 4, "TRv": 4}
TO_ORDER = [("T", 0), ("T", 1), ("O", 0), ("T", 2), ("O", 1), ("T", 3), ("O", 2), ("O", 3)]


def piece_names():
    k0 = [("ctx", k) for k in range(2)] + [("wmem", k) for k in range(2)]
    for l in "12":
        k0 += [(f"wkv{l}", i) for i in range(8)]
    k0 += [("ckv", k) for k in range(2)]
    g = [("wg", k) for k in range(8)]
    a = {l: [(f"wq{l}", i) for i in range(8)] + [(f"wo{l}", i) for i in range(8)] for l in "12"}
    f = {l: [(f"{w}{l}", j) for j in range(FF) for w in ("w1_", "w2_")] for l in "12"}
    q3 = [(f"qkv_{e}", 4 * c + k) for c in range(3) for e in "lv" for k in range(KT)]
    a3 = [(f"dense_{e}", k) for e in "lv" for k in range(KT)]
    c3 = [("cq", k) for k in range(2)] + [("cdense", k) for k in range(2)]
    m = {e: [(f"{w}_{e}", j) for j in range(HT) for w in ("gate", "up", "down")] for e in "lv"}
    return {"K0": k0, "G": g, "A1": a["1"], "F1": f["1"], "A2": a["2"], "F2": f["2"],
            "Q3": q3, "A3": a3, "C3": c3, "Ml": m["l"], "Mv": m["v"]}


def build(nc, t_in, out, phases):
    with ExitStack() as ctx:
        def sb(name, shape, dt=F32, stack=ctx):
            return stack.enter_context(nc.sbuf_tensor(name, shape, dt))

        def sem(name):
            return ctx.enter_context(nc.semaphore(name))

        x = sb("x", [P, B * T, D])
        xn = sb("xn", [P, T, D])
        xT = [sb(f"xT_{n}", [P, KT, SEQ], F32R) for n in ("hi", "lo")]
        stage = sb("stage", [P, STAGES, 512])
        wa = [sb(f"wa_{n}", [P, SLOTS_A, 512], F32R) for n in ("hi", "lo")]
        ident = sb("ident", [P, P])
        par = sb("par", [P, len(PARAMS), KT])
        gates = sb("gates", [P, len(GATES)])
        kbias = sb("kbias", [P, B, M])
        mask8 = sb("mask8", [P, B, M // 4], I32)
        types = sb("types", [P, 2, B * T], I32)
        vis = sb("vis", [P, 2, B * T])
        wrs = sb("wrs", [P, 2, T])
        pos = sb("pos", [P, T], I32)
        rope = sb("rope", [P, T, 2 * HD3])
        bst = sb("bst", [P, T, 6])
        mv = sb("mv", [P, T, 2])
        var = sb("var", [P, T])
        rs = sb("rs", [P, T])
        nt = sb("nt", [P, T])
        mx = sb("mx", [P, T, 8])
        sm = sb("sm", [P, T, 8])

        scopes = ExitStack()
        with scopes:
            wb = [sb(f"wb_{n}", [P, SLOTS - SLOTS_A, 512], F32R, scopes) for n in ("hi", "lo")]
            hf = sb("hf", [P, 512], stack=scopes)
            hT = [sb(f"hT_{n}", [P, 512], F32R, scopes) for n in ("hi", "lo")]
        scopes = ExitStack()
        with scopes:
            mpM = [sb(f"mp_{n}", [M, B, D], F32R, scopes) for n in ("hi", "lo")]
            mpT = [sb(f"mpT_{n}", [P, KT, B * M], F32R, scopes) for n in ("hi", "lo")]
            inner = ExitStack()
            with inner:
                bd = [sb(f"bd_{n}", [P, B, 1024], F32R, inner) for n in ("hi", "lo")]
                bdf = sb("bdf", [P, 512], stack=inner)
                mask_k = sb("mask_k", [P, 8, M], stack=inner)
                mask_v = sb("mask_v", [P, 4, P], stack=inner)
            cT = [sb(f"cT_{n}", [P, KT, SEQ], F32R, scopes) for n in ("hi", "lo")]
            ctxf = sb("ctxf", [P, T, D], stack=scopes)
            gPT = [sb(f"gPT_{n}", [M, SEQ], F32R, scopes) for n in ("hi", "lo")]
            gs = sb("gs", [P, T, M], stack=scopes)
            gP = sb("gP", [P, T, M], stack=scopes)
            gbias = sb("gbias", [P, D], stack=scopes)
            gnorm = sb("gnorm", [P, D], stack=scopes)
            gz = sb("gz", [P, 2, D], stack=scopes)
        scopes = ExitStack()
        with scopes:
            qT = [sb(f"qT_{n}", [P, 4, SEQ], F32R, scopes) for n in ("hi", "lo")]
            oT = [sb(f"oT_{n}", [P, 4, SEQ], F32R, scopes) for n in ("hi", "lo")]
            pT = [sb(f"pT_{n}", [P, 2, SEQ], F32R, scopes) for n in ("hi", "lo")]
            sc = sb("sc", [P, 2, 512], stack=scopes)
            pr = sb("pr", [P, T, 512], stack=scopes)
            kbd = [sb(f"kbd_{n}", [P, 1024], F32R, scopes) for n in ("hi", "lo")]
            vbd = [sb(f"vbd_{n}", [P, 1024], F32R, scopes) for n in ("hi", "lo")]

        scopes = ExitStack()
        with scopes:
            wb3 = [sb(f"wb3_{n}", [P, 8, 512], F32R, scopes) for n in ("hi", "lo")]
            xTv = [sb(f"xTv_{n}", [P, KT, SEQ], F32R, scopes) for n in ("hi", "lo")]
            xnv = sb("xnv", [P, T, D], stack=scopes)
            r3 = sb("r3", [P, 2, 2, 512], stack=scopes)
            tmp3 = sb("tmp3", [P, 512], stack=scopes)
            qk_out = [sb(f"qk_out_{n}", [P, 2, 512], F32R, scopes) for n in ("hi", "lo")]
            v_out = [sb(f"v_out_{n}", [P, 512], F32R, scopes) for n in ("hi", "lo")]
        scopes = ExitStack()
        with scopes:
            q3 = [sb(f"q3_{n}", [P, 2, SEQ], F32R, scopes) for n in ("hi", "lo")]
            k3 = [sb(f"k3_{n}", [P, 2, SEQ], F32R, scopes) for n in ("hi", "lo")]
            v3 = [sb(f"v3_{n}", [P, 2, T, P], F32R, scopes) for n in ("hi", "lo")]
            p3 = sb("p3", [P, 4, SEQ], stack=scopes)
            pT3 = [sb(f"pT3_{n}", [P, 2, SEQ], F32R, scopes) for n in ("hi", "lo")]
            o3 = sb("o3", [P, 2, P], stack=scopes)
            oT3 = [sb(f"oT3_{n}", [P, 4, SEQ], F32R, scopes) for n in ("hi", "lo")]
            causal = sb("causal", [P, P], stack=scopes)
            nm3 = sb("nm3", [P, 2, 64], stack=scopes)
            sum3 = sb("sum3", [P, 64], stack=scopes)
        scopes = ExitStack()
        with scopes:
            cqT = [sb(f"cqT_{n}", [P, 2, SEQ], F32R, scopes) for n in ("hi", "lo")]
            coT = [sb(f"coT_{n}", [P, 2, SEQ], F32R, scopes) for n in ("hi", "lo")]
            cpT = [sb(f"cpT_{n}", [P, 2, SEQ], F32R, scopes) for n in ("hi", "lo")]
            csc = sb("csc", [P, 2, 512], stack=scopes)
            cpr = sb("cpr", [P, 2 * T, 512], stack=scopes)
            ckbd = [sb(f"ckbd_{n}", [P, 1024], F32R, scopes) for n in ("hi", "lo")]
            cvbd = [sb(f"cvbd_{n}", [P, 1024], F32R, scopes) for n in ("hi", "lo")]
        scopes = ExitStack()
        with scopes:
            wbm = [sb(f"wbm_{n}", [P, 3 * HT - SLOTS_A, 512], F32R, scopes) for n in ("hi", "lo")]
            sg = sb("sg", [P, 512], stack=scopes)
            mf = sb("mf", [P, 512], stack=scopes)
            mT = [sb(f"mT_{n}", [P, 512], F32R, scopes) for n in ("hi", "lo")]

        y_psum = ctx.enter_context(nc.psum_tensor("y_psum", [P, T, 512], F32))
        ring = ctx.enter_context(nc.psum_tensor("ring", [P, 4, 512], F32))

        psum_full, act_out, operand_ready = sem("psum_full"), sem("act_out"), sem("operand_ready")
        y_done, x_done = sem("y_done"), sem("x_done")
        scores_copied, scores_shifted = sem("scores_copied"), sem("scores_shifted")
        xn_ready, w_ready, w_hi = sem("xn_ready"), sem("w_ready"), sem("w_hi")
        staged = [sem(f"staged{i}") for i in range(STAGES)]
        consts_loaded, x_loaded, zeroed = sem("consts_loaded"), sem("x_loaded"), sem("zeroed")
        bd_stored, k_loaded, v_loaded = sem("bd_stored"), sem("k_loaded"), sem("v_loaded")
        gate_in, gate_out, tanh_done = sem("gate_in"), sem("gate_out"), sem("tanh_done")
        dve_step, stored = sem("dve_step"), sem("stored")
        rope_loaded, q_stored, k_stored, v_stored = (sem(n) for n in ("rope_loaded", "q_stored", "k_stored", "v_stored"))
        sc3_full, sc3_max, p3_ready, pt3_full, pt3_hi, pt3_ready, pv3_done = (
            sem(n) for n in ("sc3_full", "sc3_max", "p3_ready", "pt3_full", "pt3_hi", "pt3_ready", "pv3_done"))
        o3_ready, ox3_full, ox3_hi, ox3_ready, dense_full, dense_added = (
            sem(n) for n in ("o3_ready", "ox3_full", "ox3_hi", "ox3_ready", "dense_full", "dense_added"))
        qkv_loaded = [sem(f"qkv_loaded{i}") for i in range(2)]
        pe_passed, act_passed, dve_passed = sem("pe_passed"), sem("act_passed"), sem("dve_passed")

        K0_KV = {"1": 8, "2": 24, "C": 40}
        N_K0, N_G, N_A, N_F = 46, 16 * B, 8 + 36 * 3 + 28, 4 + 20 * 3 + 16
        N_Q3, N_C, N_M = 8 + 28 * 3 + 20, 6 + 24 * 3 + 18, 6 + 28 * 3 + 22
        order = ["K0", "G", "A1", "F1", "A2", "F2", "Q3", "A3", "C3", "Ml", "Mv"]
        n_groups = {"K0": N_K0, "G": N_G, "A1": N_A, "A2": N_A, "F1": N_F, "F2": N_F, "Q3": N_Q3, "A3": 0, "C3": N_C,
                    "Ml": N_M, "Mv": N_M}
        n_y = {"K0": 0, "G": B, "A1": 8 * B, "A2": 8 * B, "F1": FF * B, "F2": FF * B, "Q3": 0, "A3": 0, "C3": B,
               "Ml": HT * B, "Mv": HT * B}
        n_s = {"G": 2 * B, "A1": 8 * B, "A2": 8 * B, "C3": 8 * B}
        n_xn = {"G": 4, "A1": 4, "A2": 4, "F1": 4, "F2": 4, "Q3": 4, "C3": 4, "Ml": 4, "Mv": 4}
        seq0, y0, s0, xn0, xd0 = {}, {}, {}, {}, {}
        a = b_ = c = d_ = 0
        e_ = 1
        for ph in order:
            seq0[ph], y0[ph], s0[ph], xn0[ph], xd0[ph] = a, b_, c, d_, e_
            a += n_groups[ph]
            b_ += n_y[ph]
            c += n_s.get(ph, 0)
            d_ += n_xn.get(ph, 0)
            e_ += 0 if ph in ("K0", "Q3") else B * T

        copied0 = {"A1": 0, "A2": 8 * B, "C3": 16 * B}

        def a_layout(last):
            at, n = {}, 0
            for name, k in (("S0", 4), ("Q1", 4), ("TO0", 8)) + (() if last else (("TR", 4),)) \
                    + (("S1", 4),) + (() if last else (("Q2", 4),)) + (("TO1", 8),):
                at[name] = n
                n += k
            return at, n

        names = piece_names()
        slots = {"K0": [0, 1, 2, 3] + list(range(4, 12)) + [12, 13, 14, 15, 4, 5, 6, 7] + [8, 9],
                 "G": [10, 11, 12, 13, 14, 15, 2, 3],
                 "A1": [0, 1, 4, 5, 6, 7, 8, 9, 10, 11, 12, 13, 14, 15, 2, 3],
                 "F1": list(range(32)), "A2": list(range(16)), "F2": list(range(32)),
                 "Q3": list(range(24)), "A3": list(range(8)), "C3": list(range(8, 12))}
        slots["Ml"] = slots["Mv"] = [12, 13, 14, 15] + list(range(12)) + list(range(16, 3 * HT))

        def last_use(ph, i):
            if ph == "K0":
                name, k = names["K0"][i]
                n = {"ctx": N_K0, "wmem": 8, "ckv": N_K0}.get(name)
                if n is None:
                    n = K0_KV[name[-1]] + (8 if k < 4 else 16)
                return psum_full, n
            if ph == "G":
                return y_done, y0[ph] + B
            if ph in ("A1", "A2"):
                tail = seq0[ph] + 8 + 3 * 36
                if i < 4:
                    return psum_full, tail
                if i < 8:
                    return psum_full, tail + a_layout(True)[0]["Q1"] + i - 4 + 1
                return y_done, y0[ph] + 8 * 3 + (i - 8) + 1
            if ph == "Q3":
                return psum_full, seq0[ph] + 8 + 28 * 3 + 13 + i // 8 + 1
            if ph in ("A3", "C3"):
                return x_done, xd0[ph] + B * T
            if ph[0] == "M":
                j = i // 3
                if i % 3 < 2:
                    return psum_full, seq0[ph] + 6 + 28 * 3 + 2 * j + 2
                return y_done, y0[ph] + HT * 3 + j + 1
            j = i // 2
            if i % 2 == 0:
                return psum_full, seq0[ph] + 4 + 60 + j + 1
            return y_done, y0[ph] + FF * 3 + j + 1

        pieces, index_of, owner, home = [], {}, {}, {}
        for ph in order:
            if ph not in phases:
                continue
            for i, name in enumerate(names[ph]):
                slot = slots[ph][i]
                free = [owner[slot]] if slot in owner else []
                if (ph[0] == "F" or ph in ("Q3", "Ml")) and slot >= SLOTS_A:
                    free = [(x_done, xd0[ph])]
                index_of[name] = len(pieces)
                pieces.append((name, slot, free))
                owner[slot] = last_use(ph, i)
                high = wb3 if ph == "Q3" else wbm if ph[0] == "M" else wb
                home[name] = [p_[:, slot - SLOTS_A, :] for p_ in high] if slot >= SLOTS_A \
                    else [p_[:, slot, :] for p_ in wa]

        def w(name):
            return home[name]

        def q3_order(last):
            steps_, n = [], 0
            for kind, t in Q3_BODY:
                if last and kind in ("TRl", "TRv"):
                    continue
                steps_.append((kind, t, n))
                n += Q3_SIZE[kind]
            return steps_

        block = ctx.enter_context(nc.Block())

        @block.sync
        def _(sp):
            for n, (name, slot, free) in enumerate(pieces):
                if n >= STAGES:
                    sp.wait_ge(w_ready, n - STAGES + 1)
                sp.dma_start(stage[:, n % STAGES, :], t_in["weights"][name]).then_inc(staged[n % STAGES], 16)
            sp.wait_ge(x_done, 1 + sum(B * T for ph in phases if ph not in ("K0", "Q3")))
            for b in range(B):
                sp.dma_start(out[b * SEQ:(b + 1) * SEQ, :].rearrange("(t p) d -> p t d", p=P),
                             x[:, b * T:(b + 1) * T, :]).then_inc(stored, 16)
            sp.wait_ge(stored, 16 * B)

        @block.gpsimd
        def _(pool):
            pool.wait_ge(consts_loaded, CONSTS)
            for t in range(T):
                nc.gpsimd.indirect_dma_start(
                    rope[:, t, :], None, t_in["rope_table"],
                    bass.IndirectOffsetOnAxis(ap=pos[:, t:t + 1].bitcast(mybir.dt.uint32), axis=0)).then_inc(rope_loaded, 16)
            for n, (name, slot, free) in enumerate(pieces):
                hi, lo = w(name)
                pool.wait_ge(staged[n % STAGES], 16 * (n // STAGES + 1))
                for s, v in free:
                    pool.wait_ge(s, v)
                nc.gpsimd.tensor_scalar(hi, stage[:, n % STAGES, :], 1.0, 1.0, ALU.mult, ALU.mult).then_inc(w_hi, 1)
                pool.wait_ge(w_hi, n + 1)
                nc.gpsimd.tensor_tensor(lo, stage[:, n % STAGES, :], hi.bitcast(F32), ALU.subtract).then_inc(w_ready, 1)

        @block.tensor
        def _(pe):
            def mm3(o, l, r, first, last):
                nc.tensor.matmul(o, l[0], r[0], start=first, stop=False)
                nc.tensor.matmul(o, l[0], r[1], start=False, stop=False)
                return nc.tensor.matmul(o, l[1], r[0], start=False, stop=last)

            def bank(n, s_=slice(0, 512), rows=slice(0, P)):
                return ring[rows, n % 4, s_]

            def group(n, k, *needs):
                pe.wait_ge(operand_ready, n + max(k - 3, *needs, -3))

            def weights(name):
                pe.wait_ge(w_ready, index_of[name] + 1)
                return w(name)

            def cut(parts, *index):
                return [p_[index] for p_ in parts]

            def transposes(n0, m0, src, k, count=1):
                for t in range(T):
                    last = nc.tensor.transpose(ring[:, (m0 + k) % 4, t * P:(t + 1) * P],
                                               src[:, t, k * P:(k + 1) * P], ident[:])
                last.then_inc(psum_full, count)

            def TR(ph, n0, m0, nth, src=None, spare=0):
                if nth is not None:
                    pe.wait_ge(xn_ready, nth)
                for k in range(KT):
                    group(n0, k)
                    transposes(n0, m0, xn if src is None else src, k, 1 + (spare if k == KT - 1 else 0))

            def start_k0(n):
                if n >= 4:
                    pe.wait_ge(operand_ready, n - 3)

            def phase_K0():
                ctxp = [weights(("ctx", k)) for k in range(2)]
                c4 = [[p_.rearrange("p (b u m) -> p b u m", b=B, u=2) for p_ in c_] for c_ in ctxp]
                n = 0
                wm = [weights(("wmem", k)) for k in range(2)]
                for b in range(B):
                    start_k0(n)
                    for k in range(2):
                        last = mm3(bank(n), [p_[:, b, :, :] for p_ in c4[k]], wm[k], k == 0, k == 1)
                    last.then_inc(psum_full, 1)
                    n += 1
                for d in range(KT):
                    start_k0(n)
                    for k in range(2):
                        last = mm3(bank(n, slice(0, B * M)), cut(wm[k], slice(None), slice(d * P, (d + 1) * P)),
                                   [p_[:, :, 0, :] for p_ in c4[k]], k == 0, k == 1)
                    last.then_inc(psum_full, 1)
                    n += 1
                for l in "12":
                    for pair in range(PAIRS):
                        start_k0(n)
                        for k in range(2):
                            wk = weights((f"wkv{l}", (pair // 4) * 2 + k))
                            last = mm3(bank(n, slice(0, B * M)),
                                       cut(wk, slice(None), slice((pair % 4) * P, (pair % 4 + 1) * P)),
                                       [p_[:, :, 0, :] for p_ in c4[k]], k == 0, k == 1)
                        last.then_inc(psum_full, 1)
                        n += 1
                    for h in range(2):
                        for b in range(B):
                            start_k0(n)
                            for k in range(2):
                                wv = weights((f"wkv{l}", 4 + h * 2 + k))
                                last = mm3(bank(n), [p_[:, b, :, :] for p_ in c4[k]], wv, k == 0, k == 1)
                            last.then_inc(psum_full, 1)
                            n += 1
                ck = [weights(("ckv", k)) for k in range(2)]
                for f in range(2):
                    start_k0(n)
                    for k in range(2):
                        last = mm3(bank(n, slice(0, B * M)), cut(ck[k], slice(None), slice(f * P, (f + 1) * P)),
                                   [p_[:, :, 0, :] for p_ in c4[k]], k == 0, k == 1)
                    last.then_inc(psum_full, 1)
                    n += 1
                for b in range(B):
                    start_k0(n)
                    for k in range(2):
                        last = mm3(bank(n, slice(0, MD)), [p_[:, b, :, :] for p_ in c4[k]],
                                   cut(ck[k], slice(None), slice(MD, 2 * MD)), k == 0, k == 1)
                    last.then_inc(psum_full, 1)
                    n += 1
                assert n == N_K0

            def phase_G():
                n0 = seq0["G"]
                with pe.Fori(0, B) as b:
                    n = n0 + b * 16
                    m = n0 % 4
                    TR("G", n, m, xn0["G"] + b + 1)
                    for s in range(2):
                        group(n, 4 + s, 4)
                        for tt in range(2):
                            t = 2 * s + tt
                            for k in range(KT):
                                last = mm3(ring[:, (m + 4 + s) % 4, tt * M:(tt + 1) * M],
                                           cut(xT, slice(None), k, slice(t * P, (t + 1) * P)),
                                           [p_[:, k, bass.ds(b * M, M)] for p_ in mpT], k == 0, k == KT - 1)
                        last.then_inc(psum_full, 1)
                    for s in range(2):
                        group(n, 6 + s, 5 + s)
                        pe.sem_inc(pe_passed, 1)
                        for tt in range(2):
                            last = nc.tensor.transpose(ring[0:M, (m + 6 + s) % 4, tt * P:(tt + 1) * P],
                                                       gP[:, 2 * s + tt, :], ident[:])
                        last.then_inc(psum_full, 1)
                    for t in range(T):
                        group(n, 8 + t, 7 + t // 2)
                        pe.sem_inc(pe_passed, 1)
                        mm3(ring[:, (m + 8 + t) % 4, :], cut(gPT, slice(None), slice(t * P, (t + 1) * P)),
                            [p_[:, bass.ds(b, 1), :].rearrange("p o d -> p (o d)") for p_ in mpM],
                            True, True).then_inc(psum_full, 1)
                    for k in range(KT):
                        group(n, 12 + k, 12)
                        transposes(n + 12, m, ctxf, k)
                    pe.wait_ge(x_done, xd0["G"] + b * T)
                    for half, src in ((0, xT), (1, cT)):
                        if half:
                            pe.wait_ge(operand_ready, n + 16)
                        for k in range(KT):
                            wg = weights(("wg", half * KT + k))
                            for t in range(T):
                                last = mm3(y_psum[:, t, :], cut(src, slice(None), k, slice(t * P, (t + 1) * P)), wg,
                                           half == 0 and k == 0, half == 1 and k == KT - 1)
                    last.then_inc(y_done, 1)

            def phase_A(l):
                ph = "A" + l
                start = seq0[ph]

                def Q(h, n, m, k0, scores_end=None):
                    if scores_end is not None:
                        pe.wait_ge(scores_copied, scores_end)
                    for p in range(4):
                        if scores_end is None:
                            group(n, k0 + p, k0)
                        wq = [part.rearrange("p (k c) -> p k c", k=KT) for part in weights((f"wq{l}", 4 * h + p))]
                        for k in range(KT):
                            last = mm3(ring[:, (m + k0 + p) % 4, :], cut(wq, slice(None), k),
                                       cut(xT, slice(None), k), k == 0, k == KT - 1)
                        last.then_inc(psum_full, 1)

                def S(h, n, m, k0, q_end):
                    for t in range(T):
                        group(n, k0 + t, q_end)
                        for p in range(4):
                            last = mm3(ring[:, (m + k0 + t) % 4, p * P:(p + 1) * P],
                                       cut(qT, slice(None), p, slice(t * P, (t + 1) * P)),
                                       cut(kbd, slice(None), slice((4 * h + p) * P, (4 * h + p + 1) * P)), True, True)
                        last.then_inc(psum_full, 1)

                def TO(h, n, m, k0, s_end):
                    for i, (kind, p) in enumerate(TO_ORDER):
                        if kind == "T":
                            group(n, k0 + i, s_end)
                            for t in range(T):
                                last = nc.tensor.transpose(ring[:, (m + k0 + i) % 4, t * P:(t + 1) * P],
                                                           pr[:, t, p * P:(p + 1) * P], ident[:])
                        else:
                            group(n, k0 + i, k0 + TO_ORDER.index(("T", p)) + 1)
                            last = mm3(ring[:, (m + k0 + i) % 4, :],
                                       cut(vbd, slice(None), slice((4 * h + p) * P, (4 * h + p + 1) * P)),
                                       cut(pT, slice(None), p % 2), True, True)
                        last.then_inc(psum_full, 1)

                def W(h, n, k0):
                    for p in range(4):
                        pe.wait_ge(operand_ready, n + k0 + TO_ORDER.index(("O", p)) + 1)
                        wo = weights((f"wo{l}", 4 * h + p))
                        for t in range(T):
                            last = mm3(y_psum[:, t, :], cut(oT, slice(None), p, slice(t * P, (t + 1) * P)), wo,
                                       h == 0 and p == 0, h == 1 and p == 3)
                        last.then_inc(y_done, 1)

                def body(b, n, m, last):
                    at, _ = a_layout(last)
                    u0 = copied0[ph] + b * 8
                    kv = ("12".index(l) * B + b + 1) * 32
                    pe.wait_ge(k_loaded, kv)
                    S(0, n, m, at["S0"], 0)
                    pe.wait_ge(v_loaded, kv)
                    Q(1, n, m, at["Q1"], u0 + 4)
                    TO(0, n, m, at["TO0"], at["S0"] + 4)
                    if not last:
                        TR(ph, n + at["TR"], m + at["TR"], xn0[ph] + b + 2)
                    S(1, n, m, at["S1"], at["Q1"] + 4)
                    pe.wait_ge(x_done, xd0[ph] + b * T)
                    W(0, n, at["TO0"])
                    if not last:
                        pe.wait_ge(operand_ready, n + at["TR"] + 4)
                        Q(0, n, m, at["Q2"], u0 + 8)
                    TO(1, n, m, at["TO1"], at["S1"] + 4)
                    W(1, n, at["TO1"])

                TR(ph, start, start, xn0[ph] + 1)
                Q(0, start, start, 4)
                with pe.Fori(0, B - 1) as b:
                    body(b, start + 8 + b * 36, start + 8, False)
                body(B - 1, start + 8 + (B - 1) * 36, start + 8, True)

            def phase_F(l):
                ph = "F" + l
                start = seq0[ph]

                def up(j, n, m):
                    group(n, j, 0)
                    w1 = [p_.rearrange("p (k c) -> p k c", k=KT) for p_ in weights((f"w1_{l}", j))]
                    for k in range(KT):
                        last = mm3(ring[:, (m + j) % 4, :], cut(w1, slice(None), k), cut(xT, slice(None), k),
                                   k == 0, k == KT - 1)
                    last.then_inc(psum_full, 1)

                def down(j, n):
                    pe.wait_ge(operand_ready, n + j + 1)
                    w2 = weights((f"w2_{l}", j))
                    for t in range(T):
                        last = mm3(y_psum[:, t, :], cut(hT, slice(None), slice(t * P, (t + 1) * P)), w2,
                                   j == 0, j == FF - 1)
                    last.then_inc(y_done, 1)

                def body(b, n, m, last):
                    up(0, n, m)
                    pe.wait_ge(x_done, xd0[ph] + b * T)
                    for j in range(1, FF):
                        up(j, n, m)
                        down(j - 1, n)
                    if not last:
                        TR(ph, n + FF, m + FF, xn0[ph] + b + 2)
                    down(FF - 1, n)

                TR(ph, start, start, xn0[ph] + 1)
                with pe.Fori(0, B - 1) as b:
                    body(b, start + 4 + b * 20, start + 4, False)
                body(B - 1, start + 4 + (B - 1) * 20, start + 4, True)

            def phase_Q3():
                start = seq0["Q3"]

                def body(b, n, m, last):
                    for kind, t, k0 in q3_order(last):
                        if kind == "P":
                            for c in range(3):
                                group(n, k0 + c, 0)
                                wl = [weights(("qkv_l", 4 * c + k)) for k in range(KT)]
                                wv = [weights(("qkv_v", 4 * c + k)) for k in range(KT)]
                                for i, (src, w_) in enumerate(((xT, wl), (xTv, wv))):
                                    for k in range(KT):
                                        last_mm = mm3(ring[:, (m + k0 + c) % 4, :],
                                                      cut(src, slice(None), k, slice(t * P, (t + 1) * P)), w_[k],
                                                      i == 0 and k == 0, i == 1 and k == KT - 1)
                                last_mm.then_inc(psum_full, 1)
                        elif kind == "X":
                            at_p = [k_ for x_, t_, k_ in q3_order(last) if (x_, t_) == ("P", t)][0]
                            for c in range(2):
                                group(n, k0 + c, at_p + c + 1)
                                for f in range(KT):
                                    last_mm = nc.tensor.transpose(ring[:, (m + k0 + c) % 4, f * P:(f + 1) * P],
                                                                  r3[:, t % 2, c, f * P:(f + 1) * P], ident[:])
                                last_mm.then_inc(psum_full, 1)
                        else:
                            TR("Q3", n + k0, m + k0, xn0["Q3"] + b + 2, xn if kind == "TRl" else xnv)

                TR("Q3", start, start, xn0["Q3"] + 1)
                TR("Q3", start + 4, start + 4, None, xnv)
                with pe.Fori(0, B - 1) as b:
                    body(b, start + 8 + b * 28, start + 8, False)
                body(B - 1, start + 8 + (B - 1) * 28, start + 8, True)

            def phase_A3():
                H = HEADS3 * T

                def where(h):
                    return h // 16, h // 4 % 4, h % 4

                pe.wait_ge(operand_ready, seq0["A3"])
                with pe.Fori(0, B) as b:
                    h0, u0 = b * H, b * (H // 4)

                    def S(h):
                        g, t, r = where(h)
                        if h % 16 == 0:
                            pe.wait_ge(qkv_loaded[g % 2], 96 * 2 * b + 96 * (g // 2 + 1))
                        if h == 0:
                            pe.wait_ge(x_done, xd0["A3"] + b * T)
                        if h >= 4:
                            pe.wait_ge(p3_ready, h0 + h - 3)
                        pe.sem_inc(pe_passed, 1)
                        rows = slice(HD3 * r, HD3 * (r + 1))
                        mm3(ring[:, h % 4, 0:(t + 1) * P], cut(q3, rows, g % 2, slice(t * P, (t + 1) * P)),
                            cut(k3, rows, g % 2, slice(0, (t + 1) * P)), True, True).then_inc(sc3_full, 1)

                    def T3(h):
                        g, t, r = where(h)
                        pe.wait_ge(p3_ready, h0 + h + 1)
                        if h >= 2:
                            pe.wait_ge(pt3_ready, h0 + h - 1)
                        pe.sem_inc(pe_passed, 1)
                        for k in range(t + 1):
                            last = nc.tensor.transpose(y_psum[:, h % 2, k * P:(k + 1) * P],
                                                       p3[:, h % 4, k * P:(k + 1) * P], ident[:])
                        last.then_inc(pt3_full, 1)

                    def PV(h):
                        g, t, r = where(h)
                        pe.wait_ge(pt3_ready, h0 + h + 1)
                        u = h // 4
                        if r == 0:
                            pe.wait_ge(o3_ready, u0 + max(u - 1, 0) + 1)
                        pe.sem_inc(pe_passed, 1)
                        for k in range(t + 1):
                            last = mm3(y_psum[:, 2 + u % 2, HD3 * r:HD3 * (r + 1)],
                                       cut(pT3, slice(None), h % 2, slice(k * P, (k + 1) * P)),
                                       cut(v3, slice(None), g % 2, k, slice(HD3 * r, HD3 * (r + 1))), k == 0, k == t)
                        last.then_inc(pv3_done, 1)

                    def X(u):
                        pe.wait_ge(o3_ready, u0 + u + 2)
                        if u > 1:
                            pe.wait_ge(ox3_ready, u0 + u - 1)
                        pe.sem_inc(pe_passed, 1)
                        nc.tensor.transpose(y_psum[:, 2 + u % 2, P:2 * P], o3[:, u % 2, :], ident[:]).then_inc(ox3_full, 1)

                    for h in range(3):
                        S(h)
                    for h in range(H + 6):
                        if h + 3 < H:
                            S(h + 3)
                        if h < H:
                            T3(h)
                        if 1 <= h <= H:
                            PV(h - 1)
                        if h >= 6 and h % 4 == 2:
                            X((h - 6) // 4)
                    for i in range(2 * T):
                        t, e = i // 2, "lv"[i % 2]
                        if i >= 4:
                            pe.wait_ge(*((dense_added, b * T + t - 1) if i % 2 == 0 else (x_done, xd0["A3"] + b * T + t - 1)))
                        else:
                            pe.wait_ge(ox3_ready, u0 + H // 4)
                        for k in range(KT):
                            last = mm3(ring[:, i % 4, :], cut(oT3, slice(None), k, slice(t * P, (t + 1) * P)),
                                       weights((f"dense_{e}", k)), k == 0, k == KT - 1)
                        last.then_inc(dense_full, 1)

            def phase_C3():
                start = seq0["C3"]

                def Q(n, m, k0):
                    cw = [[part.rearrange("p (k c) -> p k c", k=2) for part in weights(("cq", i))] for i in range(2)]
                    for f in range(2):
                        group(n, k0 + f, k0)
                        for k in range(KT):
                            last = mm3(ring[:, (m + k0 + f) % 4, :],
                                       cut(cw[k // 2], slice(None), k % 2, slice(f * P, (f + 1) * P)),
                                       cut(xT, slice(None), k), k == 0, k == KT - 1)
                        last.then_inc(psum_full, 1)

                def body(b, n, m, last):
                    kv = (2 * B + b + 1) * 32
                    pe.wait_ge(k_loaded, kv)
                    for i in range(2 * T):
                        f, t = i // T, i % T
                        if i >= 4:
                            pe.wait_ge(scores_copied, copied0["C3"] + b * 8 + i - 3)
                        else:
                            group(n, i, 0)
                        mm3(ring[:, (m + i) % 4, :], cut(cqT, slice(None), f, slice(t * P, (t + 1) * P)),
                            cut(ckbd, slice(None), slice(f * 512, (f + 1) * 512)), True, True).then_inc(psum_full, 1)
                    k0 = 8
                    if not last:
                        pe.wait_ge(scores_copied, copied0["C3"] + b * 8 + 8)
                        pe.wait_ge(xn_ready, xn0["C3"] + b + 2)
                        for k in range(KT):
                            transposes(n + k0, m + k0, xn, k)
                        k0 += 4
                    pe.wait_ge(v_loaded, kv)
                    for f in range(2):
                        for p in range(5):
                            if p < 4:
                                group(n, k0, 4 * f + 4)
                                for t in range(T):
                                    last_mm = nc.tensor.transpose(ring[:, (m + k0) % 4, t * P:(t + 1) * P],
                                                                  cpr[:, f * T + t, p * P:(p + 1) * P], ident[:])
                                last_mm.then_inc(psum_full, 1)
                                k0 += 1
                            if p:
                                pe.wait_ge(operand_ready, n + k0 - (1 if p < 4 else 0))
                                col = f * 512 + (p - 1) * P
                                at_o = k0 + 3 - p if p < 4 else k0
                                last_mm = mm3(ring[:, (m + at_o) % 4, :], cut(cvbd, slice(None), slice(col, col + P)),
                                              cut(cpT, slice(None), (p - 1) % 2), p == 1, p == 4)
                        last_mm.then_inc(psum_full, 1)
                        k0 += 1
                    if not last:
                        Q(n, m, k0)
                    pe.wait_ge(x_done, xd0["C3"] + b * T)
                    pe.wait_ge(operand_ready, n + k0)
                    for f in range(2):
                        wd = weights(("cdense", f))
                        for t in range(T):
                            last_mm = mm3(y_psum[:, t, :], cut(coT, slice(None), f, slice(t * P, (t + 1) * P)), wd,
                                          f == 0, f == 1)
                    last_mm.then_inc(y_done, 1)

                TR("C3", start, start, xn0["C3"] + 1)
                Q(start, start, 4)
                with pe.Fori(0, B - 1) as b:
                    body(b, start + 6 + b * 24, start + 6, False)
                body(B - 1, start + 6 + (B - 1) * 24, start + 6, True)

            def phase_M(e):
                ph = "M" + e
                start = seq0[ph]

                def up(j, n, m):
                    for i, name in enumerate(("gate", "up")):
                        group(n, 2 * j + i, 0)
                        wu = [p_.rearrange("p (k c) -> p k c", k=KT) for p_ in weights((f"{name}_{e}", j))]
                        for k in range(KT):
                            last = mm3(ring[:, (m + 2 * j + i) % 4, :], cut(wu, slice(None), k),
                                       cut(xT, slice(None), k), k == 0, k == KT - 1)
                        last.then_inc(psum_full, 1)

                def down(j, n):
                    pe.wait_ge(operand_ready, n + 2 * j + 2)
                    wd = weights((f"down_{e}", j))
                    for t in range(T):
                        last = mm3(y_psum[:, t, :], cut(mT, slice(None), slice(t * P, (t + 1) * P)), wd,
                                   j == 0, j == HT - 1)
                    last.then_inc(y_done, 1)

                def body(b, n, m, last):
                    up(0, n, m)
                    pe.wait_ge(x_done, xd0[ph] + b * T)
                    for j in range(1, HT):
                        up(j, n, m)
                        down(j - 1, n)
                    if not last:
                        TR(ph, n + 2 * HT, m + 2 * HT, xn0[ph] + b + 2, spare=2)
                    down(HT - 1, n)

                TR(ph, start, start, xn0[ph] + 1, spare=2)
                with pe.Fori(0, B - 1) as b:
                    body(b, start + 6 + b * 28, start + 6, False)
                body(B - 1, start + 6 + (B - 1) * 28, start + 6, True)

            pe.wait_ge(consts_loaded, CONSTS)
            for ph in phases:
                if ph in ("A1", "A2"):
                    phase_A(ph[1])
                elif ph[0] in "FM":
                    (phase_F if ph[0] == "F" else phase_M)(ph[1])
                else:
                    {"K0": phase_K0, "G": phase_G, "Q3": phase_Q3, "A3": phase_A3, "C3": phase_C3}[ph]()

        @block.scalar
        def _(act):
            def hi_copy(dst, src, n, scale=1.0):
                act.wait_ge(psum_full, n + 1)
                return nc.scalar.activation(dst, src, ACT.Copy, scale=scale).then_inc(act_out, 1)

            def load_kv(li, kv, b, dst, s):
                for i in range(2):
                    act.dma_start(dst[i][:].bitcast(F32),
                                  t_in["kv_scratch"][li][kv][i][bass.ds(b * P, P), :]).then_inc(s, 16)

            def phase_K0():
                n = 0
                for b in range(B):
                    hi_copy(mpM[0][:, b, :], ring[0:M, n % 4, :], n)
                    n += 1
                for d in range(KT):
                    hi_copy(mpT[0][:, d, :], ring[:, n % 4, 0:B * M], n)
                    n += 1
                act.wait_ge(zeroed, 1)
                bdh = bd[0][:].rearrange("p b (q c) -> p b q c", q=PAIRS)
                for r, l in enumerate("12"):
                    if r:
                        act.wait_ge(bd_stored, 32 * 2 * r)
                    for pair in range(PAIRS):
                        act.wait_ge(psum_full, n + 1)
                        src = ring[:, n % 4, 0:B * M].rearrange("p (b m) -> p b m", b=B)
                        nc.scalar.activation(bdh[0:64, :, pair, 0:64], src[0:64], ACT.Copy)
                        nc.scalar.activation(bdh[64:128, :, pair, 64:128], src[64:128], ACT.Copy).then_inc(act_out, 1)
                        n += 1
                    act.wait_ge(operand_ready, n)
                    for i in range(2):
                        act.dma_start(t_in["kv_scratch"][r][0][i].rearrange("(b p) c -> p b c", p=P),
                                      bd[i][:].bitcast(F32)).then_inc(bd_stored, 16)
                    act.wait_ge(bd_stored, 32 * (2 * r + 1))
                    for h in range(2):
                        for b in range(B):
                            act.wait_ge(psum_full, n + 1)
                            src = ring[:, n % 4, :].rearrange("p (q u c) -> p q u c", q=4, u=2)
                            nc.scalar.activation(bdh[0:64, b, 4 * h:4 * h + 4, 0:64], src[0:64, :, 0, :], ACT.Copy)
                            nc.scalar.activation(bdh[64:128, b, 4 * h:4 * h + 4, 64:128], src[64:128, :, 1, :],
                                                 ACT.Copy).then_inc(act_out, 1)
                            n += 1
                    act.wait_ge(operand_ready, n)
                    for i in range(2):
                        act.dma_start(t_in["kv_scratch"][r][1][i].rearrange("(b p) c -> p b c", p=P),
                                      bd[i][:].bitcast(F32)).then_inc(bd_stored, 16)
                act.wait_ge(operand_ready, n + 2)
                for i in range(2):
                    act.dma_start(t_in["kv_scratch"][2][0][i].rearrange("(b p) c -> p b c", p=P),
                                  bd[i][:].bitcast(F32)).then_inc(bd_stored, 16)
                act.wait_ge(operand_ready, n + 6)
                for i in range(2):
                    act.dma_start(t_in["kv_scratch"][2][1][i].rearrange("(b p) c -> p b c", p=P),
                                  bd[i][:].bitcast(F32)).then_inc(bd_stored, 16)
                act.wait_ge(bd_stored, 32 * 6)
                act.wait_ge(act_out, n)
                act.sem_inc(act_out, 6)

            def phase_G():
                act.dma_start(gbias[:], t_in["b_gate"]).then_inc(consts_loaded, 16)
                act.dma_start(gnorm[:], t_in["norm_w"]).then_inc(consts_loaded, 16)
                with act.Fori(0, B) as b:
                    n = seq0["G"] + b * 16
                    m = seq0["G"] % 4
                    for k in range(KT):
                        hi_copy(xT[0][:, k, :], ring[:, (m + k) % 4, :], n + k)
                    for s in range(2):
                        act.wait_ge(scores_shifted, s0["G"] + b * 2 + s + 1)
                        nc.scalar.activation(gP[:, 2 * s:2 * s + 2, :], gs[:, 2 * s:2 * s + 2, :],
                                             ACT.Exp).then_inc(act_out, 1)
                    for s in range(2):
                        hi_copy(gPT[0][:, s * 256:(s + 1) * 256], ring[0:M, (m + 6 + s) % 4, 0:256], n + 6 + s)
                    for t in range(T):
                        hi_copy(ctxf[:, t, :], ring[:, (m + 8 + t) % 4, :], n + 8 + t)
                    for k in range(KT):
                        hi_copy(cT[0][:, k, :], ring[:, (m + 12 + k) % 4, :], n + 12 + k)
                    for t in range(T):
                        act.wait_ge(gate_in, b * T + t + 1)
                        nc.scalar.activation(gz[:, t % 2, :], gz[:, t % 2, :], ACT.Sigmoid).then_inc(gate_out, 1)

            def norm_T(ph, n, m, g, bias):
                act.wait_ge(psum_full, n + KT)
                for k in range(KT):
                    nc.scalar.activation(xn[:, k, :], ring[:, (m + k) % 4, :], ACT.Identity,
                                         scale=par[:, g, k:k + 1], bias=par[:, bias, k:k + 1]).then_inc(act_out, 1)

            def phase_A(l):
                ph = "A" + l
                li = "12".index(l)
                g, bias = PARAMS.index(f"L{l}_xattn_ln_q_g"), PARAMS.index(f"L{l}_xattn_ln_q_b")
                start = seq0[ph]
                act.wait_ge(x_done, xd0[ph])
                load_kv(li, 0, 0, kbd, k_loaded)
                load_kv(li, 1, 0, vbd, v_loaded)

                def Q(n, m):
                    for p in range(4):
                        hi_copy(qT[0][:, p, :], ring[:, (m + p) % 4, :], n + p, 0.125)

                def S(s_at, n):
                    for t in range(T):
                        act.wait_ge(scores_shifted, s_at + t + 1)
                        nc.scalar.activation(pr[:, t, :], sc[:, t % 2, :], ACT.Exp).then_inc(act_out, 1)

                def TO(n, m):
                    for i, (kind, p) in enumerate(TO_ORDER):
                        dst = pT[0][:, p % 2, :] if kind == "T" else oT[0][:, p, :]
                        hi_copy(dst, ring[:, (m + i) % 4, :], n + i)

                def body(b, n, m, last):
                    at, _ = a_layout(last)
                    u0 = s0[ph] + b * 8
                    S(u0, n + at["S0"])
                    Q(n + at["Q1"], m + at["Q1"])
                    TO(n + at["TO0"], m + at["TO0"])
                    if not last:
                        norm_T(ph, n + at["TR"], m + at["TR"], g, bias)
                    S(u0 + 4, n + at["S1"])
                    if not last:
                        Q(n + at["Q2"], m + at["Q2"])
                        load_kv(li, 0, b + 1, kbd, k_loaded)
                    TO(n + at["TO1"], m + at["TO1"])
                    if not last:
                        load_kv(li, 1, b + 1, vbd, v_loaded)

                norm_T(ph, start, start, g, bias)
                Q(start + 4, start + 4)
                with act.Fori(0, B - 1) as b:
                    body(b, start + 8 + b * 36, start + 8, False)
                body(B - 1, start + 8 + (B - 1) * 36, start + 8, True)

            def phase_F(l):
                ph = "F" + l
                g, bias = PARAMS.index(f"L{l}_xattn_ln_ff_g"), PARAMS.index(f"L{l}_xattn_ln_ff_b")
                start = seq0[ph]

                def body(b, n, m, last):
                    for j in range(FF):
                        act.wait_ge(psum_full, n + j + 1)
                        act.wait_ge(operand_ready, n + j)
                        nc.scalar.activation(hf[:], ring[:, (m + j) % 4, :], ACT.Gelu).then_inc(act_out, 1)
                    if not last:
                        norm_T(ph, n + FF, m + FF, g, bias)

                norm_T(ph, start, start, g, bias)
                with act.Fori(0, B - 1) as b:
                    body(b, start + 4 + b * 20, start + 4, False)
                body(B - 1, start + 4 + (B - 1) * 20, start + 4, True)

            def norm_hi(dst, n, m, g, spare=0):
                for k in range(KT):
                    act.wait_ge(psum_full, n + k + 1)
                    nc.scalar.activation(dst[0][:, k, :], ring[:, (m + k) % 4, :], ACT.Copy,
                                         scale=par[:, g, k:k + 1]).then_inc(act_out, 1 + (spare if k == KT - 1 else 0))

            def phase_Q3():
                start = seq0["Q3"]
                g = PARAMS.index("L3_xattn_ln_in_w")

                def body(b, n, m, last):
                    for kind, t, k0 in q3_order(last):
                        if kind == "P":
                            act.wait_ge(v_stored, 32 * (b * T + t + 1))
                            act.wait_ge(psum_full, n + k0 + 3)
                            act.sem_inc(act_passed, 1)
                            nc.scalar.activation(v_out[0][:], ring[:, (m + k0 + 2) % 4, :], ACT.Copy).then_inc(act_out, 3)
                            act.wait_ge(operand_ready, n + k0 + 3)
                            for i in range(2):
                                act.dma_start(t_in["qkv_scratch"][2][i][bass.ds(b * SEQ + t * P, P), :],
                                              v_out[i][:].bitcast(F32)).then_inc(v_stored, 16)
                        elif kind == "X":
                            for c, s in enumerate((q_stored, k_stored)):
                                act.wait_ge(s, 32 * (b * T + t + 1))
                                act.wait_ge(psum_full, n + k0 + c + 1)
                                act.sem_inc(act_passed, 1)
                                nc.scalar.activation(qk_out[0][:, c, :], ring[:, (m + k0 + c) % 4, :],
                                                     ACT.Copy).then_inc(act_out, 1)
                            for c, s in enumerate((q_stored, k_stored)):
                                act.wait_ge(operand_ready, n + k0 + c + 1)
                                for i in range(2):
                                    rows = t_in["qkv_scratch"][c][i][bass.ds(b * SEQ, SEQ), t * P:(t + 1) * P]
                                    act.dma_start(rows.rearrange("(f p) c -> p f c", p=P),
                                                  qk_out[i][:, c, :].rearrange("p (f c) -> p f c", f=KT).bitcast(F32)
                                                  ).then_inc(s, 16)
                        else:
                            norm_hi(xT if kind == "TRl" else xTv, n + k0, m + k0, g)

                for s in (q_stored, k_stored, v_stored):
                    act.sem_inc(s, 32)
                norm_hi(xT, start, start, g)
                norm_hi(xTv, start + 4, start + 4, g)
                with act.Fori(0, B - 1) as b:
                    body(b, start + 8 + b * 28, start + 8, False)
                body(B - 1, start + 8 + (B - 1) * 28, start + 8, True)

            def phase_A3():
                H = HEADS3 * T
                scale = float(HD3) ** -0.5

                def load_quad(b, g):
                    s = qkv_loaded[g % 2]
                    q_, k_, v_ = t_in["qkv_scratch"]
                    for i in range(2):
                        act.dma_start(q3[i][:, g % 2, :].bitcast(F32), q_[i][bass.ds(b * SEQ + g * P, P), :]).then_inc(s, 16)
                        act.dma_start(k3[i][:, g % 2, :].bitcast(F32), k_[i][bass.ds(b * SEQ + g * P, P), :]).then_inc(s, 16)
                        act.dma_start(v3[i][:, g % 2, :, :].bitcast(F32),
                                      v_[i][bass.ds(b * SEQ, SEQ), g * P:(g + 1) * P].rearrange("(t p) c -> p t c", p=P)
                                      ).then_inc(s, 16)

                act.wait_ge(operand_ready, seq0["A3"])
                act.dma_start(causal[:], t_in["causal"]).then_inc(consts_loaded, 16)
                for s in (q_stored, k_stored, v_stored):
                    act.wait_ge(s, 32 * (B * T + 1))
                load_quad(0, 0)
                load_quad(0, 1)

                def body(b, last):
                    h0, u0 = b * H, b * (H // 4)

                    def E(h):
                        t = h // 4 % 4
                        act.wait_ge(sc3_max, h0 + h + 1)
                        nc.scalar.activation(p3[:, h % 4, 0:(t + 1) * P], ring[:, h % 4, 0:(t + 1) * P], ACT.Exp,
                                             bias=nm3[:, 1, h:h + 1], scale=scale,
                                             accum_out=sum3[:, h:h + 1]).then_inc(p3_ready, 1)

                    E(0)
                    for h in range(H + 4):
                        if h + 1 < H:
                            E(h + 1)
                        if h < H:
                            n = (h // 4 % 4 + 1) * P
                            act.wait_ge(pt3_full, h0 + h + 1)
                            nc.scalar.activation(pT3[0][:, h % 2, 0:n], y_psum[:, h % 2, 0:n], ACT.Copy).then_inc(pt3_hi, 1)
                        if h >= 7 and h % 4 == 3:
                            u = (h - 7) // 4
                            g, t = u // 4, u % 4
                            act.wait_ge(ox3_full, u0 + u + 1)
                            nc.scalar.activation(oT3[0][:, g, t * P:(t + 1) * P], y_psum[:, 2 + u % 2, P:2 * P],
                                                 ACT.Copy).then_inc(ox3_hi, 1)
                        if h in (18, 34) or (h == 50 and not last):
                            act.wait_ge(pv3_done, h0 + h - 2)
                            if h == 50:
                                load_quad(b + 1, 0)
                            else:
                                load_quad(b, (h + 14) // 16)
                    if not last:
                        load_quad(b + 1, 1)

                with act.Fori(0, B - 1) as b:
                    body(b, False)
                body(B - 1, True)

            def phase_C3():
                start = seq0["C3"]
                g = PARAMS.index("L3_xattn_ln_post_cross_w")
                act.wait_ge(x_done, xd0["C3"])
                load_kv(2, 0, 0, ckbd, k_loaded)
                load_kv(2, 1, 0, cvbd, v_loaded)

                def Q(n, m):
                    for f in range(2):
                        hi_copy(cqT[0][:, f, :], ring[:, (m + f) % 4, :], n + f)

                def body(b, n, m, last):
                    for i in range(2 * T):
                        act.wait_ge(scores_copied, copied0["C3"] + b * 8 + i + 1)
                        nc.scalar.activation(cpr[:, i, :], csc[:, i % 2, :], ACT.Exp, scale=0.25).then_inc(act_out, 1)
                    k0 = 8
                    if not last:
                        norm_hi(xT, n + k0, m + k0, g)
                        k0 += 4
                        load_kv(2, 0, b + 1, ckbd, k_loaded)
                    for f in range(2):
                        for p in range(5):
                            dst = cpT[0][:, p % 2, :] if p < 4 else coT[0][:, f, :]
                            hi_copy(dst, ring[:, (m + k0) % 4, :], n + k0)
                            k0 += 1
                    if not last:
                        load_kv(2, 1, b + 1, cvbd, v_loaded)
                        Q(n + k0, m + k0)

                norm_hi(xT, start, start, g)
                Q(start + 4, start + 4)
                with act.Fori(0, B - 1) as b:
                    body(b, start + 6 + b * 24, start + 6, False)
                body(B - 1, start + 6 + (B - 1) * 24, start + 6, True)

            def phase_M(e):
                ph = "M" + e
                start = seq0[ph]
                g = PARAMS.index("L3_xattn_ln_post_attn_w")

                def body(b, n, m, last):
                    for j in range(HT):
                        act.wait_ge(psum_full, n + 2 * j + 1)
                        nc.scalar.activation(sg[:], ring[:, (m + 2 * j) % 4, :], ACT.Silu).then_inc(act_out, 1)
                        act.wait_ge(operand_ready, n + 2 * j + 1)
                        if j:
                            act.wait_ge(y_done, y0[ph] + b * HT + j)
                        nc.scalar.activation(mT[0][:], mf[:], ACT.Copy).then_inc(act_out, 1)
                    if not last:
                        norm_hi(xT, n + 2 * HT, m + 2 * HT, g, 2)

                norm_hi(xT, start, start, g, 2)
                with act.Fori(0, B - 1) as b:
                    body(b, start + 6 + b * 28, start + 6, False)
                body(B - 1, start + 6 + (B - 1) * 28, start + 6, True)

            for dst, src in ((ident[:], t_in["ident"]), (par[:], t_in["params"]), (gates[:], t_in["gates"]),
                             (mask8[:], t_in["mask_s2"]), (mask_k[:], t_in["mask_k"]), (mask_v[:], t_in["mask_v"]),
                             (types[:], t_in["types"]), (pos[:], t_in["pos"])):
                act.dma_start(dst, src).then_inc(consts_loaded, 16)
            for b in range(B):
                act.dma_start(x[:, b * T:(b + 1) * T, :],
                              t_in["x"][b * SEQ:(b + 1) * SEQ, :].rearrange("(t p) d -> p t d", p=P)).then_inc(x_loaded, 16)
            act.wait_ge(consts_loaded, CONSTS)
            nc.scalar.activation(gates[:], gates[:], ACT.Tanh).then_inc(tanh_done, 1)
            for ph in phases:
                if ph in ("A1", "A2"):
                    phase_A(ph[1])
                elif ph[0] in "FM":
                    (phase_F if ph[0] == "F" else phase_M)(ph[1])
                else:
                    {"K0": phase_K0, "G": phase_G, "Q3": phase_Q3, "A3": phase_A3, "C3": phase_C3}[ph]()

        @block.vector
        def _(dve):
            steps = {"base": 0, "n": 0}

            def step(ins):
                ins.then_inc(dve_step, 1)
                steps["n"] += 1

            def settle():
                dve.wait_ge(dve_step, steps["base"] + steps["n"])

            def loop(count, per, run):
                base = steps["base"] + steps["n"]
                with dve.Fori(0, count) as i:
                    steps["base"], steps["n"] = base + i * per, 0
                    run(i)
                    assert steps["n"] == per, steps["n"]
                steps["base"], steps["n"] = base + count * per, 0

            def lo_of(dst, full, hi, n, scale=None):
                dve.wait_ge(act_out, n + 1)
                if scale is None:
                    ins = nc.vector.tensor_tensor(dst, full, hi.bitcast(F32), ALU.subtract)
                else:
                    ins = nc.vector.scalar_tensor_tensor(dst, full, scale, hi.bitcast(F32), ALU.mult, ALU.subtract)
                ins.then_inc(operand_ready, 1)

            def rsqrt():
                step(nc.vector.tensor_scalar(nt[:].bitcast(I32), var[:].bitcast(I32), 1, None, ALU.arith_shift_right))
                settle()
                step(nc.vector.tensor_scalar(rs[:].bitcast(I32), nt[:].bitcast(I32), -1.0, float(0x5F3759DF),
                                             ALU.mult, ALU.add))
                settle()
                for _ in range(4):
                    step(nc.vector.scalar_tensor_tensor(nt[:], rs[:], -0.5, var[:], ALU.mult, ALU.mult))
                    settle()
                    step(nc.vector.tensor_tensor(nt[:], nt[:], rs[:], ALU.mult))
                    settle()
                    step(nc.vector.scalar_tensor_tensor(rs[:], nt[:], 1.5, rs[:], ALU.add, ALU.mult))
                    settle()

            def statistics(src, eps, rms):
                dve.sem_inc(dve_passed, 1)
                for t in range(T):
                    step(nc.vector.bn_stats(bst[:, t, :], src(t)))
                settle()
                dve.sem_inc(dve_passed, 1)
                for t in range(T):
                    step(nc.vector.bn_aggr(mv[:, t, :], bst[:, t, :]))
                settle()
                if rms:
                    step(nc.vector.tensor_tensor(nt[:], mv[:, :, 0], mv[:, :, 0], ALU.mult))
                    settle()
                    step(nc.vector.scalar_tensor_tensor(var[:], nt[:], eps, mv[:, :, 1], ALU.add, ALU.add))
                else:
                    step(nc.vector.tensor_scalar(var[:], mv[:, :, 1], eps, None, ALU.add))
                settle()
                rsqrt()

            NORM_LN, NORM_RMS = T + T + 1 + 2 + 12, T + T + 2 + 2 + 12

            def tile_of(b, t):
                return x[:, bass.ds(b * T + t, 1), :].rearrange("p o d -> p (o d)")

            def norm(b):
                statistics(lambda t: tile_of(b, t), 1e-5, False)
                for t in range(T):
                    if t == T - 1:
                        settle()
                    ins = nc.vector.tensor_scalar(xn[:, t, :], tile_of(b, t), mv[:, t, 0:1], rs[:, t:t + 1],
                                                  ALU.subtract, ALU.mult)
                    if t < T - 1:
                        step(ins)
                    else:
                        ins.then_inc(xn_ready, 1)

            NORM = NORM_LN + T - 1

            def split_T(n):
                for k in range(KT):
                    dve.wait_ge(act_out, n + k + 1)
                    step(nc.vector.tensor_copy(xT[0][:, k, :], xn[:, k, :]))
                    settle()
                    nc.vector.tensor_tensor(xT[1][:, k, :], xn[:, k, :], xT[0][:, k, :].bitcast(F32),
                                            ALU.subtract).then_inc(operand_ready, 1)

            def residual(b, gate, parts):
                dve.wait_ge(y_done, parts)
                for t in range(T):
                    nc.vector.scalar_tensor_tensor(tile_of(b, t), y_psum[:, t, :], gates[:, gate:gate + 1],
                                                   tile_of(b, t), ALU.mult, ALU.add).then_inc(x_done, 1)

            def phase_K0():
                n = 0
                for b in range(B):
                    lo_of(mpM[1][:, b, :], ring[0:M, n % 4, :], mpM[0][:, b, :], n)
                    n += 1
                for d in range(KT):
                    lo_of(mpT[1][:, d, :], ring[:, n % 4, 0:B * M], mpT[0][:, d, :], n)
                    n += 1
                bh, bl = [p_[:].rearrange("p b (q c) -> p b q c", q=PAIRS) for p_ in bd]
                for r, l in enumerate("12"):
                    if r:
                        dve.wait_ge(bd_stored, 32 * 2 * r)
                    for pair in range(PAIRS):
                        src = ring[:, n % 4, 0:B * M].rearrange("p (b m) -> p b m", b=B)
                        dve.wait_ge(act_out, n + 1)
                        nc.vector.tensor_tensor(bl[0:64, :, pair, 0:64], src[0:64],
                                                bh[0:64, :, pair, 0:64].bitcast(F32), ALU.subtract)
                        nc.vector.tensor_tensor(bl[64:128, :, pair, 64:128], src[64:128],
                                                bh[64:128, :, pair, 64:128].bitcast(F32),
                                                ALU.subtract).then_inc(operand_ready, 1)
                        n += 1
                    dve.wait_ge(bd_stored, 32 * (2 * r + 1))
                    for h in range(2):
                        for b in range(B):
                            src = ring[:, n % 4, :].rearrange("p (q u c) -> p q u c", q=4, u=2)
                            q = slice(4 * h, 4 * h + 4)
                            dve.wait_ge(act_out, n + 1)
                            nc.vector.tensor_tensor(bl[0:64, b, q, 0:64], src[0:64, :, 0, :],
                                                    bh[0:64, b, q, 0:64].bitcast(F32), ALU.subtract)
                            nc.vector.tensor_tensor(bl[64:128, b, q, 64:128], src[64:128, :, 1, :],
                                                    bh[64:128, b, q, 64:128].bitcast(F32),
                                                    ALU.subtract).then_inc(operand_ready, 1)
                            n += 1
                dve.wait_ge(bd_stored, 32 * 4)

                def masked(dst, src, mask, last):
                    step(nc.vector.tensor_tensor(bdf[:].rearrange("p (q c) -> p q c", q=mask.shape[1]), src, mask,
                                                 ALU.mult))
                    settle()
                    step(nc.vector.tensor_copy(dst[0], bdf[:]))
                    settle()
                    ins = nc.vector.tensor_tensor(dst[1], bdf[:], dst[0].bitcast(F32), ALU.subtract)
                    if last:
                        ins.then_inc(operand_ready, 1)
                        dve.wait_ge(operand_ready, n + 1)
                    else:
                        step(ins)
                        settle()

                for f in range(2):
                    dve.wait_ge(psum_full, n + 1)
                    for b in range(B):
                        src = ring[:, n % 4, b * M:(b + 1) * M].unsqueeze(1).to_broadcast([P, 8, M])
                        masked([p_[:, b, f * 512:(f + 1) * 512] for p_ in bd], src, mask_k[:], b == B - 1)
                    n += 1
                dve.wait_ge(bd_stored, 32 * 5)
                for b in range(B):
                    dve.wait_ge(psum_full, n + 1)
                    for f in range(2):
                        src = ring[:, n % 4, f * P:(f + 1) * P].unsqueeze(1).to_broadcast([P, 4, P])
                        masked([p_[:, b, f * 512:(f + 1) * 512] for p_ in bd], src, mask_v[:], f == 1)
                    n += 1

            def phase_G():
                dve.wait_ge(x_loaded, 16 * B)
                dve.wait_ge(consts_loaded, CONSTS + 32)

                def body(b):
                    n = seq0["G"] + b * 16
                    m = seq0["G"] % 4
                    u = s0["G"] + b * 2
                    nc.vector.tensor_copy(xn[:], x[:, bass.ds(b * T, T), :]).then_inc(xn_ready, 1)
                    for k in range(KT):
                        lo_of(xT[1][:, k, :], ring[:, (m + k) % 4, :], xT[0][:, k, :], n + k)

                    def finish(s):
                        i = slice(2 * s, 2 * s + 2)
                        dve.wait_ge(act_out, n + 4 + s + 1)
                        step(nc.vector.tensor_reduce(sm[:, 0, i], gP[:, i, :], AX, ALU.add))
                        settle()
                        step(nc.vector.reciprocal(sm[:, 1, i], sm[:, 0, i]))
                        settle()
                        nc.vector.tensor_tensor(gP[:, i, :], gP[:, i, :],
                                                sm[:, 1, i].unsqueeze(2).to_broadcast([P, 2, M]),
                                                ALU.mult).then_inc(operand_ready, 1)

                    for s in range(2):
                        i = slice(2 * s, 2 * s + 2)
                        dve.wait_ge(psum_full, n + 4 + s + 1)
                        step(nc.vector.tensor_scalar(gs[:, i, :],
                                                     ring[:, (m + 4 + s) % 4, 0:2 * M].rearrange("p (t m) -> p t m", t=2),
                                                     float(D) ** -0.5, None, ALU.mult))
                        settle()
                        step(nc.vector.tensor_reduce(mx[:, 0, i], gs[:, i, :], AX, ALU.max))
                        settle()
                        nc.vector.tensor_tensor(gs[:, i, :], gs[:, i, :],
                                                mx[:, 0, i].unsqueeze(2).to_broadcast([P, 2, M]),
                                                ALU.subtract).then_inc(scores_shifted, 1)
                    finish(0)
                    finish(1)
                    for s in range(2):
                        i = slice(s * 256, (s + 1) * 256)
                        lo_of(gPT[1][:, i], ring[0:M, (m + 6 + s) % 4, 0:256], gPT[0][:, i], n + 6 + s)
                    for t in range(T):
                        dve.wait_ge(act_out, n + 8 + t + 1)
                        dve.wait_ge(operand_ready, n + 8 + t)
                        dve.sem_inc(operand_ready, 1)
                    for k in range(KT):
                        lo_of(cT[1][:, k, :], ring[:, (m + 12 + k) % 4, :], cT[0][:, k, :], n + 12 + k)
                    dve.wait_ge(y_done, b + 1)

                    def gated(t):
                        dve.wait_ge(gate_out, b * T + t + 1)
                        step(nc.vector.tensor_tensor(gz[:, t % 2, :], gz[:, t % 2, :], ctxf[:, t, :], ALU.mult))
                        settle()
                        step(nc.vector.tensor_tensor(tile_of(b, t), tile_of(b, t), gz[:, t % 2, :], ALU.add))
                        settle()

                    for t in range(T):
                        nc.vector.tensor_tensor(gz[:, t % 2, :], y_psum[:, t, :], gbias[:], ALU.add).then_inc(gate_in, 1)
                        if t:
                            gated(t - 1)
                    gated(T - 1)
                    statistics(lambda t: tile_of(b, t), 1e-6, True)
                    for t in range(T):
                        nc.vector.scalar_tensor_tensor(tile_of(b, t), tile_of(b, t), rs[:, t:t + 1], gnorm[:],
                                                       ALU.mult, ALU.mult).then_inc(x_done, 1)

                loop(B, 4 + 4 + 2 * T + NORM_RMS, body)

            def phase_A(l):
                ph = "A" + l
                gate = GATES.index(f"L{l}_xattn_attn_gate")
                start = seq0[ph]

                def Q(n, m):
                    for p in range(4):
                        lo_of(qT[1][:, p, :], ring[:, (m + p) % 4, :], qT[0][:, p, :], n + p, 0.125)

                def S(b, n, m):
                    def finish(t):
                        dve.wait_ge(act_out, n + t + 1)
                        pv = pr[:, t, :].rearrange("p (h k) -> p h k", k=M)
                        step(nc.vector.tensor_reduce(sm[:, t, :], pv, AX, ALU.add))
                        settle()
                        step(nc.vector.reciprocal(sm[:, t, :], sm[:, t, :]))
                        settle()
                        nc.vector.tensor_tensor(pv, pv, sm[:, t, :].unsqueeze(2).to_broadcast([P, 8, M]),
                                                ALU.mult).then_inc(operand_ready, 1)

                    for t in range(T):
                        sv = sc[:, t % 2, :].rearrange("p (h k) -> p h k", k=M)
                        dve.wait_ge(psum_full, n + t + 1)
                        nc.vector.tensor_tensor(sv, ring[:, (m + t) % 4, :].rearrange("p (h k) -> p h k", k=M),
                                                kbias[:, bass.ds(b, 1), :].to_broadcast([P, 8, M]),
                                                ALU.add).then_inc(scores_copied, 1)
                        dve.wait_ge(scores_copied, body.scores + t + 1)
                        step(nc.vector.tensor_reduce(mx[:, t, :], sv, AX, ALU.max))
                        settle()
                        nc.vector.tensor_tensor(sv, sv, mx[:, t, :].unsqueeze(2).to_broadcast([P, 8, M]),
                                                ALU.subtract).then_inc(scores_shifted, 1)
                        if t:
                            finish(t - 1)
                    finish(T - 1)

                def TO(n, m):
                    for i, (kind, p) in enumerate(TO_ORDER):
                        dst = [p_[:, p % 2, :] for p_ in pT] if kind == "T" else [p_[:, p, :] for p_ in oT]
                        lo_of(dst[1], ring[:, (m + i) % 4, :], dst[0], n + i)

                def body(b, n, m, last, prefetch):
                    at, _ = a_layout(last)
                    body.scores = copied0[ph] + b * 8
                    S(b, n + at["S0"], m + at["S0"])
                    Q(n + at["Q1"], m + at["Q1"])
                    TO(n + at["TO0"], m + at["TO0"])
                    if not last:
                        split_T(n + at["TR"])
                    body.scores = copied0[ph] + b * 8 + 4
                    S(b, n + at["S1"], m + at["S1"])
                    if not last:
                        Q(n + at["Q2"], m + at["Q2"])
                    TO(n + at["TO1"], m + at["TO1"])
                    if prefetch:
                        norm(b + 2)
                    residual(b, gate, y0[ph] + b * 8 + 8)

                dve.wait_ge(x_done, xd0[ph])
                norm(0)
                split_T(start)
                Q(start + 4, start + 4)
                norm(1)
                per = 2 * 3 * T + KT + NORM
                loop(B - 2, per, lambda b: body(b, start + 8 + b * 36, start + 8, False, True))
                body(B - 2, start + 8 + (B - 2) * 36, start + 8, False, False)
                body(B - 1, start + 8 + (B - 1) * 36, start + 8, True, False)

            def phase_F(l):
                ph = "F" + l
                gate = GATES.index(f"L{l}_xattn_ff_gate")
                start = seq0[ph]

                def body(b, n, last):
                    for j in range(FF):
                        dve.wait_ge(act_out, n + j + 1)
                        if j:
                            dve.wait_ge(y_done, y0[ph] + b * FF + j)
                        step(nc.vector.tensor_copy(hT[0][:], hf[:]))
                        settle()
                        nc.vector.tensor_tensor(hT[1][:], hf[:], hT[0][:].bitcast(F32),
                                                ALU.subtract).then_inc(operand_ready, 1)
                        if j == FF // 2 and not last:
                            norm(b + 1)
                    if not last:
                        split_T(n + FF)
                    residual(b, gate, y0[ph] + b * FF + FF)

                dve.wait_ge(x_done, xd0[ph])
                norm(0)
                split_T(start)
                loop(B - 1, FF + NORM + KT, lambda b: body(b, start + 4 + b * 20, False))
                body(B - 1, start + 4 + (B - 1) * 20, True)

            def norm_rms(b, experts=None):
                statistics(lambda t: tile_of(b, t), 1e-6, True)
                if experts is not None:
                    step(nc.vector.tensor_tensor(wrs[:], vis[:, :, bass.ds(b * T, T)],
                                                 rs[:].unsqueeze(1).to_broadcast([P, 2, T]), ALU.mult))
                    settle()
                todo = [("lv".index(e), xnv if (e, len(experts)) == ("v", 2) else xn) for e in experts or ()] or [(None, xn)]
                todo = [(e, dst, t) for e, dst in todo for t in range(T)]
                for i, (e, dst, t) in enumerate(todo):
                    if i == len(todo) - 1:
                        settle()
                    ins = nc.vector.tensor_scalar(dst[:, t, :], tile_of(b, t),
                                                  rs[:, t:t + 1] if e is None else wrs[:, e, t:t + 1], None, ALU.mult)
                    if i < len(todo) - 1:
                        step(ins)
                    else:
                        ins.then_inc(xn_ready, 1)

            NORM3 = NORM_RMS + T - 1

            def norm_lo(dst, n, m, g, spare=0):
                for k in range(KT):
                    dve.wait_ge(act_out, n + k + 1)
                    nc.vector.scalar_tensor_tensor(dst[1][:, k, :], ring[:, (m + k) % 4, :], par[:, g, k:k + 1],
                                                   dst[0][:, k, :].bitcast(F32), ALU.mult,
                                                   ALU.subtract).then_inc(operand_ready, 1 + (spare if k == KT - 1 else 0))

            def phase_Q3():
                start = seq0["Q3"]
                g = PARAMS.index("L3_xattn_ln_in_w")
                half = HD3 // 2

                def rotate(n, m, t, c):
                    src = ring[:, m % 4, :].rearrange("p (h d) -> p h d", d=HD3)
                    r = r3[:, t % 2, c, :].rearrange("p (h d) -> p h d", d=HD3)
                    tmp = tmp3[:].rearrange("p (h d) -> p h d", d=HD3)

                    def table(lo, n_):
                        return rope[:, t:t + 1, lo:lo + n_].to_broadcast([P, HEADS3, n_])

                    dve.wait_ge(psum_full, n + 1)
                    dve.wait_ge(operand_ready, n)
                    dve.sem_inc(dve_passed, 1)
                    step(nc.vector.tensor_tensor(r, src, table(0, HD3), ALU.mult))
                    step(nc.vector.tensor_tensor(tmp[:, :, 0:half], src[:, :, half:], table(HD3, half), ALU.mult))
                    step(nc.vector.tensor_tensor(tmp[:, :, half:], src[:, :, 0:half], table(HD3 + half, half), ALU.mult))
                    settle()
                    nc.vector.tensor_tensor(r, r, tmp, ALU.add).then_inc(operand_ready, 1)

                def body(b, n, m, last):
                    for kind, t, k0 in q3_order(last):
                        if kind == "P":
                            for c in range(2):
                                rotate(n + k0 + c, m + k0 + c, t, c)
                            lo_of(v_out[1][:], ring[:, (m + k0 + 2) % 4, :], v_out[0][:], n + k0 + 2)
                        elif kind == "X":
                            for c in range(2):
                                lo_of(qk_out[1][:, c, :], ring[:, (m + k0 + c) % 4, :], qk_out[0][:, c, :], n + k0 + c)
                            if t == 1 and not last:
                                norm_rms(b + 1, "lv")
                        else:
                            norm_lo(xT if kind == "TRl" else xTv, n + k0, m + k0, g)

                dve.wait_ge(x_done, xd0["Q3"])
                dve.wait_ge(rope_loaded, 16 * T)
                norm_rms(0, "lv")
                norm_lo(xT, start, start, g)
                norm_lo(xTv, start + 4, start + 4, g)
                loop(B - 1, 2 * T * 3 + NORM_RMS + 1 + 2 * T - 1, lambda b: body(b, start + 8 + b * 28, start + 8, False))
                body(B - 1, start + 8 + (B - 1) * 28, start + 8, True)

            def phase_A3():
                H = HEADS3 * T
                scale = float(HD3) ** -0.5

                def body(b):
                    h0, u0 = b * H, b * (H // 4)
                    dve.wait_ge(x_done, xd0["A3"] + b * T)
                    step(nc.vector.tensor_copy(wrs[:], vis[:, :, bass.ds(b * T, T)]))

                    def maximum(h):
                        t = h // 4 % 4
                        dve.wait_ge(sc3_full, h0 + h + 1)
                        diagonal = ring[:, h % 4, t * P:(t + 1) * P]
                        step(nc.vector.tensor_tensor(diagonal, diagonal, causal[:], ALU.add))
                        settle()
                        step(nc.vector.tensor_reduce(nm3[:, 0, h:h + 1], ring[:, h % 4, 0:(t + 1) * P], AX, ALU.max))
                        settle()
                        nc.vector.tensor_scalar(nm3[:, 1, h:h + 1], nm3[:, 0, h:h + 1], -scale, None,
                                                ALU.mult).then_inc(sc3_max, 1)

                    maximum(0)
                    maximum(1)
                    for h in range(H + 5):
                        if h + 2 < H:
                            maximum(h + 2)
                        if h >= 8 and h % 4 == 0:
                            u = (h - 8) // 4
                            g, t = u // 4, u % 4
                            at = slice(t * P, (t + 1) * P)
                            dve.wait_ge(ox3_hi, u0 + u + 1)
                            nc.vector.tensor_tensor(oT3[1][:, g, at], y_psum[:, 2 + u % 2, P:2 * P],
                                                    oT3[0][:, g, at].bitcast(F32), ALU.subtract).then_inc(ox3_ready, 1)
                        if h < H:
                            n = (h // 4 % 4 + 1) * P
                            dve.wait_ge(pt3_hi, h0 + h + 1)
                            nc.vector.tensor_tensor(pT3[1][:, h % 2, 0:n], y_psum[:, h % 2, 0:n],
                                                    pT3[0][:, h % 2, 0:n].bitcast(F32), ALU.subtract).then_inc(pt3_ready, 1)
                        if h >= 5 and h % 4 == 1 and h < H + 2:
                            u = (h - 5) // 4
                            dve.wait_ge(pv3_done, h0 + 4 * u + 4)
                            dve.sem_inc(dve_passed, 1)
                            step(nc.vector.reciprocal(sm[:, u % 2, 0:4], sum3[:, 4 * u:4 * u + 4]))
                            settle()
                            nc.vector.tensor_tensor(o3[:, u % 2, :].rearrange("p (r d) -> p r d", r=4),
                                                    y_psum[:, 2 + u % 2, 0:P].rearrange("p (r d) -> p r d", r=4),
                                                    sm[:, u % 2, 0:4].unsqueeze(2).to_broadcast([P, 4, HD3]),
                                                    ALU.mult).then_inc(o3_ready, 1)
                    for t in range(T):
                        for e, done in ((0, dense_added), (1, x_done)):
                            dve.wait_ge(dense_full, b * 2 * T + 2 * t + e + 1)
                            if e:
                                dve.wait_ge(dense_added, b * T + t + 1)
                            nc.vector.scalar_tensor_tensor(tile_of(b, t), ring[:, (2 * t + e) % 4, :], wrs[:, e, t:t + 1],
                                                           tile_of(b, t), ALU.mult, ALU.add).then_inc(done, 1)

                dve.wait_ge(consts_loaded, CONSTS + 48)
                dve.sem_inc(o3_ready, 1)
                loop(B, 1 + 2 * H + H // 4, body)

            def phase_C3():
                start = seq0["C3"]
                g = PARAMS.index("L3_xattn_ln_post_cross_w")

                def Q(n, m):
                    for f in range(2):
                        lo_of(cqT[1][:, f, :], ring[:, (m + f) % 4, :], cqT[0][:, f, :], n + f)

                def body(b, n, m, last, prefetch):
                    def finish(i):
                        pv = cpr[:, i, :].rearrange("p (h k) -> p h k", k=M)
                        total = sm[:, i % T, :]
                        dve.wait_ge(act_out, n + i + 1)
                        step(nc.vector.tensor_reduce(total, pv, AX, ALU.add))
                        settle()
                        step(nc.vector.reciprocal(total, total))
                        settle()
                        nc.vector.tensor_tensor(pv, pv, total.unsqueeze(2).to_broadcast([P, 8, M]),
                                                ALU.mult).then_inc(operand_ready, 1)

                    for i in range(2 * T):
                        scores = ring[:, (m + i) % 4, :].rearrange("p (h k) -> p h k", k=M)
                        top = mx[:, i % T, :]
                        dve.wait_ge(psum_full, n + i + 1)
                        step(nc.vector.tensor_reduce(top, scores, AX, ALU.max))
                        settle()
                        nc.vector.tensor_tensor(csc[:, i % 2, :].rearrange("p (h k) -> p h k", k=M), scores,
                                                top.unsqueeze(2).to_broadcast([P, 8, M]),
                                                ALU.subtract).then_inc(scores_copied, 1)
                        if i:
                            finish(i - 1)
                    finish(2 * T - 1)
                    k0 = 8
                    if not last:
                        norm_lo(xT, n + k0, m + k0, g)
                        k0 += 4
                    for f in range(2):
                        for p in range(5):
                            hi, lo = [p_[:, p % 2, :] for p_ in cpT] if p < 4 else [p_[:, f, :] for p_ in coT]
                            lo_of(lo, ring[:, (m + k0) % 4, :], hi, n + k0)
                            k0 += 1
                    if not last:
                        Q(n + k0, m + k0)
                    if prefetch:
                        norm_rms(b + 2)
                    dve.wait_ge(y_done, y0["C3"] + b + 1)
                    for t in range(T):
                        nc.vector.tensor_tensor(tile_of(b, t), y_psum[:, t, :], tile_of(b, t), ALU.add).then_inc(x_done, 1)

                dve.wait_ge(x_done, xd0["C3"])
                norm_rms(0)
                norm_lo(xT, start, start, g)
                Q(start + 4, start + 4)
                norm_rms(1)
                loop(B - 2, 3 * 2 * T + NORM3, lambda b: body(b, start + 6 + b * 24, start + 6, False, True))
                body(B - 2, start + 6 + (B - 2) * 24, start + 6, False, False)
                body(B - 1, start + 6 + (B - 1) * 24, start + 6, True, False)

            def phase_M(e):
                ph = "M" + e
                start = seq0[ph]
                g = PARAMS.index("L3_xattn_ln_post_attn_w")

                def body(b, n, m, last):
                    for j in range(HT):
                        dve.wait_ge(psum_full, n + 2 * j + 2)
                        dve.wait_ge(act_out, n + 2 * j + 1)
                        dve.wait_ge(operand_ready, n + 2 * j)
                        dve.sem_inc(dve_passed, 1)
                        nc.vector.tensor_tensor(mf[:], sg[:], ring[:, (m + 2 * j + 1) % 4, :],
                                                ALU.mult).then_inc(operand_ready, 1)
                        dve.wait_ge(operand_ready, n + 2 * j + 1)
                        lo_of(mT[1][:], mf[:], mT[0][:], n + 2 * j + 1)
                        if j == HT // 2 and not last:
                            norm_rms(b + 1, e)
                    if not last:
                        norm_lo(xT, n + 2 * HT, m + 2 * HT, g, 2)
                    dve.wait_ge(y_done, y0[ph] + b * HT + HT)
                    for t in range(T):
                        nc.vector.tensor_tensor(tile_of(b, t), y_psum[:, t, :], tile_of(b, t), ALU.add).then_inc(x_done, 1)

                dve.wait_ge(x_done, xd0[ph])
                norm_rms(0, e)
                norm_lo(xT, start, start, g, 2)
                loop(B - 1, NORM_RMS + 1 + T - 1, lambda b: body(b, start + 6 + b * 28, start + 6, False))
                body(B - 1, start + 6 + (B - 1) * 28, start + 6, True)

            dve.sem_inc(x_done, 1)
            step(nc.vector.memset(bd[0][:].bitcast(F32), 0.0))
            settle()
            nc.vector.memset(bd[1][:].bitcast(F32), 0.0).then_inc(zeroed, 1)
            dve.wait_ge(zeroed, 1)
            dve.wait_ge(consts_loaded, CONSTS)
            step(nc.vector.tensor_copy(kbias[:], mask8[:].bitcast(U8)))
            settle()
            step(nc.vector.tensor_scalar(kbias[:], kbias[:], -1.0, FLT_MAX, ALU.add, ALU.mult))
            settle()
            step(nc.vector.tensor_scalar(vis[:], types[:], 1, None, ALU.is_equal))
            settle()
            step(nc.vector.tensor_tensor(vis[:, 1, :], vis[:, 0, :], vis[:, 1, :], ALU.mult))
            settle()
            step(nc.vector.tensor_scalar(vis[:, 0, :], vis[:, 1, :], -1.0, 1.0, ALU.mult, ALU.add))
            settle()
            dve.wait_ge(tanh_done, 1)
            for ph in phases:
                if ph in ("A1", "A2"):
                    phase_A(ph[1])
                elif ph[0] in "FM":
                    (phase_F if ph[0] == "F" else phase_M)(ph[1])
                else:
                    {"K0": phase_K0, "G": phase_G, "Q3": phase_Q3, "A3": phase_A3, "C3": phase_C3}[ph]()


CONSTS = 8 * 16
PHASES = ["K0", "G", "A1", "F1", "A2", "F2", "Q3", "A3", "C3", "Ml", "Mv"]


def layouts(inputs):
    f = np.ascontiguousarray
    a = {k: np.asarray(v) for k, v in inputs.items()}
    p = {"x": f(a["x"].reshape(B * SEQ, D))}
    ctxT = a["ctx_1024"].transpose(2, 0, 1)
    w = {}
    for k in range(2):
        c = ctxT[k * P:(k + 1) * P]
        w["ctx", k] = np.stack([c, c], 2).reshape(P, 512)
        w["wmem", k] = a["L0_xattn_W_mem"].T[k * P:(k + 1) * P]
        w["ckv", k] = a["L3_xattn_ckv_w"][k * P:(k + 1) * P]
    for k in range(8):
        w["wg", k] = a["L0_xattn_W_gate"].T[k * P:(k + 1) * P]
    for l in "12":
        wkv, wq, wo = (a[f"L{l}_xattn_{n}"] for n in ("Wkv", "Wq", "Wo"))
        w1, w2 = a[f"L{l}_xattn_W1"], a[f"L{l}_xattn_W2"]
        for i in range(8):
            c, k = i // 2, i % 2
            w[f"wkv{l}", i] = wkv[k * P:(k + 1) * P, c * 512:(c + 1) * 512]
            w[f"wq{l}", i] = wq[:, i * P:(i + 1) * P].reshape(KT, P, P).transpose(1, 0, 2).reshape(P, 512)
            w[f"wo{l}", i] = wo[i * P:(i + 1) * P]
        for j in range(FF):
            w[f"w1_{l}", j] = w1[:, j * P:(j + 1) * P].reshape(KT, P, P).transpose(1, 0, 2).reshape(P, 512)
            w[f"w2_{l}", j] = w2[j * P:(j + 1) * P]
    for e in "lv":
        qkv, dense, gate, up, down = (a[f"L3_xattn_{e}_{n}"] for n in ("qkv", "dense", "gate", "up", "down"))
        gate, up = (np.pad(t, ((0, 0), (0, HT * P - HID))) for t in (gate, up))
        down = np.pad(down, ((0, HT * P - HID), (0, 0)))
        for k in range(KT):
            w[f"dense_{e}", k] = dense[k * P:(k + 1) * P]
            for c in range(3):
                w[f"qkv_{e}", 4 * c + k] = qkv[k * P:(k + 1) * P, c * 512:(c + 1) * 512]
        for j in range(HT):
            for name, t in (("gate", gate), ("up", up)):
                w[f"{name}_{e}", j] = t[:, j * P:(j + 1) * P].reshape(KT, P, P).transpose(1, 0, 2).reshape(P, 512)
            w[f"down_{e}", j] = down[j * P:(j + 1) * P]
    for i in range(2):
        w["cq", i] = a["L3_xattn_cq_w"][2 * i * P:2 * (i + 1) * P].reshape(2, P, MD).transpose(1, 0, 2).reshape(P, 512)
        w["cdense", i] = a["L3_xattn_cdense_w"][i * P:(i + 1) * P]
    names = [n for ph in PHASES for n in piece_names()[ph]]
    p["weights"] = f(np.stack([w[n] for n in names]))
    p["params"] = f(np.stack([a[n].reshape(KT, P).T for n in PARAMS], 1))
    p["gates"] = f(np.broadcast_to(np.concatenate([a[n] for n in GATES])[None], (P, len(GATES))))
    p["mask_s2"] = f(np.broadcast_to(a["mask_BxS2_bk0"][None], (P, B, M))).view(np.int32)
    p["b_gate"] = f(np.broadcast_to(a["L0_xattn_b_gate"][None], (P, D)))
    p["norm_w"] = f(np.broadcast_to(a["L0_xattn_norm_w"][None], (P, D)))
    tt = a["mask_BxS_ik0"]
    tt = np.stack([tt, np.pad(tt[:, 1:], ((0, 0), (0, 1)))])
    p["types"] = f(tt.reshape(2, B * T, P).transpose(2, 0, 1))
    p["pos"] = f(a["pos_1xS"].reshape(T, P).T)
    inv = (np.float32(1) / np.power(np.float32(10000), np.arange(0, HD3, 2, dtype=np.float32) / np.float32(HD3)))
    angle = np.outer(np.arange(SEQ, dtype=np.float32), inv)
    p["rope_table"] = np.concatenate([np.cos(angle), np.cos(angle), -np.sin(angle), np.sin(angle)], 1).astype(np.float32)
    p["causal"] = np.where(np.arange(P)[None, :] <= np.arange(P)[:, None], 0, -FLT_MAX).astype(np.float32)
    p["ident"] = np.eye(P, dtype=np.float32)
    row, h = np.arange(P)[:, None, None], np.arange(8)[None, :, None]
    p["mask_k"] = f(np.broadcast_to(row // 16 == h, (P, 8, M)).astype(np.float32))
    j, c = np.arange(4)[None, :, None], np.arange(P)[None, None, :]
    p["mask_v"] = f((c // 16 == 2 * j + row // 64).astype(np.float32))
    return p, names


def kernel(**inputs):
    import concourse.bacc as _bacc
    from concourse.bass_utils import run_bass_kernel_spmd as _run

    nc = _bacc.Bacc("TRN2", target_bir_lowering=False, num_devices=1)
    arrays, names = layouts(inputs)
    t_in = {n: nc.dram_tensor("in_" + n, v.shape, mybir.dt.from_np(v.dtype), kind="ExternalInput").ap() for n, v in arrays.items()}
    packed = t_in["weights"]
    t_in["weights"] = {n: packed[i] for i, n in enumerate(names)}
    t_in["kv_scratch"] = [[[nc.dram_tensor(f"kv_{l}_{kv}_{part}", (B * P, 1024), F32).ap() for part in ("hi", "lo")]
                           for kv in "kv"] for l in "12c"]
    t_in["qkv_scratch"] = [[nc.dram_tensor(f"scratch_{n}3_{part}", (B * SEQ, D), F32).ap() for part in ("hi", "lo")] for n in "qkv"]
    out = nc.dram_tensor("out_0", (B * SEQ, D), F32, kind="ExternalOutput").ap()
    build(nc, t_in, out, PHASES)
    r = _run(nc, [{"in_" + n: v for n, v in arrays.items()}], core_ids=[0])
    return r.results[0]["out_0"].reshape(B, SEQ, D)
```

```python
from contextlib import ExitStack

import numpy as np

import concourse.bass as bass
from concourse import mybir

F32 = mybir.dt.float32
F32R = mybir.dt.float32r
I32 = mybir.dt.int32
U8 = mybir.dt.uint8
ALU = mybir.AluOpType
ACT = mybir.ActivationFunctionType
AX = mybir.AxisListType.X

P = 128
B = 4
SEQ = 512
T = SEQ // P
D = 512
KT = D // P
M = 64
MD = 256
PAIRS = 8
FF = 2048 // P
HID = 1376
HT = -(-HID // P)
HEADS3 = 16
HD3 = 32
H3 = HEADS3 * T
FLT_MAX = 3.4028234663852886e38
SLOTS = 34
SLOTS_A = 16
STAGES = 3
PARAMS = ["L1_xattn_ln_q_g", "L1_xattn_ln_q_b", "L1_xattn_ln_ff_g", "L1_xattn_ln_ff_b",
          "L2_xattn_ln_q_g", "L2_xattn_ln_q_b", "L2_xattn_ln_ff_g", "L2_xattn_ln_ff_b",
          "L3_xattn_ln_in_w", "L3_xattn_ln_post_cross_w", "L3_xattn_ln_post_attn_w"]
GATES = ["L1_xattn_attn_gate", "L1_xattn_ff_gate", "L2_xattn_attn_gate", "L2_xattn_ff_gate"]

Q3_BODY = [("P", 0), ("P", 1), ("X", 0), ("P", 2), ("X", 1), ("P", 3), ("X", 2), ("TRl", 0), ("TRv", 0), ("X", 3)]
Q3_SIZE = {"P": 3, "X": 2, "TRl": 4, "TRv": 4}
TO_ORDER = [("T", 0), ("T", 1), ("O", 0), ("T", 2), ("O", 1), ("T", 3), ("O", 2), ("O", 3)]


def piece_names():
    k0 = [("ctx", k) for k in range(2)] + [("wmem", k) for k in range(2)]
    for l in "12":
        k0 += [(f"wkv{l}", i) for i in range(8)]
    k0 += [("ckv", k) for k in range(2)]
    g = [("wg", k) for k in range(8)]
    a = {l: [(f"wq{l}", i) for i in range(8)] + [(f"wo{l}", i) for i in range(8)] for l in "12"}
    f = {l: [(f"{w}{l}", j) for j in range(FF) for w in ("w1_", "w2_")] for l in "12"}
    q3 = [(f"qkv_{e}", 4 * c + k) for c in range(3) for e in "lv" for k in range(KT)]
    a3 = [(f"dense_{e}", k) for e in "lv" for k in range(KT)]
    c3 = [("cq", k) for k in range(2)] + [("cdense", k) for k in range(2)]
    m = {e: [(f"{w}_{e}", j) for j in range(HT) for w in ("gate", "up", "down")] for e in "lv"}
    return {"K0": k0, "G": g, "A1": a["1"], "F1": f["1"], "A2": a["2"], "F2": f["2"],
            "Q3": q3, "A3": a3, "C3": c3, "Ml": m["l"], "Mv": m["v"]}


def build(nc, t_in, out, phases):
    with ExitStack() as ctx:
        def sb(name, shape, dt=F32, stack=ctx):
            return stack.enter_context(nc.sbuf_tensor(name, shape, dt))

        def sem(name):
            return ctx.enter_context(nc.semaphore(name))

        x = sb("x", [P, B * T, D])
        xn = sb("xn", [P, T, D])
        xT = [sb(f"xT_{n}", [P, KT, SEQ], F32R) for n in ("hi", "lo")]
        stage = sb("stage", [P, STAGES, 512])
        wa = [sb(f"wa_{n}", [P, SLOTS_A, 512], F32R) for n in ("hi", "lo")]
        ident = sb("ident", [P, P])
        par = sb("par", [P, len(PARAMS), KT])
        gates = sb("gates", [P, len(GATES)])
        kbias = sb("kbias", [P, B, M])
        mask8 = xn[:, 3, 384:384 + B * M // 4].bitcast(I32)
        types = xn[:, 3, 448:448 + 2 * B * T].bitcast(I32)
        vis = sb("vis", [P, 2, B * T])
        wrs = sb("wrs", [P, 2, T])
        v_plan = sb("v_plan", [P, 2 * B * T + 1], I32)
        v_valid = sb("v_valid", [P, B * T])
        v_mask = sb("v_mask", [P, T])
        pos = sb("pos", [P, T], I32)
        rope = sb("rope", [P, T, 2 * HD3])
        bst = sb("bst", [P, T, 6])
        mv = sb("mv", [P, T, 2])
        var = sb("var", [P, T])
        rs = sb("rs", [P, T])
        nt = sb("nt", [P, T])
        mx = sb("mx", [P, T, 8])
        sm = sb("sm", [P, T, 8])

        scopes = ExitStack()
        with scopes:
            wb = [sb(f"wb_{n}", [P, SLOTS - SLOTS_A, 512], F32R, scopes) for n in ("hi", "lo")]
            hf = sb("hf", [P, 512], stack=scopes)
            hT = [sb(f"hT_{n}", [P, 512], F32R, scopes) for n in ("hi", "lo")]
        scopes = ExitStack()
        with scopes:
            mpM = [sb(f"mp_{n}", [M, B, D], F32R, scopes) for n in ("hi", "lo")]
            mpT = [sb(f"mpT_{n}", [P, KT, B * M], F32R, scopes) for n in ("hi", "lo")]
            inner = ExitStack()
            with inner:
                bd = [sb(f"bd_{n}", [P, B, 1024], F32R, inner) for n in ("hi", "lo")]
                bdf = sb("bdf", [P, 512], stack=inner)
                mask_k = sb("mask_k", [P, 8, M], stack=inner)
                mask_v = sb("mask_v", [P, 4, P], stack=inner)
            cT = [sb(f"cT_{n}", [P, KT, SEQ], F32R, scopes) for n in ("hi", "lo")]
            ctxf = sb("ctxf", [P, T, D], stack=scopes)
            gPT = [sb(f"gPT_{n}", [M, SEQ], F32R, scopes) for n in ("hi", "lo")]
            gs = sb("gs", [P, T, M], stack=scopes)
            gP = sb("gP", [P, T, M], stack=scopes)
            gbias = sb("gbias", [P, D], stack=scopes)
            gnorm = sb("gnorm", [P, D], stack=scopes)
            gz = sb("gz", [P, 2, D], stack=scopes)
        scopes = ExitStack()
        with scopes:
            qT = [sb(f"qT_{n}", [P, 4, SEQ], F32R, scopes) for n in ("hi", "lo")]
            oT = [sb(f"oT_{n}", [P, 4, SEQ], F32R, scopes) for n in ("hi", "lo")]
            pT = [sb(f"pT_{n}", [P, 2, SEQ], F32R, scopes) for n in ("hi", "lo")]
            sc = sb("sc", [P, 2, 512], stack=scopes)
            pr = sb("pr", [P, T, 512], stack=scopes)
            kbd = [sb(f"kbd_{n}", [P, 1024], F32R, scopes) for n in ("hi", "lo")]
            vbd = [sb(f"vbd_{n}", [P, 1024], F32R, scopes) for n in ("hi", "lo")]

        scopes = ExitStack()
        with scopes:
            wb3 = [sb(f"wb3_{n}", [P, 8, 512], F32R, scopes) for n in ("hi", "lo")]
            xTv = [sb(f"xTv_{n}", [P, KT, SEQ], F32R, scopes) for n in ("hi", "lo")]
            xnv = sb("xnv", [P, T, D], stack=scopes)
            r3 = sb("r3", [P, 2, 2, 512], stack=scopes)
            tmp3 = sb("tmp3", [P, 512], stack=scopes)
            qk_out = [sb(f"qk_out_{n}", [P, 2, 512], F32R, scopes) for n in ("hi", "lo")]
            v_out = [sb(f"v_out_{n}", [P, 512], F32R, scopes) for n in ("hi", "lo")]
        scopes = ExitStack()
        with scopes:
            q3 = sb("q3", [P, 4, SEQ], F32R, scopes)
            k3 = sb("k3", [P, 4, SEQ], F32R, scopes)
            v3 = [sb(f"v3_{n}", [P, 2, T, P], F32R, scopes) for n in ("hi", "lo")]
            p3 = sb("p3", [P, 4, SEQ], stack=scopes)
            pT3 = [sb(f"pT3_{n}", [P, 2, T, SEQ], F32R, scopes) for n in ("hi", "lo")]
            causal = sb("causal", [P, P], stack=scopes)
            causal_r = sb("causal_r", [P, P], F32R, scopes)
            ident_r = sb("ident_r", [P, P], F32R, scopes)
            nm3 = sb("nm3", [P, H3], stack=scopes)
            sum3 = sb("sum3", [P, H3], stack=scopes)
            rec3 = sb("rec3", [P, H3], stack=scopes)
        scopes = ExitStack()
        with scopes:
            cqT = [sb(f"cqT_{n}", [P, 2, SEQ], F32R, scopes) for n in ("hi", "lo")]
            coT = [sb(f"coT_{n}", [P, 2, SEQ], F32R, scopes) for n in ("hi", "lo")]
            cpT = [sb(f"cpT_{n}", [P, 2, SEQ], F32R, scopes) for n in ("hi", "lo")]
            csc = sb("csc", [P, 2, 512], stack=scopes)
            cpr = sb("cpr", [P, 2 * T, 512], stack=scopes)
            ckbd = [sb(f"ckbd_{n}", [P, 1024], F32R, scopes) for n in ("hi", "lo")]
            cvbd = [sb(f"cvbd_{n}", [P, 1024], F32R, scopes) for n in ("hi", "lo")]
        scopes = ExitStack()
        with scopes:
            wbm = [sb(f"wbm_{n}", [P, 3 * HT - SLOTS_A, 512], F32R, scopes) for n in ("hi", "lo")]
            sg = sb("sg", [P, 512], stack=scopes)
            mf = sb("mf", [P, 512], stack=scopes)
            mT = [sb(f"mT_{n}", [P, 512], F32R, scopes) for n in ("hi", "lo")]

        y_psum = ctx.enter_context(nc.psum_tensor("y_psum", [P, T, 512], F32))
        ring = ctx.enter_context(nc.psum_tensor("ring", [P, 4, 512], F32))

        psum_full, act_out, operand_ready = sem("psum_full"), sem("act_out"), sem("operand_ready")
        y_done, x_done = sem("y_done"), sem("x_done")
        scores_copied, scores_shifted = sem("scores_copied"), sem("scores_shifted")
        xn_ready, w_ready, w_hi = sem("xn_ready"), sem("w_ready"), sem("w_hi")
        staged = [sem(f"staged{i}") for i in range(STAGES)]
        consts_loaded, x_loaded, zeroed = sem("consts_loaded"), sem("x_loaded"), sem("zeroed")
        bd_stored, k_loaded, v_loaded = sem("bd_stored"), sem("k_loaded"), sem("v_loaded")
        counted, finished = sem("counted"), sem("finished")
        gate_in, gate_out, tanh_done = sem("gate_in"), sem("gate_out"), sem("tanh_done")
        dve_step, stored = sem("dve_step"), sem("stored")
        rope_loaded, q_stored, k_stored, v_stored = (sem(n) for n in ("rope_loaded", "q_stored", "k_stored", "v_stored"))
        sc3_full, sc3_max, p3_exp, rec3_ready, p3_ready, pt3_full, pt3_hi, pt3_ready = (
            sem(n) for n in ("sc3_full", "sc3_max", "p3_exp", "rec3_ready", "p3_ready", "pt3_full", "pt3_hi", "pt3_ready"))
        o3_full, o3_hi, o3_ready, dense_full, dense_added = (
            sem(n) for n in ("o3_full", "o3_hi", "o3_ready", "dense_full", "dense_added"))
        causal_ready = sem("causal_ready")
        qk3_loaded = [sem(f"qk3_loaded{i}") for i in range(4)]
        v3_loaded = [sem(f"v3_loaded{i}") for i in range(2)]
        pe_passed, act_passed, dve_passed, sp_passed = (
            sem(n) for n in ("pe_passed", "act_passed", "dve_passed", "sp_passed"))

        K0_KV = {"1": 8, "2": 24, "C": 40}
        N_K0, N_G, N_A, N_F = 46, 16 * B, 8 + 36 * 3 + 28, 4 + 20 * 3 + 16
        N_Q3, N_C, N_M = 8 + 28 * 3 + 20, 6 + 24 * 3 + 18, 6 + 28 * 3 + 22
        order = ["K0", "G", "A1", "F1", "A2", "F2", "Q3", "A3", "C3", "Ml", "Mv"]
        n_groups = {"K0": N_K0, "G": N_G, "A1": N_A, "A2": N_A, "F1": N_F, "F2": N_F, "Q3": N_Q3, "A3": 0, "C3": N_C,
                    "Ml": N_M, "Mv": N_M}
        n_y = {"K0": 0, "G": B, "A1": 8 * B, "A2": 8 * B, "F1": FF * B, "F2": FF * B, "Q3": 0, "A3": 0, "C3": B,
               "Ml": HT * B, "Mv": HT * B}
        n_s = {"G": 2 * B, "A1": 8 * B, "A2": 8 * B, "C3": 8 * B}
        n_xn = {"G": 4, "A1": 4, "A2": 4, "F1": 4, "F2": 4, "Q3": 4, "C3": 4, "Ml": 4, "Mv": 4}
        seq0, y0, s0, xn0, xd0 = {}, {}, {}, {}, {}
        a = b_ = c = d_ = 0
        e_ = 1
        for ph in order:
            seq0[ph], y0[ph], s0[ph], xn0[ph], xd0[ph] = a, b_, c, d_, e_
            a += n_groups[ph]
            b_ += n_y[ph]
            c += n_s.get(ph, 0)
            d_ += n_xn.get(ph, 0)
            e_ += 0 if ph in ("K0", "Q3") else B * T

        copied0 = {"A1": 0, "A2": 8 * B, "C3": 16 * B}

        def a_layout(last):
            at, n = {}, 0
            for name, k in (("S0", 4), ("Q1", 4), ("TO0", 8)) + (() if last else (("TR", 4),)) \
                    + (("S1", 4),) + (() if last else (("Q2", 4),)) + (("TO1", 8),):
                at[name] = n
                n += k
            return at, n

        names = piece_names()
        slots = {"K0": [0, 1, 2, 3] + list(range(4, 12)) + [12, 13, 14, 15, 4, 5, 6, 7] + [8, 9],
                 "G": [10, 11, 12, 13, 14, 15, 2, 3],
                 "A1": [0, 1, 4, 5, 6, 7, 8, 9, 10, 11, 12, 13, 14, 15, 2, 3],
                 "F1": list(range(32)), "A2": list(range(16)), "F2": list(range(32)),
                 "Q3": list(range(24)), "A3": list(range(8)), "C3": list(range(8, 12))}
        slots["Ml"] = slots["Mv"] = [12, 13, 14, 15] + list(range(12)) + list(range(16, 3 * HT))

        def last_use(ph, i):
            if ph == "K0":
                name, k = names["K0"][i]
                n = {"ctx": N_K0, "wmem": 8, "ckv": N_K0}.get(name)
                if n is None:
                    n = K0_KV[name[-1]] + (8 if k < 4 else 16)
                return psum_full, n
            if ph == "G":
                return y_done, y0[ph] + B
            if ph in ("A1", "A2"):
                tail = seq0[ph] + 8 + 3 * 36
                if i < 4:
                    return psum_full, tail
                if i < 8:
                    return psum_full, tail + a_layout(True)[0]["Q1"] + i - 4 + 1
                return y_done, y0[ph] + 8 * 3 + (i - 8) + 1
            if ph == "Q3":
                return psum_full, seq0[ph] + 8 + 28 * 3 + 13 + i // 8 + 1
            if ph in ("A3", "C3"):
                return x_done, xd0[ph] + B * T
            if ph[0] == "M":
                j = i // 3
                if i % 3 < 2:
                    return psum_full, seq0[ph] + 6 + 28 * 3 + 2 * j + 2
                return y_done, y0[ph] + HT * 3 + j + 1
            j = i // 2
            if i % 2 == 0:
                return psum_full, seq0[ph] + 4 + 60 + j + 1
            return y_done, y0[ph] + FF * 3 + j + 1

        pieces, index_of, owner, home = [], {}, {}, {}
        for ph in order:
            if ph not in phases:
                continue
            for i, name in enumerate(names[ph]):
                slot = slots[ph][i]
                free = [owner[slot]] if slot in owner else []
                if (ph[0] == "F" or ph in ("Q3", "Ml")) and slot >= SLOTS_A:
                    free = [(x_done, xd0[ph])]
                index_of[name] = len(pieces)
                pieces.append((name, slot, free))
                owner[slot] = last_use(ph, i)
                high = wb3 if ph == "Q3" else wbm if ph[0] == "M" else wb
                home[name] = [p_[:, slot - SLOTS_A, :] for p_ in high] if slot >= SLOTS_A \
                    else [p_[:, slot, :] for p_ in wa]

        def w(name):
            return home[name]

        def q3_order(last):
            steps_, n = [], 0
            for kind, t in Q3_BODY:
                if last and kind in ("TRl", "TRv"):
                    continue
                steps_.append((kind, t, n))
                n += Q3_SIZE[kind]
            return steps_

        ahead = index_of.get(("gate_l", 0), len(pieces)) + 4

        block = ctx.enter_context(nc.Block())

        @block.sync
        def _(sp):
            def load_pieces(first, end):
                for n, (name, slot, free) in list(enumerate(pieces))[first:end]:
                    if n >= STAGES:
                        sp.wait_ge(w_ready, n - STAGES + 1)
                    sp.dma_start(stage[:, n % STAGES, :], t_in["weights"][name]).then_inc(staged[n % STAGES], 16)

            def load_head(b, h):
                q_, k_, _ = t_in["qkv_scratch"]
                rows = bass.ds(b * SEQ + h * HD3, HD3)
                for i in range(2):
                    for dst, src in ((q3, q_[:, rows, :]), (k3, k_[i:i + 1, rows, :].to_broadcast([2, HD3, SEQ]))):
                        sp.dma_start(dst[i * P // 2:(i + 1) * P // 2, h % 4, :].bitcast(F32),
                                     src).then_inc(qk3_loaded[h % 4], 16)

            def load_values(b, g):
                for i in range(2):
                    sp.dma_start(v3[i][:, g % 2, :, :].bitcast(F32),
                                 t_in["qkv_scratch"][2][i, bass.ds(b * SEQ, SEQ), g * P:(g + 1) * P]
                                 .rearrange("(t p) c -> p t c", p=P)).then_inc(v3_loaded[g % 2], 16)

            def load_attention(b, last):
                def head(b_, h, ahead_by):
                    sp.wait_ge(sc3_full, b * H3 + (h + ahead_by - 3) * T)
                    sp.sem_inc(sp_passed, 1)
                    load_head(b_, h)

                def values(b_, g, ahead_by):
                    sp.wait_ge(o3_full, b * HEADS3 + 4 * (g + ahead_by - 1))
                    sp.sem_inc(sp_passed, 1)
                    load_values(b_, g)

                for h in range(4, HEADS3):
                    head(b, h, 0)
                    if h in (8, 12):
                        values(b, h // 4, 0)
                if not last:
                    for h in range(4):
                        head(b + 1, h, HEADS3)
                        if h == 0:
                            values(b + 1, 0, 4)
                    values(b + 1, 1, 4)

            load_pieces(0, ahead)
            if "A3" in phases:
                sp.wait_ge(operand_ready, seq0["A3"])
                for s in (q_stored, k_stored, v_stored):
                    sp.wait_ge(s, 32 * (B * T + 1))
                for h in range(4):
                    load_head(0, h)
                    if h % 2:
                        load_values(0, h // 2)
                with sp.Fori(0, B - 1) as b:
                    load_attention(b, False)
                load_attention(B - 1, True)
            load_pieces(ahead, len(pieces))
            if "Mv" in phases:
                sp.wait_ge(x_done, xd0["Mv"])
                sp.wait_ge(finished, 1)
            else:
                sp.wait_ge(x_done, 1 + sum(B * T for ph in phases if ph not in ("K0", "Q3")))
            for b in range(B):
                sp.dma_start(out[b * SEQ:(b + 1) * SEQ, :].rearrange("(t p) d -> p t d", p=P),
                             x[:, b * T:(b + 1) * T, :]).then_inc(stored, 16)
            sp.wait_ge(stored, 16 * B)

        @block.gpsimd
        def _(pool):
            pool.wait_ge(consts_loaded, CONSTS)
            for t in range(T):
                nc.gpsimd.indirect_dma_start(
                    rope[:, t, :], None, t_in["rope_table"],
                    bass.IndirectOffsetOnAxis(ap=pos[:, t:t + 1].bitcast(mybir.dt.uint32), axis=0)).then_inc(rope_loaded, 16)

            def split(first, end):
                for n, (name, slot, free) in list(enumerate(pieces))[first:end]:
                    hi, lo = w(name)
                    pool.wait_ge(staged[n % STAGES], 16 * (n // STAGES + 1))
                    for s, v in free:
                        pool.wait_ge(s, v)
                    nc.gpsimd.tensor_scalar(hi, stage[:, n % STAGES, :], 1.0, 1.0, ALU.mult, ALU.mult).then_inc(w_hi, 1)
                    pool.wait_ge(w_hi, n + 1)
                    nc.gpsimd.tensor_tensor(lo, stage[:, n % STAGES, :], hi.bitcast(F32),
                                            ALU.subtract).then_inc(w_ready, 1)

            split(0, ahead)
            if "A3" in phases:
                with pool.Fori(0, B) as b:
                    for s in range(H3):
                        at = slice(0, (s % T + 1) * P)
                        pool.wait_ge(rec3_ready, b * H3 + s + 1)
                        nc.gpsimd.tensor_tensor(p3[:, s % 4, at], p3[:, s % 4, at],
                                                rec3[:, s:s + 1].to_broadcast([P, (s % T + 1) * P]),
                                                ALU.mult).then_inc(p3_ready, 1)
            split(ahead, len(pieces))

        @block.tensor
        def _(pe):
            def mm3(o, l, r, first, last):
                nc.tensor.matmul(o, l[0], r[0], start=first, stop=False)
                nc.tensor.matmul(o, l[0], r[1], start=False, stop=False)
                return nc.tensor.matmul(o, l[1], r[0], start=False, stop=last)

            def bank(n, s_=slice(0, 512), rows=slice(0, P)):
                return ring[rows, n % 4, s_]

            def group(n, k, *needs):
                pe.wait_ge(operand_ready, n + max(k - 3, *needs, -3))

            def weights(name):
                pe.wait_ge(w_ready, index_of[name] + 1)
                return w(name)

            def cut(parts, *index):
                return [p_[index] for p_ in parts]

            def transposes(n0, m0, src, k, count=1):
                for t in range(T):
                    last = nc.tensor.transpose(ring[:, (m0 + k) % 4, t * P:(t + 1) * P],
                                               src[:, t, k * P:(k + 1) * P], ident[:])
                last.then_inc(psum_full, count)

            def TR(ph, n0, m0, nth, src=None, spare=0):
                if nth is not None:
                    pe.wait_ge(xn_ready, nth)
                for k in range(KT):
                    group(n0, k)
                    transposes(n0, m0, xn if src is None else src, k, 1 + (spare if k == KT - 1 else 0))

            def start_k0(n):
                if n >= 4:
                    pe.wait_ge(operand_ready, n - 3)

            def phase_K0():
                ctxp = [weights(("ctx", k)) for k in range(2)]
                c4 = [[p_.rearrange("p (b u m) -> p b u m", b=B, u=2) for p_ in c_] for c_ in ctxp]
                n = 0
                wm = [weights(("wmem", k)) for k in range(2)]
                for b in range(B):
                    start_k0(n)
                    for k in range(2):
                        last = mm3(bank(n), [p_[:, b, :, :] for p_ in c4[k]], wm[k], k == 0, k == 1)
                    last.then_inc(psum_full, 1)
                    n += 1
                for d in range(KT):
                    start_k0(n)
                    for k in range(2):
                        last = mm3(bank(n, slice(0, B * M)), cut(wm[k], slice(None), slice(d * P, (d + 1) * P)),
                                   [p_[:, :, 0, :] for p_ in c4[k]], k == 0, k == 1)
                    last.then_inc(psum_full, 1)
                    n += 1
                for l in "12":
                    for pair in range(PAIRS):
                        start_k0(n)
                        for k in range(2):
                            wk = weights((f"wkv{l}", (pair // 4) * 2 + k))
                            last = mm3(bank(n, slice(0, B * M)),
                                       cut(wk, slice(None), slice((pair % 4) * P, (pair % 4 + 1) * P)),
                                       [p_[:, :, 0, :] for p_ in c4[k]], k == 0, k == 1)
                        last.then_inc(psum_full, 1)
                        n += 1
                    for h in range(2):
                        for b in range(B):
                            start_k0(n)
                            for k in range(2):
                                wv = weights((f"wkv{l}", 4 + h * 2 + k))
                                last = mm3(bank(n), [p_[:, b, :, :] for p_ in c4[k]], wv, k == 0, k == 1)
                            last.then_inc(psum_full, 1)
                            n += 1
                ck = [weights(("ckv", k)) for k in range(2)]
                for f in range(2):
                    start_k0(n)
                    for k in range(2):
                        last = mm3(bank(n, slice(0, B * M)), cut(ck[k], slice(None), slice(f * P, (f + 1) * P)),
                                   [p_[:, :, 0, :] for p_ in c4[k]], k == 0, k == 1)
                    last.then_inc(psum_full, 1)
                    n += 1
                for b in range(B):
                    start_k0(n)
                    for k in range(2):
                        last = mm3(bank(n, slice(0, MD)), [p_[:, b, :, :] for p_ in c4[k]],
                                   cut(ck[k], slice(None), slice(MD, 2 * MD)), k == 0, k == 1)
                    last.then_inc(psum_full, 1)
                    n += 1
                assert n == N_K0

            def phase_G():
                n0 = seq0["G"]
                m = n0 % 4

                def body(b, last_batch):
                    n = n0 + b * 16
                    for s in range(2):
                        group(n, 4 + s, 4)
                        for tt in range(2):
                            t = 2 * s + tt
                            for k in range(KT):
                                last = mm3(ring[:, (m + 4 + s) % 4, tt * M:(tt + 1) * M],
                                           cut(xT, slice(None), k, slice(t * P, (t + 1) * P)),
                                           [p_[:, k, bass.ds(b * M, M)] for p_ in mpT], k == 0, k == KT - 1)
                        last.then_inc(psum_full, 1)
                    for s in range(2):
                        group(n, 6 + s, 5 + s)
                        pe.sem_inc(pe_passed, 1)
                        for tt in range(2):
                            last = nc.tensor.transpose(ring[0:M, (m + 6 + s) % 4, tt * P:(tt + 1) * P],
                                                       gP[:, 2 * s + tt, :], ident[:])
                        last.then_inc(psum_full, 1)
                    for t in range(T):
                        group(n, 8 + t, 7 + t // 2)
                        pe.sem_inc(pe_passed, 1)
                        mm3(ring[:, (m + 8 + t) % 4, :], cut(gPT, slice(None), slice(t * P, (t + 1) * P)),
                            [p_[:, bass.ds(b, 1), :].rearrange("p o d -> p (o d)") for p_ in mpM],
                            True, True).then_inc(psum_full, 1)
                    for k in range(KT):
                        group(n, 12 + k, 12)
                        transposes(n + 12, m, ctxf, k)
                    pe.wait_ge(x_done, xd0["G"] + b * T)
                    for half, src in ((0, xT), (1, cT)):
                        if half:
                            if not last_batch:
                                TR("G", n + 16, m, xn0["G"] + b + 2)
                            pe.wait_ge(operand_ready, n + 16)
                        for k in range(KT):
                            wg = weights(("wg", half * KT + k))
                            for t in range(T):
                                last = mm3(y_psum[:, t, :], cut(src, slice(None), k, slice(t * P, (t + 1) * P)), wg,
                                           half == 0 and k == 0, half == 1 and k == KT - 1)
                    last.then_inc(y_done, 1)

                TR("G", n0, m, xn0["G"] + 1)
                with pe.Fori(0, B - 1) as b:
                    body(b, False)
                body(B - 1, True)

            def phase_A(l):
                ph = "A" + l
                start = seq0[ph]

                def Q(h, n, m, k0, scores_end=None):
                    if scores_end is not None:
                        pe.wait_ge(scores_copied, scores_end)
                    for p in range(4):
                        if scores_end is None:
                            group(n, k0 + p, k0)
                        wq = [part.rearrange("p (k c) -> p k c", k=KT) for part in weights((f"wq{l}", 4 * h + p))]
                        for k in range(KT):
                            last = mm3(ring[:, (m + k0 + p) % 4, :], cut(wq, slice(None), k),
                                       cut(xT, slice(None), k), k == 0, k == KT - 1)
                        last.then_inc(psum_full, 1)

                def S(h, n, m, k0, q_end):
                    for t in range(T):
                        group(n, k0 + t, q_end)
                        for p in range(4):
                            last = mm3(ring[:, (m + k0 + t) % 4, p * P:(p + 1) * P],
                                       cut(qT, slice(None), p, slice(t * P, (t + 1) * P)),
                                       cut(kbd, slice(None), slice((4 * h + p) * P, (4 * h + p + 1) * P)), True, True)
                        last.then_inc(psum_full, 1)

                def TO(h, n, m, k0, s_end):
                    for i, (kind, p) in enumerate(TO_ORDER):
                        if kind == "T":
                            group(n, k0 + i, s_end)
                            for t in range(T):
                                last = nc.tensor.transpose(ring[:, (m + k0 + i) % 4, t * P:(t + 1) * P],
                                                           pr[:, t, p * P:(p + 1) * P], ident[:])
                        else:
                            group(n, k0 + i, k0 + TO_ORDER.index(("T", p)) + 1)
                            last = mm3(ring[:, (m + k0 + i) % 4, :],
                                       cut(vbd, slice(None), slice((4 * h + p) * P, (4 * h + p + 1) * P)),
                                       cut(pT, slice(None), p % 2), True, True)
                        last.then_inc(psum_full, 1)

                def W(h, n, k0):
                    for p in range(4):
                        pe.wait_ge(operand_ready, n + k0 + TO_ORDER.index(("O", p)) + 1)
                        wo = weights((f"wo{l}", 4 * h + p))
                        for t in range(T):
                            last = mm3(y_psum[:, t, :], cut(oT, slice(None), p, slice(t * P, (t + 1) * P)), wo,
                                       h == 0 and p == 0, h == 1 and p == 3)
                        last.then_inc(y_done, 1)

                def body(b, n, m, last):
                    at, _ = a_layout(last)
                    u0 = copied0[ph] + b * 8
                    kv = ("12".index(l) * B + b + 1) * 32
                    pe.wait_ge(k_loaded, kv)
                    S(0, n, m, at["S0"], 0)
                    pe.wait_ge(v_loaded, kv)
                    Q(1, n, m, at["Q1"], u0 + 4)
                    TO(0, n, m, at["TO0"], at["S0"] + 4)
                    if not last:
                        TR(ph, n + at["TR"], m + at["TR"], xn0[ph] + b + 2)
                    S(1, n, m, at["S1"], at["Q1"] + 4)
                    pe.wait_ge(x_done, xd0[ph] + b * T)
                    W(0, n, at["TO0"])
                    if not last:
                        pe.wait_ge(operand_ready, n + at["TR"] + 4)
                        Q(0, n, m, at["Q2"], u0 + 8)
                    TO(1, n, m, at["TO1"], at["S1"] + 4)
                    W(1, n, at["TO1"])

                TR(ph, start, start, xn0[ph] + 1)
                Q(0, start, start, 4)
                with pe.Fori(0, B - 1) as b:
                    body(b, start + 8 + b * 36, start + 8, False)
                body(B - 1, start + 8 + (B - 1) * 36, start + 8, True)

            def phase_F(l):
                ph = "F" + l
                start = seq0[ph]

                def up(j, n, m):
                    group(n, j, 0)
                    w1 = [p_.rearrange("p (k c) -> p k c", k=KT) for p_ in weights((f"w1_{l}", j))]
                    for k in range(KT):
                        last = mm3(ring[:, (m + j) % 4, :], cut(w1, slice(None), k), cut(xT, slice(None), k),
                                   k == 0, k == KT - 1)
                    last.then_inc(psum_full, 1)

                def down(j, n):
                    pe.wait_ge(operand_ready, n + j + 1)
                    w2 = weights((f"w2_{l}", j))
                    for t in range(T):
                        last = mm3(y_psum[:, t, :], cut(hT, slice(None), slice(t * P, (t + 1) * P)), w2,
                                   j == 0, j == FF - 1)
                    last.then_inc(y_done, 1)

                def body(b, n, m, last):
                    up(0, n, m)
                    pe.wait_ge(x_done, xd0[ph] + b * T)
                    for j in range(1, FF):
                        up(j, n, m)
                        down(j - 1, n)
                    if not last:
                        TR(ph, n + FF, m + FF, xn0[ph] + b + 2)
                    down(FF - 1, n)

                TR(ph, start, start, xn0[ph] + 1)
                with pe.Fori(0, B - 1) as b:
                    body(b, start + 4 + b * 20, start + 4, False)
                body(B - 1, start + 4 + (B - 1) * 20, start + 4, True)

            def phase_Q3():
                start = seq0["Q3"]

                def body(b, n, m, last):
                    for kind, t, k0 in q3_order(last):
                        if kind == "P":
                            has_v = pe.value_load(v_plan[0:1, bass.ds(b * T + t, 1)], min_val=0, max_val=1)
                            for c in range(3):
                                group(n, k0 + c, 0)
                                wl = [weights(("qkv_l", 4 * c + k)) for k in range(KT)]
                                wv = [weights(("qkv_v", 4 * c + k)) for k in range(KT)]
                                at = slice(t * P, (t + 1) * P)

                                def part(src, w_, k):
                                    return mm3(ring[:, (m + k0 + c) % 4, :], cut(src, slice(None), k, at), w_[k],
                                               (src, k) == (xT, 0), (src, k) == (xT, KT - 1))

                                for k in range(KT - 1):
                                    part(xT, wl, k)
                                with pe.If(has_v > 0):
                                    for k in range(KT):
                                        part(xTv, wv, k)
                                last_mm = part(xT, wl, KT - 1)
                                last_mm.then_inc(psum_full, 1)
                        elif kind == "X":
                            at_p = [k_ for x_, t_, k_ in q3_order(last) if (x_, t_) == ("P", t)][0]
                            for c in range(2):
                                group(n, k0 + c, at_p + c + 1)
                                for f in range(KT):
                                    last_mm = nc.tensor.transpose(ring[:, (m + k0 + c) % 4, f * P:(f + 1) * P],
                                                                  r3[:, t % 2, c, f * P:(f + 1) * P], ident[:])
                                last_mm.then_inc(psum_full, 1)
                        else:
                            TR("Q3", n + k0, m + k0, xn0["Q3"] + b + 2, xn if kind == "TRl" else xnv)

                pe.wait_ge(counted, 3)
                TR("Q3", start, start, xn0["Q3"] + 1)
                TR("Q3", start + 4, start + 4, None, xnv)
                with pe.Fori(0, B - 1) as b:
                    body(b, start + 8 + b * 28, start + 8, False)
                body(B - 1, start + 8 + (B - 1) * 28, start + 8, True)

            def phase_A3():
                pe.wait_ge(operand_ready, seq0["A3"])
                pe.wait_ge(causal_ready, 2)
                with pe.Fori(0, B) as b:
                    s0_, h0 = b * H3, b * HEADS3

                    def S(s):
                        h, t = s // T, s % T
                        if t == 0:
                            pe.wait_ge(qk3_loaded[h % 4], 64 * 4 * b + 64 * (h // 4 + 1))
                        if s == 0:
                            pe.wait_ge(x_done, xd0["A3"] + b * T)
                        if s >= 4:
                            pe.wait_ge(p3_exp, s0_ + s - 3)
                        pe.sem_inc(pe_passed, 1)
                        nc.tensor.matmul(ring[:, s % 4, 0:(t + 1) * P], q3[:, h % 4, t * P:(t + 1) * P],
                                         k3[:, h % 4, 0:(t + 1) * P], start=True, stop=False)
                        nc.tensor.matmul(ring[:, s % 4, t * P:(t + 1) * P], ident_r[:], causal_r[:],
                                         start=False, stop=True).then_inc(sc3_full, 1)

                    def T3(s):
                        t = s % T
                        pe.wait_ge(p3_ready, s0_ + s + 1)
                        if s >= 2:
                            pe.wait_ge(pt3_ready, s0_ + s - 1)
                        pe.sem_inc(pe_passed, 1)
                        for k in range(t + 1):
                            last = nc.tensor.transpose(y_psum[:, s % 2, k * P:(k + 1) * P],
                                                       p3[:, s % 4, k * P:(k + 1) * P], ident[:])
                        last.then_inc(pt3_full, 1)

                    def PV(s):
                        h, part = s // T, s % T
                        passes = {0: [(0, 0, 0), (3, 0, 0), (3, 0, 1), (3, 1, 0)], 1: [(1, 0, 0), (1, 0, 1), (1, 1, 0)],
                                  2: [(2, 0, 0), (2, 0, 1), (2, 1, 0)], 3: [(0, 0, 1), (0, 1, 0)]}[part]
                        if part == 0:
                            pe.wait_ge(pt3_ready, s0_ + 4 * h + 4)
                            if h >= 2:
                                pe.wait_ge(o3_ready, h0 + h - 1)
                            if h % 4 == 0:
                                pe.wait_ge(v3_loaded[h // 4 % 2], 32 * 2 * b + 32 * (h // 8 + 1))
                            pe.sem_inc(pe_passed, 1)
                        for k, i, j in passes:
                            last = nc.tensor.matmul(y_psum[:, 2 + h % 2, k * P:SEQ], v3[i][:, h // 4 % 2, k, :],
                                                    pT3[j][:, h % 2, k, k * P:SEQ],
                                                    start=(k, i, j) == (0, 0, 0), stop=(k, i, j) == (0, 1, 0))
                        if part == 3:
                            last.then_inc(o3_full, 1)

                    for s in range(3):
                        S(s)
                    for s in range(H3 + 5):
                        if s + 3 < H3:
                            S(s + 3)
                        if s >= 5:
                            PV(s - 5)
                        if s < H3:
                            T3(s)
                    for i in range(2 * T):
                        t, e = i // 2, "lv"[i % 2]
                        if i >= 4:
                            pe.wait_ge(*((dense_added, b * T + t - 1) if i % 2 == 0 else (x_done, xd0["A3"] + b * T + t - 1)))
                        else:
                            pe.wait_ge(o3_ready, h0 + HEADS3)
                        for k in range(KT):
                            last = mm3(ring[:, i % 4, :], cut(xT, slice(None), k, slice(t * P, (t + 1) * P)),
                                       weights((f"dense_{e}", k)), k == 0, k == KT - 1)
                        last.then_inc(dense_full, 1)

            def phase_C3():
                start = seq0["C3"]

                def Q(n, m, k0):
                    cw = [[part.rearrange("p (k c) -> p k c", k=2) for part in weights(("cq", i))] for i in range(2)]
                    for f in range(2):
                        group(n, k0 + f, k0)
                        for k in range(KT):
                            last = mm3(ring[:, (m + k0 + f) % 4, :],
                                       cut(cw[k // 2], slice(None), k % 2, slice(f * P, (f + 1) * P)),
                                       cut(xT, slice(None), k), k == 0, k == KT - 1)
                        last.then_inc(psum_full, 1)

                def body(b, n, m, last):
                    kv = (2 * B + b + 1) * 32
                    pe.wait_ge(k_loaded, kv)
                    for i in range(2 * T):
                        f, t = i // T, i % T
                        if i >= 4:
                            pe.wait_ge(scores_copied, copied0["C3"] + b * 8 + i - 3)
                        else:
                            group(n, i, 0)
                        mm3(ring[:, (m + i) % 4, :], cut(cqT, slice(None), f, slice(t * P, (t + 1) * P)),
                            cut(ckbd, slice(None), slice(f * 512, (f + 1) * 512)), True, True).then_inc(psum_full, 1)
                    k0 = 8
                    if not last:
                        pe.wait_ge(scores_copied, copied0["C3"] + b * 8 + 8)
                        pe.wait_ge(xn_ready, xn0["C3"] + b + 2)
                        for k in range(KT):
                            transposes(n + k0, m + k0, xn, k)
                        k0 += 4
                    pe.wait_ge(v_loaded, kv)
                    for f in range(2):
                        for p in range(5):
                            if p < 4:
                                group(n, k0, 4 * f + 4)
                                for t in range(T):
                                    last_mm = nc.tensor.transpose(ring[:, (m + k0) % 4, t * P:(t + 1) * P],
                                                                  cpr[:, f * T + t, p * P:(p + 1) * P], ident[:])
                                last_mm.then_inc(psum_full, 1)
                                k0 += 1
                            if p:
                                pe.wait_ge(operand_ready, n + k0 - (1 if p < 4 else 0))
                                col = f * 512 + (p - 1) * P
                                at_o = k0 + 3 - p if p < 4 else k0
                                last_mm = mm3(ring[:, (m + at_o) % 4, :], cut(cvbd, slice(None), slice(col, col + P)),
                                              cut(cpT, slice(None), (p - 1) % 2), p == 1, p == 4)
                        last_mm.then_inc(psum_full, 1)
                        k0 += 1
                    if not last:
                        Q(n, m, k0)
                    pe.wait_ge(x_done, xd0["C3"] + b * T)
                    pe.wait_ge(operand_ready, n + k0)
                    for f in range(2):
                        wd = weights(("cdense", f))
                        for t in range(T):
                            last_mm = mm3(y_psum[:, t, :], cut(coT, slice(None), f, slice(t * P, (t + 1) * P)), wd,
                                          f == 0, f == 1)
                    last_mm.then_inc(y_done, 1)

                TR("C3", start, start, xn0["C3"] + 1)
                Q(start, start, 4)
                with pe.Fori(0, B - 1) as b:
                    body(b, start + 6 + b * 24, start + 6, False)
                body(B - 1, start + 6 + (B - 1) * 24, start + 6, True)

            def phase_M(e):
                ph = "M" + e
                start = seq0[ph]

                def up(j, n, m):
                    for i, name in enumerate(("gate", "up")):
                        group(n, 2 * j + i, 0)
                        wu = [p_.rearrange("p (k c) -> p k c", k=KT) for p_ in weights((f"{name}_{e}", j))]
                        for k in range(KT):
                            last = mm3(ring[:, (m + 2 * j + i) % 4, :], cut(wu, slice(None), k),
                                       cut(xT, slice(None), k), k == 0, k == KT - 1)
                        last.then_inc(psum_full, 1)

                def down(j, n):
                    pe.wait_ge(operand_ready, n + 2 * j + 2)
                    wd = weights((f"down_{e}", j))
                    for t in range(T):
                        last = mm3(y_psum[:, t, :], cut(mT, slice(None), slice(t * P, (t + 1) * P)), wd,
                                   j == 0, j == HT - 1)
                    last.then_inc(y_done, 1)

                def body(b, n, m, last):
                    up(0, n, m)
                    pe.wait_ge(x_done, xd0[ph] + b * T)
                    for j in range(1, HT):
                        up(j, n, m)
                        down(j - 1, n)
                    if not last:
                        TR(ph, n + 2 * HT, m + 2 * HT, xn0[ph] + b + 2, spare=2)
                    down(HT - 1, n)

                if e == "l":
                    TR(ph, start, start, xn0[ph] + 1, spare=2)
                    with pe.Fori(0, B - 1) as b:
                        body(b, start + 6 + b * 28, start + 6, False)
                    body(B - 1, start + 6 + (B - 1) * 28, start + 6, True)
                else:
                    with pe.Fori(0, pe.value_load(v_plan[0:1, 2 * B * T:], min_val=1, max_val=B)) as i:
                        n = start + i * 28
                        TR(ph, n, start, xn0[ph] + i + 1, spare=2)
                        body(i, n + 6, start + 6, True)

            pe.wait_ge(consts_loaded, CONSTS)
            pe.wait_ge(counted, 1)
            nc.tensor.matmul(y_psum[:, 0, 0:B * T], xn[:, 3, 256:256 + P], vis[:, 1, :], start=True, stop=True).then_inc(counted, 1)
            for ph in phases:
                if ph in ("A1", "A2"):
                    phase_A(ph[1])
                elif ph[0] in "FM":
                    (phase_F if ph[0] == "F" else phase_M)(ph[1])
                else:
                    {"K0": phase_K0, "G": phase_G, "Q3": phase_Q3, "A3": phase_A3, "C3": phase_C3}[ph]()

        @block.scalar
        def _(act):
            def hi_copy(dst, src, n, scale=1.0):
                act.wait_ge(psum_full, n + 1)
                return nc.scalar.activation(dst, src, ACT.Copy, scale=scale).then_inc(act_out, 1)

            def load_kv(li, kv, b, dst, s):
                for i in range(2):
                    act.dma_start(dst[i][:].bitcast(F32),
                                  t_in["kv_scratch"][li][kv][i][bass.ds(b * P, P), :]).then_inc(s, 16)

            def phase_K0():
                n = 0
                for b in range(B):
                    hi_copy(mpM[0][:, b, :], ring[0:M, n % 4, :], n)
                    n += 1
                for d in range(KT):
                    hi_copy(mpT[0][:, d, :], ring[:, n % 4, 0:B * M], n)
                    n += 1
                act.wait_ge(zeroed, 1)
                bdh = bd[0][:].rearrange("p b (q c) -> p b q c", q=PAIRS)
                for r, l in enumerate("12"):
                    if r:
                        act.wait_ge(bd_stored, 32 * 2 * r)
                    for pair in range(PAIRS):
                        act.wait_ge(psum_full, n + 1)
                        src = ring[:, n % 4, 0:B * M].rearrange("p (b m) -> p b m", b=B)
                        nc.scalar.activation(bdh[0:64, :, pair, 0:64], src[0:64], ACT.Copy)
                        nc.scalar.activation(bdh[64:128, :, pair, 64:128], src[64:128], ACT.Copy).then_inc(act_out, 1)
                        n += 1
                    act.wait_ge(operand_ready, n)
                    for i in range(2):
                        act.dma_start(t_in["kv_scratch"][r][0][i].rearrange("(b p) c -> p b c", p=P),
                                      bd[i][:].bitcast(F32)).then_inc(bd_stored, 16)
                    act.wait_ge(bd_stored, 32 * (2 * r + 1))
                    for h in range(2):
                        for b in range(B):
                            act.wait_ge(psum_full, n + 1)
                            src = ring[:, n % 4, :].rearrange("p (q u c) -> p q u c", q=4, u=2)
                            nc.scalar.activation(bdh[0:64, b, 4 * h:4 * h + 4, 0:64], src[0:64, :, 0, :], ACT.Copy)
                            nc.scalar.activation(bdh[64:128, b, 4 * h:4 * h + 4, 64:128], src[64:128, :, 1, :],
                                                 ACT.Copy).then_inc(act_out, 1)
                            n += 1
                    act.wait_ge(operand_ready, n)
                    for i in range(2):
                        act.dma_start(t_in["kv_scratch"][r][1][i].rearrange("(b p) c -> p b c", p=P),
                                      bd[i][:].bitcast(F32)).then_inc(bd_stored, 16)
                act.wait_ge(operand_ready, n + 2)
                for i in range(2):
                    act.dma_start(t_in["kv_scratch"][2][0][i].rearrange("(b p) c -> p b c", p=P),
                                  bd[i][:].bitcast(F32)).then_inc(bd_stored, 16)
                act.wait_ge(operand_ready, n + 6)
                for i in range(2):
                    act.dma_start(t_in["kv_scratch"][2][1][i].rearrange("(b p) c -> p b c", p=P),
                                  bd[i][:].bitcast(F32)).then_inc(bd_stored, 16)
                act.wait_ge(bd_stored, 32 * 6)
                act.wait_ge(act_out, n)
                act.sem_inc(act_out, 6)

            def phase_G():
                act.dma_start(gbias[:], t_in["b_gate"]).then_inc(consts_loaded, 16)
                act.dma_start(gnorm[:], t_in["norm_w"]).then_inc(consts_loaded, 16)
                m = seq0["G"] % 4

                def transposed(n):
                    for k in range(KT):
                        hi_copy(xT[0][:, k, :], ring[:, (m + k) % 4, :], n + k)

                def body(b, last):
                    n = seq0["G"] + b * 16
                    if not last:
                        act.wait_ge(x_loaded, 16 * b + 16)
                        act.sem_inc(act_passed, 1)
                        act.dma_start(x[:, bass.ds((b + 1) * T, T), :],
                                      t_in["x"][bass.ds((b + 1) * SEQ, SEQ), :].rearrange("(t p) d -> p t d", p=P)
                                      ).then_inc(x_loaded, 16)
                    for s in range(2):
                        act.wait_ge(scores_shifted, s0["G"] + b * 2 + s + 1)
                        nc.scalar.activation(gP[:, 2 * s:2 * s + 2, :], gs[:, 2 * s:2 * s + 2, :],
                                             ACT.Exp).then_inc(act_out, 1)
                    for s in range(2):
                        hi_copy(gPT[0][:, s * 256:(s + 1) * 256], ring[0:M, (m + 6 + s) % 4, 0:256], n + 6 + s)
                    for t in range(T):
                        hi_copy(ctxf[:, t, :], ring[:, (m + 8 + t) % 4, :], n + 8 + t)
                    for k in range(KT):
                        hi_copy(cT[0][:, k, :], ring[:, (m + 12 + k) % 4, :], n + 12 + k)
                    if not last:
                        transposed(n + 16)
                    for t in range(T):
                        act.wait_ge(gate_in, b * T + t + 1)
                        nc.scalar.activation(gz[:, t % 2, :], gz[:, t % 2, :], ACT.Sigmoid).then_inc(gate_out, 1)

                transposed(seq0["G"])
                with act.Fori(0, B - 1) as b:
                    body(b, False)
                body(B - 1, True)

            def norm_T(ph, n, m, g, bias):
                act.wait_ge(psum_full, n + KT)
                for k in range(KT):
                    nc.scalar.activation(xn[:, k, :], ring[:, (m + k) % 4, :], ACT.Identity,
                                         scale=par[:, g, k:k + 1], bias=par[:, bias, k:k + 1]).then_inc(act_out, 1)

            def phase_A(l):
                ph = "A" + l
                li = "12".index(l)
                g, bias = PARAMS.index(f"L{l}_xattn_ln_q_g"), PARAMS.index(f"L{l}_xattn_ln_q_b")
                start = seq0[ph]
                act.wait_ge(x_done, xd0[ph])
                load_kv(li, 0, 0, kbd, k_loaded)
                load_kv(li, 1, 0, vbd, v_loaded)

                def Q(n, m):
                    for p in range(4):
                        hi_copy(qT[0][:, p, :], ring[:, (m + p) % 4, :], n + p, 0.125)

                def S(s_at, n):
                    for t in range(T):
                        act.wait_ge(scores_shifted, s_at + t + 1)
                        nc.scalar.activation(pr[:, t, :], sc[:, t % 2, :], ACT.Exp).then_inc(act_out, 1)

                def TO(n, m):
                    for i, (kind, p) in enumerate(TO_ORDER):
                        dst = pT[0][:, p % 2, :] if kind == "T" else oT[0][:, p, :]
                        hi_copy(dst, ring[:, (m + i) % 4, :], n + i)

                def body(b, n, m, last):
                    at, _ = a_layout(last)
                    u0 = s0[ph] + b * 8
                    S(u0, n + at["S0"])
                    Q(n + at["Q1"], m + at["Q1"])
                    TO(n + at["TO0"], m + at["TO0"])
                    if not last:
                        norm_T(ph, n + at["TR"], m + at["TR"], g, bias)
                    S(u0 + 4, n + at["S1"])
                    if not last:
                        Q(n + at["Q2"], m + at["Q2"])
                        load_kv(li, 0, b + 1, kbd, k_loaded)
                    TO(n + at["TO1"], m + at["TO1"])
                    if not last:
                        load_kv(li, 1, b + 1, vbd, v_loaded)

                norm_T(ph, start, start, g, bias)
                Q(start + 4, start + 4)
                with act.Fori(0, B - 1) as b:
                    body(b, start + 8 + b * 36, start + 8, False)
                body(B - 1, start + 8 + (B - 1) * 36, start + 8, True)

            def phase_F(l):
                ph = "F" + l
                g, bias = PARAMS.index(f"L{l}_xattn_ln_ff_g"), PARAMS.index(f"L{l}_xattn_ln_ff_b")
                start = seq0[ph]

                def body(b, n, m, last):
                    for j in range(FF):
                        act.wait_ge(psum_full, n + j + 1)
                        act.wait_ge(operand_ready, n + j)
                        nc.scalar.activation(hf[:], ring[:, (m + j) % 4, :], ACT.Gelu).then_inc(act_out, 1)
                    if not last:
                        norm_T(ph, n + FF, m + FF, g, bias)

                norm_T(ph, start, start, g, bias)
                with act.Fori(0, B - 1) as b:
                    body(b, start + 4 + b * 20, start + 4, False)
                body(B - 1, start + 4 + (B - 1) * 20, start + 4, True)

            def norm_hi(dst, n, m, g, spare=0):
                for k in range(KT):
                    act.wait_ge(psum_full, n + k + 1)
                    nc.scalar.activation(dst[0][:, k, :], ring[:, (m + k) % 4, :], ACT.Copy,
                                         scale=par[:, g, k:k + 1]).then_inc(act_out, 1 + (spare if k == KT - 1 else 0))

            def phase_Q3():
                start = seq0["Q3"]
                g = PARAMS.index("L3_xattn_ln_in_w")

                def body(b, n, m, last):
                    for kind, t, k0 in q3_order(last):
                        if kind == "P":
                            act.wait_ge(v_stored, 32 * (b * T + t + 1))
                            act.wait_ge(psum_full, n + k0 + 3)
                            act.sem_inc(act_passed, 1)
                            nc.scalar.activation(v_out[0][:], ring[:, (m + k0 + 2) % 4, :], ACT.Copy).then_inc(act_out, 3)
                            act.wait_ge(operand_ready, n + k0 + 3)
                            for i in range(2):
                                act.dma_start(t_in["qkv_scratch"][2][i, bass.ds(b * SEQ + t * P, P), :],
                                              v_out[i][:].bitcast(F32)).then_inc(v_stored, 16)
                        elif kind == "X":
                            for c, s in enumerate((q_stored, k_stored)):
                                act.wait_ge(s, 32 * (b * T + t + 1))
                                act.wait_ge(psum_full, n + k0 + c + 1)
                                act.sem_inc(act_passed, 1)
                                nc.scalar.activation(qk_out[0][:, c, :], ring[:, (m + k0 + c) % 4, :],
                                                     ACT.Copy).then_inc(act_out, 1)
                            for c, s in enumerate((q_stored, k_stored)):
                                act.wait_ge(operand_ready, n + k0 + c + 1)
                                for i in range(2):
                                    rows = t_in["qkv_scratch"][c][i, bass.ds(b * SEQ, SEQ), t * P:(t + 1) * P]
                                    act.dma_start(rows.rearrange("(f p) c -> p f c", p=P),
                                                  qk_out[i][:, c, :].rearrange("p (f c) -> p f c", f=KT).bitcast(F32)
                                                  ).then_inc(s, 16)
                        else:
                            norm_hi(xT if kind == "TRl" else xTv, n + k0, m + k0, g)

                for s in (q_stored, k_stored, v_stored):
                    act.sem_inc(s, 32)
                norm_hi(xT, start, start, g)
                norm_hi(xTv, start + 4, start + 4, g)
                with act.Fori(0, B - 1) as b:
                    body(b, start + 8 + b * 28, start + 8, False)
                body(B - 1, start + 8 + (B - 1) * 28, start + 8, True)

            def phase_A3():
                act.wait_ge(operand_ready, seq0["A3"])
                act.dma_start(causal[:], t_in["causal"]).then_inc(consts_loaded, 16)

                def body(b):
                    s0_, h0 = b * H3, b * HEADS3

                    def E(s):
                        n = (s % T + 1) * P
                        act.wait_ge(sc3_max, s0_ + s + 1)
                        nc.scalar.activation(p3[:, s % 4, 0:n], ring[:, s % 4, 0:n], ACT.Exp,
                                             bias=nm3[:, s:s + 1],
                                             accum_out=sum3[:, s:s + 1]).then_inc(p3_exp, 1)

                    E(0)
                    E(1)
                    for s in range(H3 + 5):
                        if s + 2 < H3:
                            E(s + 2)
                        if s < H3:
                            t = s % T
                            act.wait_ge(pt3_full, s0_ + s + 1)
                            nc.scalar.activation(pT3[0][:, s // T % 2, 0:t + 1, t * P:(t + 1) * P],
                                                 y_psum[:, s % 2, 0:(t + 1) * P].rearrange("p (k q) -> p k q", q=P),
                                                 ACT.Copy).then_inc(pt3_hi, 1)
                        if s >= 8 and s % 4 == 0:
                            h = (s - 8) // 4
                            rows = slice(HD3 * (h % 4), HD3 * (h % 4 + 1))
                            act.wait_ge(o3_full, h0 + h + 1)
                            nc.scalar.activation(xT[0][rows, h // 4, :], y_psum[rows, 2 + h % 2, :],
                                                 ACT.Copy).then_inc(o3_hi, 1)

                with act.Fori(0, B) as b:
                    body(b)

            def phase_C3():
                start = seq0["C3"]
                g = PARAMS.index("L3_xattn_ln_post_cross_w")
                act.wait_ge(x_done, xd0["C3"])
                load_kv(2, 0, 0, ckbd, k_loaded)
                load_kv(2, 1, 0, cvbd, v_loaded)

                def Q(n, m):
                    for f in range(2):
                        hi_copy(cqT[0][:, f, :], ring[:, (m + f) % 4, :], n + f)

                def body(b, n, m, last):
                    for i in range(2 * T):
                        act.wait_ge(scores_copied, copied0["C3"] + b * 8 + i + 1)
                        nc.scalar.activation(cpr[:, i, :], csc[:, i % 2, :], ACT.Exp, scale=0.25).then_inc(act_out, 1)
                    k0 = 8
                    if not last:
                        norm_hi(xT, n + k0, m + k0, g)
                        k0 += 4
                        load_kv(2, 0, b + 1, ckbd, k_loaded)
                    for f in range(2):
                        for p in range(5):
                            dst = cpT[0][:, p % 2, :] if p < 4 else coT[0][:, f, :]
                            hi_copy(dst, ring[:, (m + k0) % 4, :], n + k0)
                            k0 += 1
                    if not last:
                        load_kv(2, 1, b + 1, cvbd, v_loaded)
                        Q(n + k0, m + k0)

                norm_hi(xT, start, start, g)
                Q(start + 4, start + 4)
                with act.Fori(0, B - 1) as b:
                    body(b, start + 6 + b * 24, start + 6, False)
                body(B - 1, start + 6 + (B - 1) * 24, start + 6, True)

            def phase_M(e):
                ph = "M" + e
                start = seq0[ph]
                g = PARAMS.index("L3_xattn_ln_post_attn_w")

                def body(b, n, m, last):
                    for j in range(HT):
                        act.wait_ge(psum_full, n + 2 * j + 1)
                        nc.scalar.activation(sg[:], ring[:, (m + 2 * j) % 4, :], ACT.Silu).then_inc(act_out, 1)
                        act.wait_ge(operand_ready, n + 2 * j + 1)
                        if j:
                            act.wait_ge(y_done, y0[ph] + b * HT + j)
                        nc.scalar.activation(mT[0][:], mf[:], ACT.Copy).then_inc(act_out, 1)
                    if not last:
                        norm_hi(xT, n + 2 * HT, m + 2 * HT, g, 2)

                if e == "l":
                    norm_hi(xT, start, start, g, 2)
                    with act.Fori(0, B - 1) as b:
                        body(b, start + 6 + b * 28, start + 6, False)
                    body(B - 1, start + 6 + (B - 1) * 28, start + 6, True)
                else:
                    act.wait_ge(counted, 3)
                    with act.Fori(0, act.value_load(v_plan[0:1, 2 * B * T:], min_val=1, max_val=B)) as i:
                        n = start + i * 28
                        norm_hi(xT, n, start, g, 2)
                        body(i, n + 6, start + 6, True)

            for dst, src in ((ident[:], t_in["ident"]), (par[:], t_in["params"]), (gates[:], t_in["gates"]),
                             (mask8, t_in["mask_s2"].rearrange("p b m -> p (b m)")), (mask_k[:], t_in["mask_k"]), (mask_v[:], t_in["mask_v"]),
                             (types, t_in["types"].rearrange("p a t -> p (a t)")), (pos[:], t_in["pos"]),
                             (xn[:, 0:3, 0:(B * T) ** 2], t_in["tile_tables"])):
                act.dma_start(dst, src).then_inc(consts_loaded, 16)
            act.dma_start(x[:, 0:T, :], t_in["x"][0:SEQ, :].rearrange("(t p) d -> p t d", p=P)).then_inc(x_loaded, 16)
            act.wait_ge(consts_loaded, CONSTS)
            nc.scalar.activation(gates[:], gates[:], ACT.Tanh).then_inc(tanh_done, 1)
            for ph in phases:
                if ph in ("A1", "A2"):
                    phase_A(ph[1])
                elif ph[0] in "FM":
                    (phase_F if ph[0] == "F" else phase_M)(ph[1])
                else:
                    {"K0": phase_K0, "G": phase_G, "Q3": phase_Q3, "A3": phase_A3, "C3": phase_C3}[ph]()

        @block.vector
        def _(dve):
            steps = {"base": 0, "n": 0}

            def step(ins):
                ins.then_inc(dve_step, 1)
                steps["n"] += 1

            def settle():
                dve.wait_ge(dve_step, steps["base"] + steps["n"])

            def loop(count, per, run):
                base = steps["base"] + steps["n"]
                with dve.Fori(0, count) as i:
                    steps["base"], steps["n"] = base + i * per, 0
                    run(i)
                    assert steps["n"] == per, steps["n"]
                steps["base"], steps["n"] = base + count * per, 0

            def lo_of(dst, full, hi, n, scale=None):
                dve.wait_ge(act_out, n + 1)
                if scale is None:
                    ins = nc.vector.tensor_tensor(dst, full, hi.bitcast(F32), ALU.subtract)
                else:
                    ins = nc.vector.scalar_tensor_tensor(dst, full, scale, hi.bitcast(F32), ALU.mult, ALU.subtract)
                ins.then_inc(operand_ready, 1)

            def rsqrt():
                step(nc.vector.tensor_scalar(nt[:].bitcast(I32), var[:].bitcast(I32), 1, None, ALU.arith_shift_right))
                settle()
                step(nc.vector.tensor_scalar(rs[:].bitcast(I32), nt[:].bitcast(I32), -1.0, float(0x5F3759DF),
                                             ALU.mult, ALU.add))
                settle()
                for _ in range(4):
                    step(nc.vector.scalar_tensor_tensor(nt[:], rs[:], -0.5, var[:], ALU.mult, ALU.mult))
                    settle()
                    step(nc.vector.tensor_tensor(nt[:], nt[:], rs[:], ALU.mult))
                    settle()
                    step(nc.vector.scalar_tensor_tensor(rs[:], nt[:], 1.5, rs[:], ALU.add, ALU.mult))
                    settle()

            def statistics(src, eps, rms):
                dve.sem_inc(dve_passed, 1)
                for t in range(T):
                    step(nc.vector.bn_stats(bst[:, t, :], src(t)))
                settle()
                dve.sem_inc(dve_passed, 1)
                for t in range(T):
                    step(nc.vector.bn_aggr(mv[:, t, :], bst[:, t, :]))
                settle()
                if rms:
                    step(nc.vector.tensor_tensor(nt[:], mv[:, :, 0], mv[:, :, 0], ALU.mult))
                    settle()
                    step(nc.vector.scalar_tensor_tensor(var[:], nt[:], eps, mv[:, :, 1], ALU.add, ALU.add))
                else:
                    step(nc.vector.tensor_scalar(var[:], mv[:, :, 1], eps, None, ALU.add))
                settle()
                rsqrt()

            NORM_LN, NORM_RMS = T + T + 1 + 2 + 12, T + T + 2 + 2 + 12

            def tile_of(b, t):
                return x[:, bass.ds(b * T + t, 1), :].rearrange("p o d -> p (o d)")

            def norm(b):
                statistics(lambda t: tile_of(b, t), 1e-5, False)
                for t in range(T):
                    if t == T - 1:
                        settle()
                    ins = nc.vector.tensor_scalar(xn[:, t, :], tile_of(b, t), mv[:, t, 0:1], rs[:, t:t + 1],
                                                  ALU.subtract, ALU.mult)
                    if t < T - 1:
                        step(ins)
                    else:
                        ins.then_inc(xn_ready, 1)

            NORM = NORM_LN + T - 1

            def split_T(n):
                for k in range(KT):
                    dve.wait_ge(act_out, n + k + 1)
                    step(nc.vector.tensor_copy(xT[0][:, k, :], xn[:, k, :]))
                    settle()
                    nc.vector.tensor_tensor(xT[1][:, k, :], xn[:, k, :], xT[0][:, k, :].bitcast(F32),
                                            ALU.subtract).then_inc(operand_ready, 1)

            def residual(b, gate, parts):
                dve.wait_ge(y_done, parts)
                for t in range(T):
                    nc.vector.scalar_tensor_tensor(tile_of(b, t), y_psum[:, t, :], gates[:, gate:gate + 1],
                                                   tile_of(b, t), ALU.mult, ALU.add).then_inc(x_done, 1)

            def phase_K0():
                n = 0
                for b in range(B):
                    lo_of(mpM[1][:, b, :], ring[0:M, n % 4, :], mpM[0][:, b, :], n)
                    n += 1
                for d in range(KT):
                    lo_of(mpT[1][:, d, :], ring[:, n % 4, 0:B * M], mpT[0][:, d, :], n)
                    n += 1
                bh, bl = [p_[:].rearrange("p b (q c) -> p b q c", q=PAIRS) for p_ in bd]
                for r, l in enumerate("12"):
                    if r:
                        dve.wait_ge(bd_stored, 32 * 2 * r)
                    for pair in range(PAIRS):
                        src = ring[:, n % 4, 0:B * M].rearrange("p (b m) -> p b m", b=B)
                        dve.wait_ge(act_out, n + 1)
                        nc.vector.tensor_tensor(bl[0:64, :, pair, 0:64], src[0:64],
                                                bh[0:64, :, pair, 0:64].bitcast(F32), ALU.subtract)
                        nc.vector.tensor_tensor(bl[64:128, :, pair, 64:128], src[64:128],
                                                bh[64:128, :, pair, 64:128].bitcast(F32),
                                                ALU.subtract).then_inc(operand_ready, 1)
                        n += 1
                    dve.wait_ge(bd_stored, 32 * (2 * r + 1))
                    for h in range(2):
                        for b in range(B):
                            src = ring[:, n % 4, :].rearrange("p (q u c) -> p q u c", q=4, u=2)
                            q = slice(4 * h, 4 * h + 4)
                            dve.wait_ge(act_out, n + 1)
                            nc.vector.tensor_tensor(bl[0:64, b, q, 0:64], src[0:64, :, 0, :],
                                                    bh[0:64, b, q, 0:64].bitcast(F32), ALU.subtract)
                            nc.vector.tensor_tensor(bl[64:128, b, q, 64:128], src[64:128, :, 1, :],
                                                    bh[64:128, b, q, 64:128].bitcast(F32),
                                                    ALU.subtract).then_inc(operand_ready, 1)
                            n += 1
                dve.wait_ge(bd_stored, 32 * 4)

                def masked(dst, src, mask, last):
                    step(nc.vector.tensor_tensor(bdf[:].rearrange("p (q c) -> p q c", q=mask.shape[1]), src, mask,
                                                 ALU.mult))
                    settle()
                    step(nc.vector.tensor_copy(dst[0], bdf[:]))
                    settle()
                    ins = nc.vector.tensor_tensor(dst[1], bdf[:], dst[0].bitcast(F32), ALU.subtract)
                    if last:
                        ins.then_inc(operand_ready, 1)
                        dve.wait_ge(operand_ready, n + 1)
                    else:
                        step(ins)
                        settle()

                for f in range(2):
                    dve.wait_ge(psum_full, n + 1)
                    for b in range(B):
                        src = ring[:, n % 4, b * M:(b + 1) * M].unsqueeze(1).to_broadcast([P, 8, M])
                        masked([p_[:, b, f * 512:(f + 1) * 512] for p_ in bd], src, mask_k[:], b == B - 1)
                    n += 1
                dve.wait_ge(bd_stored, 32 * 5)
                for b in range(B):
                    dve.wait_ge(psum_full, n + 1)
                    for f in range(2):
                        src = ring[:, n % 4, f * P:(f + 1) * P].unsqueeze(1).to_broadcast([P, 4, P])
                        masked([p_[:, b, f * 512:(f + 1) * 512] for p_ in bd], src, mask_v[:], f == 1)
                    n += 1

            def phase_G():
                dve.wait_ge(consts_loaded, CONSTS + 32)

                m = seq0["G"] % 4

                def transposed(b):
                    dve.wait_ge(x_loaded, 16 * b + 16)
                    dve.sem_inc(dve_passed, 1)
                    nc.vector.tensor_copy(xn[:], x[:, bass.ds(b * T, T), :]).then_inc(xn_ready, 1)
                    for k in range(KT):
                        lo_of(xT[1][:, k, :], ring[:, (m + k) % 4, :], xT[0][:, k, :], seq0["G"] + b * 16 + k)

                def body(b, last):
                    n = seq0["G"] + b * 16

                    def finish(s):
                        i = slice(2 * s, 2 * s + 2)
                        dve.wait_ge(act_out, n + 4 + s + 1)
                        step(nc.vector.tensor_reduce(sm[:, 0, i], gP[:, i, :], AX, ALU.add))
                        settle()
                        step(nc.vector.reciprocal(sm[:, 1, i], sm[:, 0, i]))
                        settle()
                        nc.vector.tensor_tensor(gP[:, i, :], gP[:, i, :],
                                                sm[:, 1, i].unsqueeze(2).to_broadcast([P, 2, M]),
                                                ALU.mult).then_inc(operand_ready, 1)

                    for s in range(2):
                        i = slice(2 * s, 2 * s + 2)
                        dve.wait_ge(psum_full, n + 4 + s + 1)
                        step(nc.vector.tensor_scalar(gs[:, i, :],
                                                     ring[:, (m + 4 + s) % 4, 0:2 * M].rearrange("p (t m) -> p t m", t=2),
                                                     float(D) ** -0.5, None, ALU.mult))
                        settle()
                        step(nc.vector.tensor_reduce(mx[:, 0, i], gs[:, i, :], AX, ALU.max))
                        settle()
                        nc.vector.tensor_tensor(gs[:, i, :], gs[:, i, :],
                                                mx[:, 0, i].unsqueeze(2).to_broadcast([P, 2, M]),
                                                ALU.subtract).then_inc(scores_shifted, 1)
                    finish(0)
                    finish(1)
                    for s in range(2):
                        i = slice(s * 256, (s + 1) * 256)
                        lo_of(gPT[1][:, i], ring[0:M, (m + 6 + s) % 4, 0:256], gPT[0][:, i], n + 6 + s)
                    for t in range(T):
                        dve.wait_ge(act_out, n + 8 + t + 1)
                        dve.wait_ge(operand_ready, n + 8 + t)
                        dve.sem_inc(operand_ready, 1)
                    for k in range(KT):
                        lo_of(cT[1][:, k, :], ring[:, (m + 12 + k) % 4, :], cT[0][:, k, :], n + 12 + k)
                    if not last:
                        transposed(b + 1)
                    dve.wait_ge(y_done, b + 1)

                    def gated(t):
                        dve.wait_ge(gate_out, b * T + t + 1)
                        step(nc.vector.tensor_tensor(gz[:, t % 2, :], gz[:, t % 2, :], ctxf[:, t, :], ALU.mult))
                        settle()
                        step(nc.vector.tensor_tensor(tile_of(b, t), tile_of(b, t), gz[:, t % 2, :], ALU.add))
                        settle()

                    for t in range(T):
                        nc.vector.tensor_tensor(gz[:, t % 2, :], y_psum[:, t, :], gbias[:], ALU.add).then_inc(gate_in, 1)
                        if t:
                            gated(t - 1)
                    gated(T - 1)
                    statistics(lambda t: tile_of(b, t), 1e-6, True)
                    for t in range(T):
                        nc.vector.scalar_tensor_tensor(tile_of(b, t), tile_of(b, t), rs[:, t:t + 1], gnorm[:],
                                                       ALU.mult, ALU.mult).then_inc(x_done, 1)

                transposed(0)
                loop(B - 1, 4 + 4 + 2 * T + NORM_RMS, lambda b: body(b, False))
                body(B - 1, True)

            def phase_A(l):
                ph = "A" + l
                gate = GATES.index(f"L{l}_xattn_attn_gate")
                start = seq0[ph]

                def Q(n, m):
                    for p in range(4):
                        lo_of(qT[1][:, p, :], ring[:, (m + p) % 4, :], qT[0][:, p, :], n + p, 0.125)

                def S(b, n, m):
                    def finish(t):
                        dve.wait_ge(act_out, n + t + 1)
                        pv = pr[:, t, :].rearrange("p (h k) -> p h k", k=M)
                        step(nc.vector.tensor_reduce(sm[:, t, :], pv, AX, ALU.add))
                        settle()
                        step(nc.vector.reciprocal(sm[:, t, :], sm[:, t, :]))
                        settle()
                        nc.vector.tensor_tensor(pv, pv, sm[:, t, :].unsqueeze(2).to_broadcast([P, 8, M]),
                                                ALU.mult).then_inc(operand_ready, 1)

                    for t in range(T):
                        sv = sc[:, t % 2, :].rearrange("p (h k) -> p h k", k=M)
                        dve.wait_ge(psum_full, n + t + 1)
                        nc.vector.tensor_tensor(sv, ring[:, (m + t) % 4, :].rearrange("p (h k) -> p h k", k=M),
                                                kbias[:, bass.ds(b, 1), :].to_broadcast([P, 8, M]),
                                                ALU.add).then_inc(scores_copied, 1)
                        dve.wait_ge(scores_copied, body.scores + t + 1)
                        step(nc.vector.tensor_reduce(mx[:, t, :], sv, AX, ALU.max))
                        settle()
                        nc.vector.tensor_tensor(sv, sv, mx[:, t, :].unsqueeze(2).to_broadcast([P, 8, M]),
                                                ALU.subtract).then_inc(scores_shifted, 1)
                        if t:
                            finish(t - 1)
                    finish(T - 1)

                def TO(n, m):
                    for i, (kind, p) in enumerate(TO_ORDER):
                        dst = [p_[:, p % 2, :] for p_ in pT] if kind == "T" else [p_[:, p, :] for p_ in oT]
                        lo_of(dst[1], ring[:, (m + i) % 4, :], dst[0], n + i)

                def body(b, n, m, last, prefetch):
                    at, _ = a_layout(last)
                    body.scores = copied0[ph] + b * 8
                    S(b, n + at["S0"], m + at["S0"])
                    Q(n + at["Q1"], m + at["Q1"])
                    TO(n + at["TO0"], m + at["TO0"])
                    if not last:
                        split_T(n + at["TR"])
                    body.scores = copied0[ph] + b * 8 + 4
                    S(b, n + at["S1"], m + at["S1"])
                    if not last:
                        Q(n + at["Q2"], m + at["Q2"])
                    TO(n + at["TO1"], m + at["TO1"])
                    if prefetch:
                        norm(b + 2)
                    residual(b, gate, y0[ph] + b * 8 + 8)

                dve.wait_ge(x_done, xd0[ph])
                norm(0)
                split_T(start)
                Q(start + 4, start + 4)
                norm(1)
                per = 2 * 3 * T + KT + NORM
                loop(B - 2, per, lambda b: body(b, start + 8 + b * 36, start + 8, False, True))
                body(B - 2, start + 8 + (B - 2) * 36, start + 8, False, False)
                body(B - 1, start + 8 + (B - 1) * 36, start + 8, True, False)

            def phase_F(l):
                ph = "F" + l
                gate = GATES.index(f"L{l}_xattn_ff_gate")
                start = seq0[ph]

                def body(b, n, last):
                    for j in range(FF):
                        dve.wait_ge(act_out, n + j + 1)
                        if j:
                            dve.wait_ge(y_done, y0[ph] + b * FF + j)
                        step(nc.vector.tensor_copy(hT[0][:], hf[:]))
                        settle()
                        nc.vector.tensor_tensor(hT[1][:], hf[:], hT[0][:].bitcast(F32),
                                                ALU.subtract).then_inc(operand_ready, 1)
                        if j == FF // 2 and not last:
                            norm(b + 1)
                    if not last:
                        split_T(n + FF)
                    residual(b, gate, y0[ph] + b * FF + FF)

                dve.wait_ge(x_done, xd0[ph])
                norm(0)
                split_T(start)
                loop(B - 1, FF + NORM + KT, lambda b: body(b, start + 4 + b * 20, False))
                body(B - 1, start + 4 + (B - 1) * 20, True)

            def norm_rms(b, experts=None):
                statistics(lambda t: tile_of(b, t), 1e-6, True)
                if experts is not None:
                    step(nc.vector.tensor_tensor(wrs[:], vis[:, :, bass.ds(b * T, T)],
                                                 rs[:].unsqueeze(1).to_broadcast([P, 2, T]), ALU.mult))
                    settle()
                todo = [("lv".index(e), xnv if (e, len(experts)) == ("v", 2) else xn) for e in experts or ()] or [(None, xn)]
                todo = [(e, dst, t) for e, dst in todo for t in range(T)]
                for i, (e, dst, t) in enumerate(todo):
                    if i == len(todo) - 1:
                        settle()
                    ins = nc.vector.tensor_scalar(dst[:, t, :], tile_of(b, t),
                                                  rs[:, t:t + 1] if e is None else wrs[:, e, t:t + 1], None, ALU.mult)
                    if i < len(todo) - 1:
                        step(ins)
                    else:
                        ins.then_inc(xn_ready, 1)

            NORM3 = NORM_RMS + T - 1

            def norm_lo(dst, n, m, g, spare=0):
                for k in range(KT):
                    dve.wait_ge(act_out, n + k + 1)
                    nc.vector.scalar_tensor_tensor(dst[1][:, k, :], ring[:, (m + k) % 4, :], par[:, g, k:k + 1],
                                                   dst[0][:, k, :].bitcast(F32), ALU.mult,
                                                   ALU.subtract).then_inc(operand_ready, 1 + (spare if k == KT - 1 else 0))

            def phase_Q3():
                start = seq0["Q3"]
                g = PARAMS.index("L3_xattn_ln_in_w")
                half = HD3 // 2

                def rotate(n, m, t, c):
                    src = ring[:, m % 4, :].rearrange("p (h d) -> p h d", d=HD3)
                    r = r3[:, t % 2, c, :].rearrange("p (h d) -> p h d", d=HD3)
                    tmp = tmp3[:].rearrange("p (h d) -> p h d", d=HD3)

                    def table(lo, n_):
                        return rope[:, t:t + 1, lo:lo + n_].to_broadcast([P, HEADS3, n_])

                    dve.wait_ge(psum_full, n + 1)
                    dve.wait_ge(operand_ready, n)
                    dve.sem_inc(dve_passed, 1)
                    scale = float(HD3) ** -0.5 if c == 0 else 1.0

                    def times(dst, a, b_):
                        step(nc.vector.scalar_tensor_tensor(dst, a, scale, b_, ALU.mult, ALU.mult))

                    times(r, src, table(0, HD3))
                    times(tmp[:, :, 0:half], src[:, :, half:], table(HD3, half))
                    times(tmp[:, :, half:], src[:, :, 0:half], table(HD3 + half, half))
                    settle()
                    nc.vector.tensor_tensor(r, r, tmp, ALU.add).then_inc(operand_ready, 1)

                def body(b, n, m, last):
                    for kind, t, k0 in q3_order(last):
                        if kind == "P":
                            for c in range(2):
                                rotate(n + k0 + c, m + k0 + c, t, c)
                            lo_of(v_out[1][:], ring[:, (m + k0 + 2) % 4, :], v_out[0][:], n + k0 + 2)
                        elif kind == "X":
                            for c in range(2):
                                lo_of(qk_out[1][:, c, :], ring[:, (m + k0 + c) % 4, :], qk_out[0][:, c, :], n + k0 + c)
                            if t == 1 and not last:
                                norm_rms(b + 1, "lv")
                        else:
                            norm_lo(xT if kind == "TRl" else xTv, n + k0, m + k0, g)

                dve.wait_ge(x_done, xd0["Q3"])
                dve.wait_ge(rope_loaded, 16 * T)
                norm_rms(0, "lv")
                norm_lo(xT, start, start, g)
                norm_lo(xTv, start + 4, start + 4, g)
                loop(B - 1, 2 * T * 3 + NORM_RMS + 1 + 2 * T - 1, lambda b: body(b, start + 8 + b * 28, start + 8, False))
                body(B - 1, start + 8 + (B - 1) * 28, start + 8, True)

            def phase_A3():
                def body(b):
                    s0_, h0 = b * H3, b * HEADS3
                    dve.wait_ge(x_done, xd0["A3"] + b * T)
                    step(nc.vector.tensor_copy(wrs[:], vis[:, :, bass.ds(b * T, T)]))

                    def maximum(s):
                        dve.wait_ge(sc3_full, s0_ + s + 1)
                        nc.vector.tensor_reduce(nm3[:, s:s + 1], ring[:, s % 4, 0:(s % T + 1) * P], AX, ALU.max,
                                                negate=True).then_inc(sc3_max, 1)

                    def over_sum(s):
                        dve.wait_ge(p3_exp, s0_ + s + 1)
                        nc.vector.reciprocal(rec3[:, s:s + 1], sum3[:, s:s + 1]).then_inc(rec3_ready, 1)

                    for s in range(3):
                        maximum(s)
                    over_sum(0)
                    over_sum(1)
                    for s in range(H3 + 6):
                        if s + 3 < H3:
                            maximum(s + 3)
                        if s + 2 < H3:
                            over_sum(s + 2)
                        if s < H3:
                            t = s % T
                            dve.wait_ge(pt3_hi, s0_ + s + 1)
                            hi, lo = [p_[:, s // T % 2, 0:t + 1, t * P:(t + 1) * P] for p_ in pT3]
                            nc.vector.tensor_tensor(lo, y_psum[:, s % 2, 0:(t + 1) * P].rearrange("p (k q) -> p k q", q=P),
                                                    hi.bitcast(F32), ALU.subtract).then_inc(pt3_ready, 1)
                        if s >= 9 and s % 4 == 1:
                            h = (s - 9) // 4
                            rows = slice(HD3 * (h % 4), HD3 * (h % 4 + 1))
                            dve.wait_ge(o3_hi, h0 + h + 1)
                            nc.vector.tensor_tensor(xT[1][rows, h // 4, :], y_psum[rows, 2 + h % 2, :],
                                                    xT[0][rows, h // 4, :].bitcast(F32), ALU.subtract).then_inc(o3_ready, 1)
                    for t in range(T):
                        for e, done in ((0, dense_added), (1, x_done)):
                            dve.wait_ge(dense_full, b * 2 * T + 2 * t + e + 1)
                            if e:
                                dve.wait_ge(dense_added, b * T + t + 1)
                            nc.vector.scalar_tensor_tensor(tile_of(b, t), ring[:, (2 * t + e) % 4, :], wrs[:, e, t:t + 1],
                                                           tile_of(b, t), ALU.mult, ALU.add).then_inc(done, 1)

                dve.wait_ge(consts_loaded, CONSTS + 48)
                nc.vector.tensor_copy(causal_r[:], causal[:]).then_inc(causal_ready, 1)
                nc.vector.tensor_copy(ident_r[:], ident[:]).then_inc(causal_ready, 1)
                loop(B, 1, body)

            def phase_C3():
                start = seq0["C3"]
                g = PARAMS.index("L3_xattn_ln_post_cross_w")

                def Q(n, m):
                    for f in range(2):
                        lo_of(cqT[1][:, f, :], ring[:, (m + f) % 4, :], cqT[0][:, f, :], n + f)

                def body(b, n, m, last, prefetch):
                    def finish(i):
                        pv = cpr[:, i, :].rearrange("p (h k) -> p h k", k=M)
                        total = sm[:, i % T, :]
                        dve.wait_ge(act_out, n + i + 1)
                        step(nc.vector.tensor_reduce(total, pv, AX, ALU.add))
                        settle()
                        step(nc.vector.reciprocal(total, total))
                        settle()
                        nc.vector.tensor_tensor(pv, pv, total.unsqueeze(2).to_broadcast([P, 8, M]),
                                                ALU.mult).then_inc(operand_ready, 1)

                    for i in range(2 * T):
                        scores = ring[:, (m + i) % 4, :].rearrange("p (h k) -> p h k", k=M)
                        top = mx[:, i % T, :]
                        dve.wait_ge(psum_full, n + i + 1)
                        step(nc.vector.tensor_reduce(top, scores, AX, ALU.max))
                        settle()
                        nc.vector.tensor_tensor(csc[:, i % 2, :].rearrange("p (h k) -> p h k", k=M), scores,
                                                top.unsqueeze(2).to_broadcast([P, 8, M]),
                                                ALU.subtract).then_inc(scores_copied, 1)
                        if i:
                            finish(i - 1)
                    finish(2 * T - 1)
                    k0 = 8
                    if not last:
                        norm_lo(xT, n + k0, m + k0, g)
                        k0 += 4
                    for f in range(2):
                        for p in range(5):
                            hi, lo = [p_[:, p % 2, :] for p_ in cpT] if p < 4 else [p_[:, f, :] for p_ in coT]
                            lo_of(lo, ring[:, (m + k0) % 4, :], hi, n + k0)
                            k0 += 1
                    if not last:
                        Q(n + k0, m + k0)
                    if prefetch:
                        norm_rms(b + 2)
                    dve.wait_ge(y_done, y0["C3"] + b + 1)
                    for t in range(T):
                        nc.vector.tensor_tensor(tile_of(b, t), y_psum[:, t, :], tile_of(b, t), ALU.add).then_inc(x_done, 1)

                dve.wait_ge(x_done, xd0["C3"])
                norm_rms(0)
                norm_lo(xT, start, start, g)
                Q(start + 4, start + 4)
                norm_rms(1)
                loop(B - 2, 3 * 2 * T + NORM3, lambda b: body(b, start + 6 + b * 24, start + 6, False, True))
                body(B - 2, start + 6 + (B - 2) * 24, start + 6, False, False)
                body(B - 1, start + 6 + (B - 1) * 24, start + 6, True, False)

            def phase_M(e):
                ph = "M" + e
                start = seq0[ph]
                g = PARAMS.index("L3_xattn_ln_post_attn_w")

                def hidden(n, m, j):
                    dve.wait_ge(psum_full, n + 2 * j + 2)
                    dve.wait_ge(act_out, n + 2 * j + 1)
                    dve.wait_ge(operand_ready, n + 2 * j)
                    dve.sem_inc(dve_passed, 1)
                    nc.vector.tensor_tensor(mf[:], sg[:], ring[:, (m + 2 * j + 1) % 4, :],
                                            ALU.mult).then_inc(operand_ready, 1)
                    dve.wait_ge(operand_ready, n + 2 * j + 1)
                    lo_of(mT[1][:], mf[:], mT[0][:], n + 2 * j + 1)

                def body(b, n, m, last):
                    for j in range(HT):
                        hidden(n, m, j)
                        if j == HT // 2 and not last:
                            norm_rms(b + 1, e)
                    if not last:
                        norm_lo(xT, n + 2 * HT, m + 2 * HT, g, 2)
                    dve.wait_ge(y_done, y0[ph] + b * HT + HT)
                    for t in range(T):
                        nc.vector.tensor_tensor(tile_of(b, t), y_psum[:, t, :], tile_of(b, t), ALU.add).then_inc(x_done, 1)

                def listed(i):
                    n = start + i * 28
                    entries = [i * T + t for t in range(T)]
                    tiles = [dve.value_load(v_plan[0:1, bass.ds(B * T + entry, 1)], min_val=0, max_val=B * T - 1)
                             for entry in entries]

                    def tile(t):
                        return x[:, bass.ds(tiles[t], 1), :].rearrange("p o d -> p (o d)")

                    dve.wait_ge(x_done, xd0[ph] + i * T)
                    for t in range(T):
                        step(nc.vector.tensor_tensor(v_mask[:, t:t + 1], vis[:, 1, bass.ds(tiles[t], 1)],
                                                     v_valid[:, bass.ds(entries[t], 1)], ALU.mult))
                    statistics(tile, 1e-6, True)
                    step(nc.vector.tensor_tensor(v_mask[:], v_mask[:], rs[:], ALU.mult))
                    settle()
                    for t in range(T):
                        if t == T - 1:
                            settle()
                        ins = nc.vector.tensor_scalar(xn[:, t, :], tile(t), v_mask[:, t:t + 1], None, ALU.mult)
                        if t < T - 1:
                            step(ins)
                        else:
                            ins.then_inc(xn_ready, 1)
                    norm_lo(xT, n, start, g, 2)
                    for j in range(HT):
                        hidden(n + 6, start + 6, j)
                    dve.wait_ge(y_done, y0[ph] + i * HT + HT)
                    for t in range(T):
                        if t:
                            dve.wait_ge(x_done, xd0[ph] + i * T + t)
                        dve.sem_inc(dve_passed, 1)
                        nc.vector.tensor_tensor(tile(t), y_psum[:, t, :], tile(t), ALU.add).then_inc(x_done, 1)

                dve.wait_ge(x_done, xd0[ph])
                if e == "l":
                    norm_rms(0, e)
                    norm_lo(xT, start, start, g, 2)
                    loop(B - 1, NORM_RMS + 1 + T - 1, lambda b: body(b, start + 6 + b * 28, start + 6, False))
                    body(B - 1, start + 6 + (B - 1) * 28, start + 6, True)
                else:
                    groups = dve.value_load(v_plan[0:1, 2 * B * T:], min_val=1, max_val=B)
                    loop(groups, T + NORM_RMS + 1 + T - 1, listed)
                    dve.wait_ge(x_done, xd0[ph] + groups * T)
                    dve.sem_inc(finished, 1)

            dve.sem_inc(x_done, 1)
            step(nc.vector.memset(bd[0][:].bitcast(F32), 0.0))
            settle()
            nc.vector.memset(bd[1][:].bitcast(F32), 0.0).then_inc(zeroed, 1)
            dve.wait_ge(zeroed, 1)
            dve.wait_ge(consts_loaded, CONSTS)
            step(nc.vector.tensor_copy(kbias[:].rearrange("p b m -> p (b m)"), mask8.bitcast(U8)))
            settle()
            step(nc.vector.tensor_scalar(kbias[:], kbias[:], -1.0, FLT_MAX, ALU.add, ALU.mult))
            settle()
            step(nc.vector.tensor_scalar(vis[:].rearrange("p a t -> p (a t)"), types, 1, None, ALU.is_equal))
            settle()
            step(nc.vector.tensor_tensor(vis[:, 1, :], vis[:, 0, :], vis[:, 1, :], ALU.mult))
            settle()
            step(nc.vector.tensor_scalar(vis[:, 0, :], vis[:, 1, :], -1.0, 1.0, ALU.mult, ALU.add))
            settle()
            step(nc.vector.memset(xn[:, 3, 256:256 + P], 1.0))
            settle()
            dve.sem_inc(counted, 1)
            dve.wait_ge(counted, 2)
            has, rank, key = (xn[:, i, 256:256 + B * T] for i in range(3))
            before, number, entry = (xn[:, i, 0:(B * T) ** 2].rearrange("p (a c) -> p a c", a=B * T) for i in range(3))
            work = xn[:, 3, 0:(B * T) ** 2].rearrange("p (a c) -> p a c", a=B * T)

            def row(v):
                return v.unsqueeze(1).to_broadcast([P, B * T, B * T])

            def then(ins):
                step(ins)
                settle()

            then(nc.vector.tensor_scalar(has, y_psum[:, 0, 0:B * T], 1.0, None, ALU.min))
            then(nc.vector.tensor_tensor(work, row(has), before, ALU.mult))
            then(nc.vector.tensor_reduce(rank, work, AX, ALU.add))
            then(nc.vector.scalar_tensor_tensor(key, rank, 1.0, has, ALU.add, ALU.mult))
            then(nc.vector.tensor_tensor(work, row(key), entry, ALU.is_equal))
            then(nc.vector.tensor_reduce(v_valid[:], work, AX, ALU.add))
            then(nc.vector.tensor_tensor(work, work, number, ALU.mult))
            then(nc.vector.tensor_reduce(rank, work, AX, ALU.add))
            then(nc.vector.tensor_copy(v_plan[:, 0:B * T], has))
            then(nc.vector.tensor_copy(v_plan[:, B * T:2 * B * T], rank))
            then(nc.vector.tensor_reduce(key[:, 0:1], v_valid[:].rearrange("p (g t) -> p t g", t=T)[:, 0, :], AX, ALU.add))
            then(nc.vector.tensor_scalar(v_plan[:, 2 * B * T:], key[:, 0:1], 1.0, None, ALU.max))
            dve.sem_inc(counted, 1)
            dve.wait_ge(tanh_done, 1)
            for ph in phases:
                if ph in ("A1", "A2"):
                    phase_A(ph[1])
                elif ph[0] in "FM":
                    (phase_F if ph[0] == "F" else phase_M)(ph[1])
                else:
                    {"K0": phase_K0, "G": phase_G, "Q3": phase_Q3, "A3": phase_A3, "C3": phase_C3}[ph]()


CONSTS = 9 * 16
PHASES = ["K0", "G", "A1", "F1", "A2", "F2", "Q3", "A3", "C3", "Ml", "Mv"]


def layouts(inputs):
    f = np.ascontiguousarray
    a = {k: np.asarray(v) for k, v in inputs.items()}
    p = {"x": f(a["x"].reshape(B * SEQ, D))}
    ctxT = a["ctx_1024"].transpose(2, 0, 1)
    w = {}
    for k in range(2):
        c = ctxT[k * P:(k + 1) * P]
        w["ctx", k] = np.stack([c, c], 2).reshape(P, 512)
        w["wmem", k] = a["L0_xattn_W_mem"].T[k * P:(k + 1) * P]
        w["ckv", k] = a["L3_xattn_ckv_w"][k * P:(k + 1) * P]
    for k in range(8):
        w["wg", k] = a["L0_xattn_W_gate"].T[k * P:(k + 1) * P]
    for l in "12":
        wkv, wq, wo = (a[f"L{l}_xattn_{n}"] for n in ("Wkv", "Wq", "Wo"))
        w1, w2 = a[f"L{l}_xattn_W1"], a[f"L{l}_xattn_W2"]
        for i in range(8):
            c, k = i // 2, i % 2
            w[f"wkv{l}", i] = wkv[k * P:(k + 1) * P, c * 512:(c + 1) * 512]
            w[f"wq{l}", i] = wq[:, i * P:(i + 1) * P].reshape(KT, P, P).transpose(1, 0, 2).reshape(P, 512)
            w[f"wo{l}", i] = wo[i * P:(i + 1) * P]
        for j in range(FF):
            w[f"w1_{l}", j] = w1[:, j * P:(j + 1) * P].reshape(KT, P, P).transpose(1, 0, 2).reshape(P, 512)
            w[f"w2_{l}", j] = w2[j * P:(j + 1) * P]
    for e in "lv":
        qkv, dense, gate, up, down = (a[f"L3_xattn_{e}_{n}"] for n in ("qkv", "dense", "gate", "up", "down"))
        gate, up = (np.pad(t, ((0, 0), (0, HT * P - HID))) for t in (gate, up))
        down = np.pad(down, ((0, HT * P - HID), (0, 0)))
        for k in range(KT):
            w[f"dense_{e}", k] = dense[k * P:(k + 1) * P]
            for c in range(3):
                w[f"qkv_{e}", 4 * c + k] = qkv[k * P:(k + 1) * P, c * 512:(c + 1) * 512]
        for j in range(HT):
            for name, t in (("gate", gate), ("up", up)):
                w[f"{name}_{e}", j] = t[:, j * P:(j + 1) * P].reshape(KT, P, P).transpose(1, 0, 2).reshape(P, 512)
            w[f"down_{e}", j] = down[j * P:(j + 1) * P]
    for i in range(2):
        w["cq", i] = a["L3_xattn_cq_w"][2 * i * P:2 * (i + 1) * P].reshape(2, P, MD).transpose(1, 0, 2).reshape(P, 512)
        w["cdense", i] = a["L3_xattn_cdense_w"][i * P:(i + 1) * P]
    names = [n for ph in PHASES for n in piece_names()[ph]]
    p["weights"] = f(np.stack([w[n] for n in names]))
    p["params"] = f(np.stack([a[n].reshape(KT, P).T for n in PARAMS], 1))
    p["gates"] = f(np.broadcast_to(np.concatenate([a[n] for n in GATES])[None], (P, len(GATES))))
    p["mask_s2"] = f(np.broadcast_to(a["mask_BxS2_bk0"][None], (P, B, M))).view(np.int32)
    p["b_gate"] = f(np.broadcast_to(a["L0_xattn_b_gate"][None], (P, D)))
    p["norm_w"] = f(np.broadcast_to(a["L0_xattn_norm_w"][None], (P, D)))
    tt = a["mask_BxS_ik0"]
    tt = np.stack([tt, np.pad(tt[:, 1:], ((0, 0), (0, 1)))])
    p["types"] = f(tt.reshape(2, B * T, P).transpose(2, 0, 1))
    p["pos"] = f(a["pos_1xS"].reshape(T, P).T)
    inv = (np.float32(1) / np.power(np.float32(10000), np.arange(0, HD3, 2, dtype=np.float32) / np.float32(HD3)))
    angle = np.outer(np.arange(SEQ, dtype=np.float32), inv)
    p["rope_table"] = np.concatenate([np.cos(angle), np.cos(angle), -np.sin(angle), np.sin(angle)], 1).astype(np.float32)
    p["causal"] = np.where(np.arange(P)[None, :] <= np.arange(P)[:, None], 0, -2.0 ** 127).astype(np.float32)
    p["ident"] = np.eye(P, dtype=np.float32)
    i, j = np.arange(B * T)[:, None], np.arange(B * T)[None, :]
    tables = np.stack([t.astype(np.float32) for t in (j < i, j + 0 * i, i + 1 + 0 * j)]).reshape(3, -1)
    p["tile_tables"] = f(np.broadcast_to(tables[None], (P, 3, (B * T) ** 2)))
    row, h = np.arange(P)[:, None, None], np.arange(8)[None, :, None]
    p["mask_k"] = f(np.broadcast_to(row // 16 == h, (P, 8, M)).astype(np.float32))
    j, c = np.arange(4)[None, :, None], np.arange(P)[None, None, :]
    p["mask_v"] = f((c // 16 == 2 * j + row // 64).astype(np.float32))
    return p, names


def kernel(**inputs):
    import concourse.bacc as _bacc
    from concourse.bass_utils import run_bass_kernel_spmd as _run

    nc = _bacc.Bacc("TRN2", target_bir_lowering=False, num_devices=1)
    arrays, names = layouts(inputs)
    t_in = {n: nc.dram_tensor("in_" + n, v.shape, mybir.dt.from_np(v.dtype), kind="ExternalInput").ap() for n, v in arrays.items()}
    packed = t_in["weights"]
    t_in["weights"] = {n: packed[i] for i, n in enumerate(names)}
    t_in["kv_scratch"] = [[[nc.dram_tensor(f"kv_{l}_{kv}_{part}", (B * P, 1024), F32).ap() for part in ("hi", "lo")]
                           for kv in "kv"] for l in "12c"]
    t_in["qkv_scratch"] = [nc.dram_tensor(f"scratch_{n}3", (2, B * SEQ, D), F32).ap() for n in "qkv"]
    out = nc.dram_tensor("out_0", (B * SEQ, D), F32, kind="ExternalOutput").ap()
    build(nc, t_in, out, PHASES)
    r = _run(nc, [{"in_" + n: v for n, v in arrays.items()}], core_ids=[0])
    return r.results[0]["out_0"].reshape(B, SEQ, D)
```
